# Optimizing a Trainium2 kernel written in Bass

```python
import numpy as np
import jax
import jax.numpy as jnp

def _softmax(x, axis=-1):
    return jax.nn.softmax(x, axis=axis)

def _gelu(x):
    return jax.nn.gelu(x, approximate=True)

def _silu(x):
    return jax.nn.silu(x)

def _sigmoid(x):
    return jax.nn.sigmoid(x)

def _layernorm(x, axis=-1, eps=1e-05):
    m = jnp.mean(x, axis=axis, keepdims=True)
    v = jnp.var(x, axis=axis, keepdims=True)
    return (x - m) / jnp.sqrt(v + eps)

def _scatter_add(tgt, idx, src, axis=0):
    return tgt.at[idx].add(src)

def _segment_sum(src, seg, n):
    return jax.ops.segment_sum(src, seg, n)
kernel_name = 'mk_decoder_postln_d2_seqx_r4_0580c3'

def setup_inputs(seed: int=0):
    np.random.seed(seed)
    _w = jnp.asarray

    def _rec_inputs():
        import jax
        import jax.numpy as jnp
        _rk = jax.random.key(seed)
        x = -0.0003929 + 0.9999 * jax.random.normal(jax.random.fold_in(_rk, 1), (8, 112, 256), jnp.float32)
        _lenS = 112 - jax.random.randint(jax.random.fold_in(_rk, 7), (8,), 0, max(1, 112 // 4) + 1, jnp.int32)
        _lenS2 = 375 - jax.random.randint(jax.random.fold_in(_rk, 8), (8,), 0, max(1, 375 // 4) + 1, jnp.int32)
        _ctx_768P = jax.random.normal(jax.random.fold_in(_rk, 11), (8, 16, 192), jnp.float32)
        _ctx_768c = jax.random.dirichlet(jax.random.fold_in(_rk, 511), 0.3 * jnp.ones((16,), jnp.float32), (8, 375))
        _ctx_768t = jnp.einsum('bsk,bkd->bsd', _ctx_768c, _ctx_768P)
        _ctx_768t = _ctx_768t * jax.lax.rsqrt(jnp.mean(jnp.square(_ctx_768t)) + 1e-12) * 0.953939
        ctx_768 = -0.00055796 + 0.999787 * (_ctx_768t + 0.3 * jax.random.normal(jax.random.fold_in(_rk, 611), (8, 375, 192), jnp.float32))
        return (x, ctx_768)
    x, ctx_768 = _rec_inputs()

    def _L0_attn_setup():
        import jax, jax.numpy as jnp
        import numpy as np
        B, N, D = (4, 1024, 256)
        H, M = (16, 64)
        DH = D // H

        def _feature_map(t, omega):
            t_omega = jnp.einsum('bhnd,dm->bhnm', t, omega)
            norm_sq = 0.5 * jnp.sum(t * t, axis=-1, keepdims=True)
            return jnp.exp(t_omega - norm_sq)
        key = jax.random.key(seed)
        ks = jax.random.split(key, 6)
        x = jax.random.normal(ks[0], (B, N, D), dtype=jnp.float32)
        Wqkv = jax.random.normal(ks[1], (D, 3 * D), dtype=jnp.float32) * 0.02
        bqkv = jnp.zeros((3 * D,), dtype=jnp.float32)
        Wout = jax.random.normal(ks[2], (D, D), dtype=jnp.float32) * 0.02
        bout = jnp.zeros((D,), dtype=jnp.float32)
        omega = jax.random.normal(ks[3], (DH, M), dtype=jnp.float32)
        return {'x': x, 'Wqkv': Wqkv, 'bqkv': bqkv, 'Wout': Wout, 'bout': bout, 'omega': omega}
    _L0_attn_all = _L0_attn_setup()
    _L0_attn_in = {k: v for k, v in _L0_attn_all.items() if k in ('Wqkv', 'bqkv', 'Wout', 'bout', 'omega')}
    del _L0_attn_all

    def _L0_xattn_setup():
        import jax, jax.numpy as jnp
        import numpy as np
        IMAGE_DIM = 256
        TEXT_DIM = 192
        NUM_HEADS = 16
        HEAD_DIM = IMAGE_DIM // NUM_HEADS
        key = jax.random.key(seed)
        ks = jax.random.split(key, 14)
        B, N, M = (4, 1024, 128)
        s_img = 1.0 / np.sqrt(IMAGE_DIM)
        s_txt = 1.0 / np.sqrt(TEXT_DIM)
        s_ff = 1.0 / np.sqrt(2 * IMAGE_DIM)
        return {'x': jax.random.normal(ks[0], (B, N, IMAGE_DIM), jnp.float32), 'y': jax.random.normal(ks[1], (B, M, TEXT_DIM), jnp.float32), 'Wq': jax.random.normal(ks[2], (IMAGE_DIM, IMAGE_DIM), jnp.float32) * s_img, 'bq': jax.random.normal(ks[3], (IMAGE_DIM,), jnp.float32) * s_img, 'Wk': jax.random.normal(ks[4], (TEXT_DIM, IMAGE_DIM), jnp.float32) * s_txt, 'bk': jax.random.normal(ks[5], (IMAGE_DIM,), jnp.float32) * s_txt, 'Wv': jax.random.normal(ks[6], (TEXT_DIM, IMAGE_DIM), jnp.float32) * s_txt, 'bv': jax.random.normal(ks[7], (IMAGE_DIM,), jnp.float32) * s_txt, 'W1': jax.random.normal(ks[8], (IMAGE_DIM, 2 * IMAGE_DIM), jnp.float32) * s_img, 'b1': jax.random.normal(ks[9], (2 * IMAGE_DIM,), jnp.float32) * s_img, 'W2': jax.random.normal(ks[10], (2 * IMAGE_DIM, IMAGE_DIM), jnp.float32) * s_ff, 'b2': jax.random.normal(ks[11], (IMAGE_DIM,), jnp.float32) * s_ff}
    _L0_xattn_all = _L0_xattn_setup()
    _L0_xattn_in = {k: v for k, v in _L0_xattn_all.items() if k in ('Wq', 'bq', 'Wk', 'bk', 'Wv', 'bv', 'W1', 'b1', 'W2', 'b2')}
    del _L0_xattn_all

    def _L0_ffn_setup():
        import jax, jax.numpy as jnp
        import numpy as np
        E = 8
        K = 2
        CF = 1.25
        key = jax.random.key(seed)
        kx, kr, kg, ku, kd = jax.random.split(key, 5)
        D, F = (256, 1024)
        x = jax.random.normal(kx, (4, 512, D), dtype=jnp.float32)
        router_w = 0.02 * jax.random.normal(kr, (E, D), dtype=jnp.float32)
        wg = jax.random.normal(kg, (E, D, F), dtype=jnp.float32) / np.sqrt(D)
        wu = jax.random.normal(ku, (E, D, F), dtype=jnp.float32) / np.sqrt(D)
        wd = jax.random.normal(kd, (E, F, D), dtype=jnp.float32) / np.sqrt(F)
        return {'x': x, 'router_w': router_w, 'wg': wg, 'wu': wu, 'wd': wd}
    _L0_ffn_all = _L0_ffn_setup()
    _L0_ffn_in = {k: v for k, v in _L0_ffn_all.items() if k in ('router_w', 'wg', 'wu', 'wd')}
    del _L0_ffn_all

    def _L1_attn_setup():
        import jax, jax.numpy as jnp
        import numpy as np
        FEATURE_DIM = 16
        NUM_HEADS = 16
        HEAD_DIM = 64
        R2 = float(np.sqrt(2.0))
        RD = float(np.sqrt(FEATURE_DIM))
        RRD = float(np.sqrt(RD))
        RMS_EPS = 1e-05

        def taylor_exp(x):
            x2 = (x[..., :, None] * x[..., None, :]).reshape(*x.shape[:-1], FEATURE_DIM * FEATURE_DIM) / R2
            ones = jnp.ones_like(x[..., :1])
            return jnp.concatenate([ones, x / RRD, x2 / RD], axis=-1)

        def _reference_tuple_inner(hidden_states, Wq, Wk, Wv, Wo, g_weight):
            b, l, _ = hidden_states.shape
            q = (hidden_states @ Wq.T).reshape(b, l, NUM_HEADS, FEATURE_DIM).transpose(0, 2, 1, 3)
            k = (hidden_states @ Wk.T).reshape(b, l, NUM_HEADS, FEATURE_DIM).transpose(0, 2, 1, 3)
            v = (hidden_states @ Wv.T).reshape(b, l, NUM_HEADS, HEAD_DIM).transpose(0, 2, 1, 3)
            qf = taylor_exp(q)
            kf = taylor_exp(k)
            A_qk = jnp.einsum('bhnd,bhmd->bhnm', qf, kf)
            A_qk = jnp.tril(A_qk)
            y = jnp.einsum('bhnm,bhme->bhne', A_qk, v)
            kv_state = jnp.einsum('bhnd,bhnf->bhfd', kf, v)[:, :, None]
            rms = jax.lax.rsqrt(jnp.mean(y * y, axis=-1, keepdims=True) + RMS_EPS)
            y = y * rms * g_weight
            y = y.transpose(0, 2, 1, 3).reshape(b, l, NUM_HEADS * HEAD_DIM)
            out = y @ Wo.T
            return (out, kv_state)
        key = jax.random.key(seed)
        ks = jax.random.split(key, 5)
        b, l, d_model = (4, 512, 256)
        inp = {'hidden_states': jax.random.normal(ks[0], (b, l, d_model), dtype=jnp.float32), 'Wq': jax.random.normal(ks[1], (FEATURE_DIM * NUM_HEADS, d_model), dtype=jnp.float32) * 0.02, 'Wk': jax.random.normal(ks[2], (FEATURE_DIM * NUM_HEADS, d_model), dtype=jnp.float32) * 0.02, 'Wv': jax.random.normal(ks[3], (NUM_HEADS * HEAD_DIM, d_model), dtype=jnp.float32) * 0.02, 'Wo': jax.random.normal(ks[4], (d_model, NUM_HEADS * HEAD_DIM), dtype=jnp.float32) * 0.02, 'g_weight': jnp.ones((HEAD_DIM,), dtype=jnp.float32)}
        return inp
    _L1_attn_all = _L1_attn_setup()
    _L1_attn_in = {k: v for k, v in _L1_attn_all.items() if k in ('Wq', 'Wk', 'Wv', 'Wo', 'g_weight')}
    del _L1_attn_all

    def _L1_xattn_setup():
        import jax, jax.numpy as jnp
        import numpy as np
        N_HEADS = 16
        D_HEAD = 64
        key = jax.random.key(seed)
        ks = jax.random.split(key, 7)
        B, SQ, SKV = (2, 512, 512)
        D_MODEL, D_COND, D_ATTN = (256, 192, N_HEADS * D_HEAD)
        return {'x': jax.random.normal(ks[0], (B, SQ, D_MODEL), jnp.float32), 'cond': jax.random.normal(ks[1], (B, SKV, D_COND), jnp.float32), 'w_q': jax.random.normal(ks[2], (D_MODEL, D_ATTN), jnp.float32) * D_MODEL ** (-0.5), 'w_k': jax.random.normal(ks[3], (D_COND, D_ATTN), jnp.float32) * D_COND ** (-0.5), 'w_v': jax.random.normal(ks[4], (D_COND, D_ATTN), jnp.float32) * D_COND ** (-0.5), 'w_out': jax.random.normal(ks[5], (D_ATTN, D_MODEL), jnp.float32) * D_ATTN ** (-0.5), 'b_out': jnp.zeros((D_MODEL,), jnp.float32)}
    _L1_xattn_all = _L1_xattn_setup()
    _L1_xattn_in = {k: v for k, v in _L1_xattn_all.items() if k in ('w_q', 'w_k', 'w_v', 'w_out', 'b_out')}
    del _L1_xattn_all

    def _L1_ffn_setup():
        import jax, jax.numpy as jnp
        import numpy as np
        DIM = 256
        HEADS = 16
        HD = DIM // HEADS
        M = 64
        E = 4
        K = 2
        HID = 512
        MID = 512
        LB = 0.01
        EPS = 1.1920929e-07

        def _rms(x, w):
            return x * jax.lax.rsqrt(jnp.mean(x * x, axis=-1, keepdims=True) + EPS) * w

        def _gelu(x):
            return jax.nn.gelu(x, approximate=False)
        key = jax.random.key(seed)
        ks = jax.random.split(key, 20)
        d = DIM
        w = lambda k, s: jax.random.normal(k, s, jnp.float32) * 0.02
        return {'x': jax.random.normal(ks[0], (4, 256, d), jnp.float32), 'n1_w': jnp.ones((d,), jnp.float32), 'n2_w': jnp.ones((d,), jnp.float32), 'wq': w(ks[1], (d, d)), 'wk': w(ks[2], (d, d)), 'wv': w(ks[3], (d, d)), 'wo': w(ks[4], (d, d)), 'qn_w': jnp.ones((HD,), jnp.float32), 'kn_w': jnp.ones((HD,), jnp.float32), 'gate_w': w(ks[5], (E, d)), 'e0_up': w(ks[6], (HID, d)), 'e0_down': w(ks[7], (d, HID)), 'e1_w1': w(ks[8], (HID, d)), 'e1_w2': w(ks[9], (HID, d)), 'e1_down': w(ks[10], (d, HID)), 'e2_l1': w(ks[11], (MID, d)), 'e2_l2': w(ks[12], (HID, MID)), 'e2_l3': w(ks[13], (MID, HID)), 'e2_l4': w(ks[14], (d, MID)), 'e3_down': w(ks[15], (d, d)), 'e3_up': w(ks[16], (HID, d)), 'e3_out': w(ks[17], (d, HID))}
    _L1_ffn_all = _L1_ffn_setup()
    _L1_ffn_in = {k: v for k, v in _L1_ffn_all.items() if k in ('n1_w', 'n2_w', 'wq', 'wk', 'wv', 'wo', 'qn_w', 'kn_w', 'gate_w', 'e0_up', 'e0_down', 'e1_w1', 'e1_w2', 'e1_down', 'e2_l1', 'e2_l2', 'e2_l3', 'e2_l4', 'e3_down', 'e3_up', 'e3_out')}
    del _L1_ffn_all
    return {'x': x, 'ctx_768': ctx_768, 'L0_attn_Wqkv': _L0_attn_in['Wqkv'], 'L0_attn_bqkv': _L0_attn_in['bqkv'], 'L0_attn_Wout': _L0_attn_in['Wout'], 'L0_attn_bout': _L0_attn_in['bout'], 'L0_attn_omega': _L0_attn_in['omega'], 'L0_xattn_Wq': _L0_xattn_in['Wq'], 'L0_xattn_bq': _L0_xattn_in['bq'], 'L0_xattn_Wk': _L0_xattn_in['Wk'], 'L0_xattn_bk': _L0_xattn_in['bk'], 'L0_xattn_Wv': _L0_xattn_in['Wv'], 'L0_xattn_bv': _L0_xattn_in['bv'], 'L0_xattn_W1': _L0_xattn_in['W1'], 'L0_xattn_b1': _L0_xattn_in['b1'], 'L0_xattn_W2': _L0_xattn_in['W2'], 'L0_xattn_b2': _L0_xattn_in['b2'], 'L0_ffn_router_w': _L0_ffn_in['router_w'], 'L0_ffn_wg': _L0_ffn_in['wg'], 'L0_ffn_wu': _L0_ffn_in['wu'], 'L0_ffn_wd': _L0_ffn_in['wd'], 'L1_attn_Wq': _L1_attn_in['Wq'], 'L1_attn_Wk': _L1_attn_in['Wk'], 'L1_attn_Wv': _L1_attn_in['Wv'], 'L1_attn_Wo': _L1_attn_in['Wo'], 'L1_attn_g_weight': _L1_attn_in['g_weight'], 'L1_xattn_w_q': _L1_xattn_in['w_q'], 'L1_xattn_w_k': _L1_xattn_in['w_k'], 'L1_xattn_w_v': _L1_xattn_in['w_v'], 'L1_xattn_w_out': _L1_xattn_in['w_out'], 'L1_xattn_b_out': _L1_xattn_in['b_out'], 'L1_ffn_n1_w': _L1_ffn_in['n1_w'], 'L1_ffn_n2_w': _L1_ffn_in['n2_w'], 'L1_ffn_wq': _L1_ffn_in['wq'], 'L1_ffn_wk': _L1_ffn_in['wk'], 'L1_ffn_wv': _L1_ffn_in['wv'], 'L1_ffn_wo': _L1_ffn_in['wo'], 'L1_ffn_qn_w': _L1_ffn_in['qn_w'], 'L1_ffn_kn_w': _L1_ffn_in['kn_w'], 'L1_ffn_gate_w': _L1_ffn_in['gate_w'], 'L1_ffn_e0_up': _L1_ffn_in['e0_up'], 'L1_ffn_e0_down': _L1_ffn_in['e0_down'], 'L1_ffn_e1_w1': _L1_ffn_in['e1_w1'], 'L1_ffn_e1_w2': _L1_ffn_in['e1_w2'], 'L1_ffn_e1_down': _L1_ffn_in['e1_down'], 'L1_ffn_e2_l1': _L1_ffn_in['e2_l1'], 'L1_ffn_e2_l2': _L1_ffn_in['e2_l2'], 'L1_ffn_e2_l3': _L1_ffn_in['e2_l3'], 'L1_ffn_e2_l4': _L1_ffn_in['e2_l4'], 'L1_ffn_e3_down': _L1_ffn_in['e3_down'], 'L1_ffn_e3_up': _L1_ffn_in['e3_up'], 'L1_ffn_e3_out': _L1_ffn_in['e3_out']}

def reference(x, ctx_768, L0_attn_Wqkv, L0_attn_bqkv, L0_attn_Wout, L0_attn_bout, L0_attn_omega, L0_xattn_Wq, L0_xattn_bq, L0_xattn_Wk, L0_xattn_bk, L0_xattn_Wv, L0_xattn_bv, L0_xattn_W1, L0_xattn_b1, L0_xattn_W2, L0_xattn_b2, L0_ffn_router_w, L0_ffn_wg, L0_ffn_wu, L0_ffn_wd, L1_attn_Wq, L1_attn_Wk, L1_attn_Wv, L1_attn_Wo, L1_attn_g_weight, L1_xattn_w_q, L1_xattn_w_k, L1_xattn_w_v, L1_xattn_w_out, L1_xattn_b_out, L1_ffn_n1_w, L1_ffn_n2_w, L1_ffn_wq, L1_ffn_wk, L1_ffn_wv, L1_ffn_wo, L1_ffn_qn_w, L1_ffn_kn_w, L1_ffn_gate_w, L1_ffn_e0_up, L1_ffn_e0_down, L1_ffn_e1_w1, L1_ffn_e1_w2, L1_ffn_e1_down, L1_ffn_e2_l1, L1_ffn_e2_l2, L1_ffn_e2_l3, L1_ffn_e2_l4, L1_ffn_e3_down, L1_ffn_e3_up, L1_ffn_e3_out):
    import jax
    import jax.numpy as jnp

    def _L0_attn_ref(x, Wqkv, bqkv, Wout, bout, omega):
        import jax, jax.numpy as jnp
        import numpy as np
        B, N, D = (4, 1024, 256)
        H, M = (16, 64)
        DH = D // H

        def _feature_map(t, omega):
            t_omega = jnp.einsum('bhnd,dm->bhnm', t, omega)
            norm_sq = 0.5 * jnp.sum(t * t, axis=-1, keepdims=True)
            return jnp.exp(t_omega - norm_sq)
        b, n, d = x.shape
        qkv = x @ Wqkv + bqkv
        q, k, v = jnp.split(qkv, 3, axis=-1)

        def to_heads(t):
            return t.reshape(b, n, H, DH).transpose(0, 2, 1, 3)
        q, k, v = (to_heads(q), to_heads(k), to_heads(v))
        q_prime = _feature_map(q, omega)
        k_prime = _feature_map(k, omega)
        k_sum = jnp.sum(k_prime, axis=2)
        denominator = jnp.einsum('bhnm,bhm->bhn', q_prime, k_sum)[..., None]
        k_v = jnp.einsum('bhnm,bhnd->bhmd', k_prime, v)
        numerator = jnp.einsum('bhnm,bhmd->bhnd', q_prime, k_v)
        out = numerator / (denominator + 1e-06)
        out = out.transpose(0, 2, 1, 3).reshape(b, n, d)
        return out @ Wout + bout

    def _L0_xattn_ref(x, y, Wq, bq, Wk, bk, Wv, bv, W1, b1, W2, b2):
        import jax, jax.numpy as jnp
        import numpy as np
        IMAGE_DIM = 256
        TEXT_DIM = 192
        NUM_HEADS = 16
        HEAD_DIM = IMAGE_DIM // NUM_HEADS
        B, N, _ = x.shape
        M = y.shape[1]
        q = (x @ Wq + bq).reshape(B, N, NUM_HEADS, HEAD_DIM)
        k = (y @ Wk + bk).reshape(B, M, NUM_HEADS, HEAD_DIM)
        v = (y @ Wv + bv).reshape(B, M, NUM_HEADS, HEAD_DIM)
        scale = 1.0 / np.sqrt(HEAD_DIM)
        scores = jnp.einsum('bnhd,bmhd->bhnm', q, k) * scale
        attn = jax.nn.softmax(scores, axis=-1)
        out = jnp.einsum('bhnm,bmhd->bnhd', attn, v).reshape(B, N, IMAGE_DIM)
        h = jax.nn.relu(out @ W1 + b1)
        return h @ W2 + b2

    def _L0_ffn_ref(x, router_w, wg, wu, wd):
        import jax, jax.numpy as jnp
        import numpy as np
        E = 8
        K = 2
        CF = 1.25
        B, L, D = x.shape
        xf = x.reshape(-1, D)
        N = xf.shape[0]
        capacity = max(1, int(CF * N / E))
        logits = xf @ router_w.T
        probs = jax.nn.softmax(logits, axis=-1)
        topw, topi = jax.lax.top_k(probs, K)
        topw = topw / (topw.sum(-1, keepdims=True) + 1e-06)
        fe = topi.reshape(-1)
        fw = topw.reshape(-1)
        ft = jnp.repeat(jnp.arange(N), K)
        order = jnp.lexsort((-fw, fe))
        se, sw, st = (fe[order], fw[order], ft[order])
        counts = jax.ops.segment_sum(jnp.ones_like(se), se, num_segments=E)
        starts = jnp.cumsum(counts) - counts
        rank = jnp.arange(N * K) - starts[se]
        keep = rank < capacity
        pos = jnp.where(keep, rank, capacity)
        disp = jnp.zeros((E, capacity + 1, D), x.dtype).at[se, pos].set(xf[st])
        disp = disp[:, :capacity]
        g = jnp.einsum('ecd,edf->ecf', disp, wg)
        u = jnp.einsum('ecd,edf->ecf', disp, wu)
        eo = jnp.einsum('ecf,efd->ecd', jax.nn.silu(g) * u, wd)
        gathered = eo[se, jnp.minimum(pos, capacity - 1)]
        contrib = gathered * (sw * keep.astype(x.dtype))[:, None]
        out = jnp.zeros_like(xf).at[st].add(contrib)
        return out.reshape(B, L, D)

    def _L1_attn_ref(hidden_states, Wq, Wk, Wv, Wo, g_weight):
        import jax, jax.numpy as jnp
        import numpy as np
        FEATURE_DIM = 16
        NUM_HEADS = 16
        HEAD_DIM = 64
        R2 = float(np.sqrt(2.0))
        RD = float(np.sqrt(FEATURE_DIM))
        RRD = float(np.sqrt(RD))
        RMS_EPS = 1e-05

        def taylor_exp(x):
            x2 = (x[..., :, None] * x[..., None, :]).reshape(*x.shape[:-1], FEATURE_DIM * FEATURE_DIM) / R2
            ones = jnp.ones_like(x[..., :1])
            return jnp.concatenate([ones, x / RRD, x2 / RD], axis=-1)

        def _reference_tuple_inner(hidden_states, Wq, Wk, Wv, Wo, g_weight):
            b, l, _ = hidden_states.shape
            q = (hidden_states @ Wq.T).reshape(b, l, NUM_HEADS, FEATURE_DIM).transpose(0, 2, 1, 3)
            k = (hidden_states @ Wk.T).reshape(b, l, NUM_HEADS, FEATURE_DIM).transpose(0, 2, 1, 3)
            v = (hidden_states @ Wv.T).reshape(b, l, NUM_HEADS, HEAD_DIM).transpose(0, 2, 1, 3)
            qf = taylor_exp(q)
            kf = taylor_exp(k)
            A_qk = jnp.einsum('bhnd,bhmd->bhnm', qf, kf)
            A_qk = jnp.tril(A_qk)
            y = jnp.einsum('bhnm,bhme->bhne', A_qk, v)
            kv_state = jnp.einsum('bhnd,bhnf->bhfd', kf, v)[:, :, None]
            rms = jax.lax.rsqrt(jnp.mean(y * y, axis=-1, keepdims=True) + RMS_EPS)
            y = y * rms * g_weight
            y = y.transpose(0, 2, 1, 3).reshape(b, l, NUM_HEADS * HEAD_DIM)
            out = y @ Wo.T
            return (out, kv_state)
        return _reference_tuple_inner(hidden_states, Wq, Wk, Wv, Wo, g_weight)[0]

    def _L1_xattn_ref(x, cond, w_q, w_k, w_v, w_out, b_out):
        import jax, jax.numpy as jnp
        import numpy as np
        N_HEADS = 16
        D_HEAD = 64
        B, SQ, _ = x.shape
        SKV = cond.shape[1]
        scale = D_HEAD ** (-0.5)
        q = (x @ w_q).reshape(B, SQ, N_HEADS, D_HEAD)
        k = (cond @ w_k).reshape(B, SKV, N_HEADS, D_HEAD)
        v = (cond @ w_v).reshape(B, SKV, N_HEADS, D_HEAD)
        attn = jnp.einsum('bqhd,bkhd->bhqk', q, k) * scale
        attn = jax.nn.softmax(attn, axis=-1)
        out = jnp.einsum('bhqk,bkhd->bqhd', attn, v).reshape(B, SQ, N_HEADS * D_HEAD)
        return out @ w_out + b_out

    def _L1_ffn_ref(x, n1_w, n2_w, wq, wk, wv, wo, qn_w, kn_w, gate_w, e0_up, e0_down, e1_w1, e1_w2, e1_down, e2_l1, e2_l2, e2_l3, e2_l4, e3_down, e3_up, e3_out):
        import jax, jax.numpy as jnp
        import numpy as np
        DIM = 256
        HEADS = 16
        HD = DIM // HEADS
        M = 64
        E = 4
        K = 2
        HID = 512
        MID = 512
        LB = 0.01
        EPS = 1.1920929e-07

        def _rms(x, w):
            return x * jax.lax.rsqrt(jnp.mean(x * x, axis=-1, keepdims=True) + EPS) * w

        def _gelu(x):
            return jax.nn.gelu(x, approximate=False)
        B, T, C = x.shape
        h = _rms(x, n1_w)
        heads = lambda w_: (h @ w_.T).reshape(B, T, HEADS, HD).transpose(0, 2, 1, 3)
        q = _rms(heads(wq), qn_w)
        k = _rms(heads(wk), kn_w)
        v = heads(wv)
        scores = jnp.einsum('bhqd,bhkd->bhqk', q, k) * HD ** (-0.5)
        causal = jnp.tril(jnp.ones((T, T), bool))
        scores = jnp.where(causal[None, None], scores, -jnp.inf)
        attn = jax.nn.softmax(scores, axis=-1)
        ao = jnp.einsum('bhqk,bhkd->bhqd', attn, v).transpose(0, 2, 1, 3).reshape(B, T, C) @ wo.T
        ao = ao.at[:, :, :M].set(0.0)
        x = x + ao
        xf = _rms(x, n2_w).reshape(-1, C)
        N = xf.shape[0]
        logits = jnp.nan_to_num(xf @ gate_w.T)
        probs = jax.nn.softmax(logits, axis=-1)
        topv, topi = jax.lax.top_k(probs, K)
        topv = topv / (topv.sum(-1, keepdims=True) + 1e-08)
        wts = jnp.zeros((N, E), x.dtype).at[jnp.arange(N)[:, None], topi].add(topv)
        o0 = _gelu(xf @ e0_up.T) @ e0_down.T
        o1 = jax.nn.silu(xf @ e1_w1.T) * (xf @ e1_w2.T) @ e1_down.T
        o2 = _gelu(_gelu(_gelu(xf @ e2_l1.T) @ e2_l2.T) @ e2_l3.T) @ e2_l4.T
        o3 = _gelu(_gelu(xf @ e3_down.T) @ e3_up.T) @ e3_out.T
        moe = wts[:, 0:1] * o0 + wts[:, 1:2] * o1 + wts[:, 2:3] * o2 + wts[:, 3:4] * o3
        moe = moe.reshape(B, T, C).at[:, :, :M].set(0.0)
        return x + moe
    x = _layernorm(x + _L0_attn_ref(x, L0_attn_Wqkv, L0_attn_bqkv, L0_attn_Wout, L0_attn_bout, L0_attn_omega), axis=-1)
    x = _layernorm(x + _L0_xattn_ref(x, ctx_768, L0_xattn_Wq, L0_xattn_bq, L0_xattn_Wk, L0_xattn_bk, L0_xattn_Wv, L0_xattn_bv, L0_xattn_W1, L0_xattn_b1, L0_xattn_W2, L0_xattn_b2), axis=-1)
    x = _layernorm(x + _L0_ffn_ref(x, L0_ffn_router_w, L0_ffn_wg, L0_ffn_wu, L0_ffn_wd), axis=-1)
    x = _layernorm(x + _L1_attn_ref(x, L1_attn_Wq, L1_attn_Wk, L1_attn_Wv, L1_attn_Wo, L1_attn_g_weight), axis=-1)
    x = _layernorm(x + _L1_xattn_ref(x, ctx_768, L1_xattn_w_q, L1_xattn_w_k, L1_xattn_w_v, L1_xattn_w_out, L1_xattn_b_out), axis=-1)
    x = _layernorm(x + _L1_ffn_ref(x, L1_ffn_n1_w, L1_ffn_n2_w, L1_ffn_wq, L1_ffn_wk, L1_ffn_wv, L1_ffn_wo, L1_ffn_qn_w, L1_ffn_kn_w, L1_ffn_gate_w, L1_ffn_e0_up, L1_ffn_e0_down, L1_ffn_e1_w1, L1_ffn_e1_w2, L1_ffn_e1_down, L1_ffn_e2_l1, L1_ffn_e2_l2, L1_ffn_e2_l3, L1_ffn_e2_l4, L1_ffn_e3_down, L1_ffn_e3_up, L1_ffn_e3_out), axis=-1)
    return x

_drawn_inputs = setup_inputs


def setup_inputs(seed=0):
    import zlib

    import numpy as np

    out = dict(_drawn_inputs(seed))
    spreads = {'L0_attn_bqkv': (0.0, 0.1),
     'L0_attn_bout': (0.0, 0.1),
     'L1_attn_g_weight': (1.0, 0.2),
     'L1_xattn_b_out': (0.0, 0.1),
     'L1_ffn_n1_w': (1.0, 0.6),
     'L1_ffn_n2_w': (1.0, 0.6),
     'L1_ffn_qn_w': (1.0, 0.6),
     'L1_ffn_kn_w': (1.0, 0.6)}
    factors = {'L0_xattn_bk': 8.0,
     'L1_ffn_wq': 8.0,
     'L1_ffn_wk': 8.0,
     'L1_ffn_gate_w': 6.489,
     'L1_ffn_e0_up': 5.093,
     'L1_ffn_e0_down': 4.989,
     'L1_ffn_e1_w1': 8.0,
     'L1_ffn_e1_w2': 8.0,
     'L1_ffn_e1_down': 8.0,
     'L1_ffn_e2_l1': 8.0,
     'L1_ffn_e2_l2': 8.0,
     'L1_ffn_e2_l3': 8.0,
     'L1_ffn_e2_l4': 8.0,
     'L1_ffn_e3_down': 8.0,
     'L1_ffn_e3_up': 8.0,
     'L1_ffn_e3_out': 8.0}
    for name, (base, spread) in spreads.items():
        noise = np.random.default_rng([zlib.crc32(name.encode()), seed]).standard_normal(out[name].shape)
        drawn = base * np.exp(spread * noise) if base else spread * noise
        out[name] = jnp.asarray(drawn.astype(out[name].dtype))
    for name, factor in factors.items():
        out[name] = (out[name] * factor).astype(out[name].dtype)
    return out
```

```python
from contextlib import ExitStack

import numpy as np

import concourse.bass as bass
from concourse import mybir

F32 = mybir.dt.float32
BF16 = mybir.dt.bfloat16
U32 = mybir.dt.uint32
I32 = mybir.dt.int32
ALU = mybir.AluOpType
ACT = mybir.ActivationFunctionType
X = mybir.AxisListType.X

P = 128
B, N, D = 8, 112, 256
T = B * N
KC = D // P
S, DC = 375, 192
SCH = 125
NCH = S // SCH
CK = 96
CKC = DC // CK
H, DH = 16, 16
DHW = 64
HW = H * DHW
FM = 64
HALF = 4 * N
HPT = P // DH
E0, F0, CAP = 8, 1024, int(1.25 * T / 8)
SLOTS = E0 * CAP
HC = CAP // 2
E1, HID = 4, 512
KEPT = D - 64
BANK = 512
LN_EPS, RMS1_EPS, RMS_EPS = 1e-5, 1e-5, 1.1920929e-07
KB = 1024


class Sem:

    def __init__(self, nc, ctx, name):
        self.handle = ctx.enter_context(nc.semaphore(name))
        self.value = 0

    def add(self, by):
        self.value += by
        return (self, self.value)


class Lane:

    def __init__(self, nc, ctx, name):
        self.sem = Sem(nc, ctx, "done_" + name)
        self.queue = []
        self.waited = {}

    def wait(self, *marks):
        for mark in marks:
            if mark is None:
                continue
            sem, value = mark
            if self.waited.get(sem, 0) < value:
                self.waited[sem] = value
                self.queue.append((None, sem, value, None))

    def do(self, op, *args, signal=True, **kw):
        self.queue.append((op, args, kw, self.sem.handle if signal else None))
        return self.sem.add(1) if signal else None

    def dma(self, op, sem, *args, **kw):
        self.queue.append((op, args, kw, (sem.handle, 16)))
        return sem.add(16)

    def run(self, eng):
        for op, args, kw, sem in self.queue:
            if op is None:
                eng.wait_ge(args.handle, kw)
            else:
                ins = op(*args, **kw)
                if isinstance(sem, tuple):
                    ins.then_inc(sem[0], sem[1])
                elif sem is not None:
                    ins.then_inc(sem, 1)


class Buf:

    def __init__(self, ap):
        self.ap = ap
        self.free = ()


class Ring:

    def __init__(self, aps):
        self.bufs = [Buf(a) for a in aps]
        self.at = 0

    def take(self, *writers):
        buf = self.bufs[self.at % len(self.bufs)]
        self.at += 1
        assert buf.free is not None, "a buffer is taken while it is in use"
        for lane in writers:
            lane.wait(*buf.free)
        buf.free = None
        return buf


class Region:

    def __init__(self, nc, base, size):
        self.nc, self.base, self.size, self.at = nc, base, size, 0

    def tensor(self, name, shape, dtype=F32):
        words = 1
        for n in shape[1:]:
            words *= n
        size = words * mybir.dt.size(dtype)
        size += -size % 32
        assert self.at + size <= self.size, (name, self.at, size, self.size)
        t = self.nc.alloc_sbuf_tensor_at(name, list(shape), dtype, offset=self.base + self.at)
        self.at += size
        return t

    def restart(self, at=0):
        self.at = at


def weave(*steps):
    live = [s for s in steps if s is not None]
    while live:
        for s in list(live):
            if next(s, "end") == "end":
                live.remove(s)


def program(nc, a, out):
    ctx = ExitStack()
    with ctx:
        pe, act, dve, pool, sp = (Lane(nc, ctx, n) for n in ("pe", "act", "dve", "pool", "sp"))
        TE, SC, VE, GP, SY = nc.tensor, nc.scalar, nc.vector, nc.gpsimd, nc.sync

        def sem(name):
            return Sem(nc, ctx, name)

        START = -(-nc.sbuf_base // 32) * 32
        ARENA = (nc.sbuf_usable_end - START) // 32 * 32
        ctx.enter_context(nc.sbuf_tensor("arena", [P, ARENA], mybir.dt.uint8))
        keep_kb, wts_kb, ring_kb = 36, 51, 48
        keep = Region(nc, START, keep_kb * KB)
        wts = Region(nc, START + keep_kb * KB, wts_kb * KB)
        ring = Region(nc, START + (keep_kb + wts_kb) * KB, ring_kb * KB)
        work = Region(nc, START + (keep_kb + wts_kb + ring_kb) * KB,
                      ARENA - (keep_kb + wts_kb + ring_kb) * KB)

        psum = ctx.enter_context(nc.psum_tensor("psum", [P, 8, BANK], F32))
        psum16 = psum[:, :, :].bitcast(BF16)

        def banks(first, count):
            return Ring([psum[:, i, :] for i in range(first, first + count)])

        x_tok = keep.tensor("x_tok", [N, B, D])
        x_ch = keep.tensor("x_ch", [P, KC, T])
        res = keep.tensor("res", [N, B, D])
        ctx_sb = [keep.tensor(f"ctx{i}", [CK, CKC, S]) for i in range(3)]
        ident = keep.tensor("ident", [P, P])
        ident16 = keep.tensor("ident16", [P, P], BF16)
        headq = keep.tensor("headq", [P, HPT])
        half_causal = keep.tensor("half_causal", [N, N])
        causal_add = keep.tensor("causal_add", [N, N])
        before = keep.tensor("before", [N, N])
        chan = keep.tensor("chan", [P, 19])
        stats = keep.tensor("stats", [N, B, 6])
        meanvar = keep.tensor("meanvar", [N, B, 2])
        rstd = keep.tensor("rstd", [N, B, 1])
        minus_half = keep.tensor("minus_half", [N, 2 * H])
        slot_tab = keep.tensor("slot_tab", [N, 2 * B])
        iota8 = keep.tensor("iota8", [N, E0])

        s_const, s_x = sem("dma_const"), sem("dma_x")
        for name, t in (("xT", x_ch), ("chan", chan)):
            sp.dma(SY.dma_start, s_x, t[:], a[name])
        x_ready = (s_x, s_x.value)

        def load(region, name, shape, s, lane=sp, q=SY):
            t = region.tensor("w_" + name, shape)
            return t, lane.dma(q.dma_start, s, t[:], a[name])

        s_w0 = sem("dma_w0")
        Wqkv, _ = load(wts, "Wqkv", [P, KC, 3 * D], s_w0)
        omega, _ = load(wts, "omega", [P, 4 * FM], s_w0)
        vbias0, _ = load(wts, "vbias0", [N, D], s_w0)
        w0_ready = (s_w0, s_w0.value)
        for name, t in (("x_tok", x_tok), ("ident", ident), ("headq", headq),
                        ("half_causal", half_causal), ("causal_add", causal_add),
                        ("before", before), ("slot_tab", slot_tab), ("iota8", iota8)):
            sp.dma(SY.dma_start, s_const, t[:], a[name])
        s_w0b = sem("dma_w0b")
        Wout0, _ = load(wts, "Wout0", [P, KC, D], s_w0b)
        bout0, _ = load(wts, "bout0", [N, D], s_w0b)
        const_ready = (s_const, s_const.value)
        w0b_ready = (s_w0b, s_w0b.value)
        s_ctx = [sem(f"dma_ctx{i}") for i in range(3)]
        ctx_ready, ctx_read = {}, {}

        def load_ctx(i):
            if i >= 3:
                sp.wait(ctx_read[i - 3])
            ctx_ready[i] = sp.dma(SY.dma_start, s_ctx[i % 3], ctx_sb[i % 3][:], a["ctxT"][i % B])

        s_w1 = sem("dma_w1")
        Wq1, _ = load(wts, "Wq1", [P, KC, D], s_w1)
        Wk1, _ = load(wts, "Wk1", [CK, CKC, D], s_w1)
        Wv1, _ = load(wts, "Wv1", [CK, CKC, D], s_w1)
        bv1, _ = load(wts, "bv1", [SCH, D], s_w1)
        W1, _ = load(wts, "W1", [P, KC, 2 * D], s_w1)
        W2, _ = load(wts, "W2", [P, 2 * KC, D], s_w1)
        b2, _ = load(wts, "b2", [N, D], s_w1)
        w1_ready = (s_w1, s_w1.value)
        for i in range(3):
            load_ctx(i)
        s_w2 = sem("dma_w2")
        router, _ = load(wts, "router", [P, KC, E0], s_w2)
        w2_ready = (s_w2, s_w2.value)

        NEB = 2
        wg_sb = [ring.tensor(f"wg{i}", [P, KC, F0]) for i in range(NEB)]
        wu_sb = [ring.tensor(f"wu{i}", [P, KC, F0]) for i in range(NEB)]
        wd_sb = [ring.tensor(f"wd{i}", [P, F0 // P, D]) for i in range(NEB)]
        s_exp = [sem(f"dma_expert{i}") for i in range(NEB)]
        expert_ready, expert_read = {}, {}

        def load_expert(e):
            i = e % NEB
            if e >= NEB:
                sp.wait(expert_read[e - NEB])
            sp.dma(SY.dma_start, s_exp[i], wg_sb[i][:], a["wg"][e])
            sp.dma(SY.dma_start, s_exp[i], wu_sb[i][:], a["wu"][e])
            expert_ready[e] = sp.dma(SY.dma_start, s_exp[i], wd_sb[i][:], a["wd"][e])

        for e in range(NEB):
            load_expert(e)
        s_w3 = sem("dma_w3")
        Wq3, _ = load(wts, "Wq3", [P, KC, D], s_w3)
        Wk3, _ = load(wts, "Wk3", [P, KC, D], s_w3)
        Wv3, _ = load(wts, "Wv3", [P, KC, HW], s_w3)
        Wo3, _ = load(wts, "Wo3", [P, HW // P, D], s_w3)
        w3_ready = (s_w3, s_w3.value)

        disp = nc.dram_tensor("dispatched", [SLOTS + 2 * T, D], F32)
        eout = nc.dram_tensor("expert_out", [SLOTS, D], F32)

        zeros = keep.tensor("zeros", [P, D])
        m_zero = pool.do(GP.memset, zeros[:], 0.0)
        pool.do(GP.memset, minus_half[:], -0.5)
        pool.wait(const_ready)
        m_ident16 = pool.do(GP.tensor_copy, ident16[:], ident[:])
        s_zero = sem("dma_zero")
        sp.wait(m_zero)
        for i in range(SLOTS // HC // 2):
            rows = disp[2 * i * HC:2 * (i + 1) * HC, :].rearrange("(t p) d -> p t d", p=HC)
            for t in range(2):
                sp.dma(SY.dma_start, s_zero, rows[:, t, :], zeros[0:HC, :])
        disp_zeroed = (s_zero, s_zero.value)

        def cols(b):
            return slice(b * N, (b + 1) * N)

        x_tok_mark = {b: const_ready for b in range(B)}
        x_ch_mark = {b: x_ready for b in range(B)}
        res_mark = {}

        def add_bias(b, bias, ready):
            pool.wait(ready, x_tok_mark[b])
            res_mark[b] = pool.do(GP.tensor_tensor, res[:, b, :], x_tok[:, b, :], bias[:], ALU.add)

        def power(out_ap, in_ap, mark):
            pool.wait(mark)
            return pool.do(GP.tensor_tensor, out_ap, in_ap, minus_half[:, 0:in_ap.shape[-1]],
                           ALU.pow)

        def norm(b, y, y_mark, base, base_mark, misc, lo=0, done=None):
            if y is not None:
                dve.wait(y_mark, base_mark)
                m = dve.do(VE.tensor_tensor, res[:, b, lo:], base[:, b, lo:], y.ap, ALU.add)
                y.done(m)
            else:
                m = base_mark
            dve.wait(m)
            m = dve.do(VE.bn_stats, stats[:, b, :], res[:, b, :])
            dve.wait(m)
            m = dve.do(VE.bn_aggr, meanvar[:, b, :], stats[:, b, :])
            dve.wait(m)
            m = dve.do(VE.tensor_scalar, meanvar[:, b, 1:2], meanvar[:, b, 1:2], LN_EPS, None,
                       ALU.add)
            yield
            m = power(rstd[:, b, :], meanvar[:, b, 1:2], m)
            yield
            dve.wait(m)
            m = dve.do(VE.tensor_scalar, x_tok[:, b, :], res[:, b, :], meanvar[:, b, 0:1],
                       rstd[:, b, :], ALU.subtract, ALU.mult)
            x_tok_mark[b] = m
            if done is not None:
                done(b, m)
                return
            yield
            yield from to_channels(x_tok[:, b, :], m, KC, misc, x_ch[:, :, cols(b)], x_ch_mark, b)

        def to_channels(tok, mark, tiles, misc, ch, marks, key, wait=(), lane=None):
            for t0 in range(0, tiles, 4):
                n = min(4, tiles - t0)
                bank = misc.take(pe)
                pe.wait(mark, const_ready)
                for t in range(n):
                    m = pe.do(TE.transpose, bank.ap[:, t * N:(t + 1) * N],
                              tok[:, (t0 + t) * P:(t0 + t + 1) * P], ident[0:N, 0:N],
                              signal=t == n - 1)
                yield
                act.wait(m, *wait)
                m2 = act.do(SC.activation, ch[:, t0:t0 + n, :],
                            bank.ap[:, 0:n * N].rearrange("p (t n) -> p t n", n=N), ACT.Copy)
                bank.free = (m2,)
                marks[key] = m2

        class Result:

            def __init__(self, ap, bank):
                self.ap, self.bank = ap, bank

            def done(self, mark):
                self.bank.free = (mark,)

        def project(bank_ap, pairs, signal=True):
            for i, (l, r) in enumerate(pairs):
                last = i == len(pairs) - 1
                m = pe.do(TE.matmul, bank_ap, l, r, start=i == 0, stop=last,
                          signal=signal and last)
            return m

        CH = dict(bq0=0, bk0=2, bq1=4, bk1=6, b1=8, g3=12, n1=13, n2=15, qn=17, kn=18)

        def ch(name, i=0):
            return chan[:, CH[name] + i:CH[name] + i + 1]

        def end_marks():
            return [(l.sem, l.sem.value) for l in (pe, act, dve, pool) if l.sem.value]

        def fence():
            marks = end_marks()
            for l in (pe, act, dve, pool):
                l.wait(*marks)
            return marks

        q_f = work.tensor("q_f", [P, 4, HALF])
        k_f = [work.tensor(f"k_f{i}", [P, 4, HALF]) for i in range(2)]
        q_feat = [work.tensor(f"q_feat{i}", [P, H // 2, HALF]) for i in range(2)]
        k_feat = [work.tensor(f"k_feat{i}", [N, H * FM]) for i in range(2)]
        v_one = [work.tensor(f"v_one{i}", [N, H, DH + 1]) for i in range(2)]
        kv = [work.tensor(f"kv{i}", [P, H // 2, 2 * (DH + 1)]) for i in range(2)]
        att0 = [work.tensor(f"att0_{i}", [N, D]) for i in range(2)]
        att0T = [work.tensor(f"att0T_{i}", [P, KC, N]) for i in range(2)]
        rden = [work.tensor(f"rden{i}", [N, H]) for i in range(2)]
        for i in range(2):
            m_v_one = dve.do(VE.memset, v_one[i][:], 1.0)
            m_kv0 = dve.do(VE.memset, kv[i][:], 0.0)
        proj, misc = banks(0, 4), banks(4, 4)
        q_feat_mark, k_f_mark, q_f_read, feat_read, kf_read, read = {}, {}, {}, {}, {}, {}

        def features(hf):
            for kind, dst, bias in ((0, q_f, "bq0"), (1, k_f[hf], "bk0")):
                for c in range(KC):
                    bank = proj.take(pe)
                    pe.wait(w0_ready, x_ready)
                    m = project(bank.ap[:, 0:HALF],
                                [(Wqkv[:, k, kind * D + c * P:kind * D + (c + 1) * P],
                                  x_ch[:, k, hf * HALF:(hf + 1) * HALF]) for k in range(KC)])
                    if kind == 0 and hf:
                        act.wait(q_f_read[hf - 1])
                        dve.wait(q_f_read[hf - 1])
                    act.wait(m)
                    dve.wait(m)
                    md = ma = None
                    for turn in range(2):
                        jd, ja = turn, 1 - turn
                        dve.wait(ma)
                        act.wait(md)

                        def half(j):
                            return (bank.ap[64 * j:64 * j + 64, 0:HALF],
                                    chan[64 * j:64 * j + 64, CH[bias] + c:CH[bias] + c + 1])

                        src, bp = half(jd)
                        md_next = dve.do(VE.tensor_scalar, dst[0:64, 2 * c + jd, :], src, bp, None,
                                         ALU.add)
                        src, bp = half(ja)
                        ma = act.do(SC.activation, dst[64:128, 2 * c + ja, :], src, ACT.Square,
                                    bias=bp)
                        md = md_next
                    bank.free = (md, ma)
                    yield
                if kind == 0:
                    q_marks = (md, ma)
                else:
                    k_f_mark[hf] = (md, ma)
            for pair in range(H // 2):
                bank = proj.take(pe)
                pe.wait(*q_marks)
                m = project(bank.ap[:, 0:HALF], [(omega[:, pair % 2 * P:(pair % 2 + 1) * P],
                                                  q_f[:, pair // 2, :])])
                act.wait(m)
                q_feat_mark[hf] = act.do(SC.activation, q_feat[hf][:, pair, :],
                                         bank.ap[:, 0:HALF], ACT.Exp)
                bank.free = (q_feat_mark[hf],)
                yield
            q_f_read[hf] = m

        def linear_attention(b):
            i, hf, lc = b % 2, b // 4, slice(b % 4 * N, (b % 4 + 1) * N)
            if b >= 2:
                act.wait(read[b - 2])
                dve.wait(read[b - 2])
            pe.wait(*k_f_mark[hf])
            for t0 in (0, 2):
                bank = misc.take(pe)
                for t in (t0, t0 + 1):
                    m = project(bank.ap[0:N, (t - t0) * 256:(t - t0 + 1) * 256],
                                [(k_f[hf][:, t, lc], omega[:])])
                act.wait(m)
                k_mark = act.do(SC.activation, k_feat[i][:, t0 * 256:(t0 + 2) * 256],
                                bank.ap[0:N, :], ACT.Exp)
                bank.free = (k_mark,)
                yield
            bank = misc.take(pe)
            m = project(bank.ap[0:N, 0:D], [(x_ch[:, k, cols(b)], Wqkv[:, k, 2 * D:])
                                            for k in range(KC)])
            dve.wait(m, m_v_one)
            v_mark = dve.do(VE.tensor_tensor, v_one[i][:, :, 0:DH],
                            bank.ap[0:N, 0:D].rearrange("p (h d) -> p h d", d=DH),
                            vbias0[:].rearrange("p (h d) -> p h d", d=DH), ALU.add)
            bank.free = (v_mark,)
            add_bias(b, bout0, w0b_ready)
            yield
            bank = misc.take(pe)
            pe.wait(k_mark, v_mark)
            W = 2 * (DH + 1)
            for pair in range(H // 2):
                m = project(bank.ap[:, pair * W:(pair + 1) * W],
                            [(k_feat[i][:, pair * P:(pair + 1) * P],
                              v_one[i][:, 2 * pair:2 * pair + 2, :].rearrange("p h d -> p (h d)"))])
            dve.wait(m, m_kv0)
            blocks = bank.ap[:, 0:H // 2 * W].rearrange("p (g w) -> p g w", w=W)
            for j in range(2):
                kv_mark = dve.do(VE.tensor_copy, kv[i][64 * j:64 * j + 64, :, (DH + 1) * j:(DH + 1) * (j + 1)],
                                 blocks[64 * j:64 * j + 64, :, (DH + 1) * j:(DH + 1) * (j + 1)])
            bank.free = (kv_mark,)
            yield
            yield
            bank = misc.take(pe)
            pe.wait(kv_mark, q_feat_mark[hf])
            for pair in range(H // 2):
                m = project(bank.ap[0:N, pair * W:(pair + 1) * W],
                            [(q_feat[hf][:, pair, lc], kv[i][:, pair, :])])
            read[b] = m
            nd = bank.ap[0:N, 0:H * (DH + 1)].rearrange("p (h d) -> p h d", d=DH + 1)
            dve.wait(m)
            m = dve.do(VE.tensor_scalar, rden[i][:], nd[:, :, DH], 1e-6, None, ALU.add)
            dve.wait(m)
            m = dve.do(VE.reciprocal, rden[i][:], rden[i][:])
            dve.wait(m)
            m = dve.do(VE.tensor_tensor, att0[i][:].rearrange("p (h d) -> p h d", d=DH),
                       nd[:, :, 0:DH], rden[i][:].unsqueeze(2).to_broadcast([N, H, DH]), ALU.mult)
            bank.free = (m,)
            yield
            marks = {}
            yield from to_channels(att0[i][:], m, KC, misc, att0T[i][:], marks, 0)
            yield
            bank = misc.take(pe)
            pe.wait(marks[0], w0b_ready)
            m = project(bank.ap[0:N, 0:D], [(att0T[i][:, k, :], Wout0[:, k, :]) for k in range(KC)])
            yield from norm(b, Result(bank.ap[0:N, 0:D], bank), m, res, res_mark[b], misc)

        weave(features(0))
        weave(features(1), linear_attention(0))
        weave(linear_attention(1), linear_attention(2))
        weave(linear_attention(3), linear_attention(4))
        weave(linear_attention(5), linear_attention(6))
        weave(linear_attention(7))

        fence()
        work.restart()

        def softmax_heads(b, scores, queries, keys, values, dv, p_sb, pT_sb, s_banks, t_banks,
                          o_bank, row_sum, nmax, chunk_rows, first, count):
            waiting = None
            for h in list(range(first, first + count)) + [None]:
                if h is not None:
                    bank = s_banks.take(pe)
                    m = project(bank.ap[0:N, 0:S], [(queries(h), keys(h))])
                    dve.wait(m)
                    mm = dve.do(VE.tensor_reduce, nmax[:, h:h + 1], bank.ap[0:N, 0:S], X, ALU.max,
                                negate=True)
                    act.wait(mm)
                    p = p_sb.take(act)
                    pm = act.do(SC.activation, p.ap, bank.ap[0:N, 0:S], ACT.Exp,
                                bias=nmax[:, h:h + 1], accum_out=row_sum[:, h:h + 1])
                    bank.free = (pm,)
                    now = (h, p, pm)
                else:
                    now = None
                if waiting is not None:
                    wh, p, pm = waiting
                    bank = t_banks.take(pe)
                    pe.wait(pm)
                    for c in range(NCH):
                        m = pe.do(TE.transpose, bank.ap[0:SCH, c * N:(c + 1) * N],
                                  p.ap[:, c * SCH:(c + 1) * SCH], ident[0:N, 0:N],
                                  signal=c == NCH - 1)
                    p.free = (m,)
                    if wh % 2:
                        pT = pT_sb.take(dve)
                        dve.wait(m)
                        m = dve.do(VE.tensor_copy, pT.ap, bank.ap[0:SCH, 0:NCH * N])
                    else:
                        pT = pT_sb.take(act)
                        act.wait(m)
                        m = act.do(SC.activation, pT.ap, bank.ap[0:SCH, 0:NCH * N], ACT.Copy)
                    bank.free = (m,)
                    ready.append((wh, pT, m))
                if len(ready) > (1 if h is not None else 0):
                    while len(ready) > (1 if h is not None else 0):
                        wh, pT, m = ready.pop(0)
                        pe.wait(m)
                        o = o_bank.ap[0:N, (wh - first) * dv:(wh - first + 1) * dv]
                        m = project(o, [(pT.ap[:, c * N:(c + 1) * N], values(c, wh))
                                        for c in range(NCH)])
                        pT.free = (m,)
                        o_mark[0] = m
                waiting = now
                yield

        ready, o_mark = [], [None]

        s1_q = [work.tensor(f"s1_q{i}", [P, KC, HPT, N]) for i in range(2)]
        s1_k = [work.tensor(f"s1_k{i}", [P, KC, S]) for i in range(2)]
        s1_v = [work.tensor(f"s1_v{i}", [SCH, NCH, D]) for i in range(2)]
        s1_p = Ring([work.tensor(f"s1_p{i}", [N, S])[:] for i in range(3)])
        s1_pT = Ring([work.tensor(f"s1_pT{i}", [SCH, NCH * N])[:] for i in range(3)])
        s1_att = [work.tensor(f"s1_att{i}", [N, D]) for i in range(2)]
        s1_attT = [work.tensor(f"s1_attT{i}", [P, KC, N]) for i in range(2)]
        s1_h = [work.tensor(f"s1_h{i}", [P, 2 * KC, N]) for i in range(2)]
        s1_sum = [work.tensor(f"s1_sum{i}", [N, H]) for i in range(2)]
        s1_max = [work.tensor(f"s1_max{i}", [N, H]) for i in range(2)]
        s_banks, t_banks, o_banks, misc = banks(0, 3), banks(3, 2), banks(5, 1), banks(6, 2)
        qkv_mark, attn_read, o_done = {}, {}, {}

        def cross0_operands(b):
            i = b % 2
            if b >= 2:
                act.wait(attn_read[b - 2])
                dve.wait(attn_read[b - 2])
            kbank_marks = []
            for c in range(KC):
                bank = misc.take(pe)
                pe.wait(w1_ready, ctx_ready[b])
                m = project(bank.ap[:, 0:S], [(Wk1[:, k, c * P:(c + 1) * P], ctx_sb[b % 3][:, k, :])
                                              for k in range(CKC)])
                act.wait(m)
                mk = act.do(SC.activation, s1_k[i][:, c, :], bank.ap[:, 0:S], ACT.Identity,
                            bias=ch("bk1", c))
                bank.free = (mk,)
                yield
            for c in range(NCH):
                bank = misc.take(pe)
                m = project(bank.ap[0:SCH, 0:D], [(ctx_sb[b % 3][:, k, c * SCH:(c + 1) * SCH],
                                                   Wv1[:, k, :]) for k in range(CKC)])
                dve.wait(m)
                mv = dve.do(VE.tensor_tensor, s1_v[i][:, c, :], bank.ap[0:SCH, 0:D], bv1[:],
                            ALU.add)
                bank.free = (mv,)
                yield
            ctx_read[b] = m
            load_ctx(b + 3)
            for c in range(KC):
                bank = misc.take(pe)
                pe.wait(x_ch_mark[b])
                m = project(bank.ap[:, 0:N], [(Wq1[:, k, c * P:(c + 1) * P], x_ch[:, k, cols(b)])
                                              for k in range(KC)])
                dve.wait(m)
                mq = dve.do(VE.scalar_tensor_tensor, s1_q[i][:, c, :, :],
                            bank.ap[:, 0:N].unsqueeze(1).to_broadcast([P, HPT, N]), ch("bq1", c),
                            headq[:].unsqueeze(2).to_broadcast([P, HPT, N]), ALU.add, ALU.mult)
                bank.free = (mq,)
                yield
            add_bias(b, b2, w1_ready)
            qkv_mark[b] = (mk, mv, mq)

        def cross0_heads(b):
            i = b % 2
            pe.wait(*qkv_mark[b])
            o = o_banks.take(pe)
            yield from softmax_heads(
                b, None, lambda h: s1_q[i][:, h // HPT, h % HPT, :],
                lambda h: s1_k[i][:, h // HPT, :],
                lambda c, h: s1_v[i][:, c, h * DH:(h + 1) * DH], DH, s1_p, s1_pT, s_banks, t_banks,
                o, s1_sum[i], s1_max[i], SCH, 0, H)
            attn_read[b] = o_mark[0]
            dve.wait((act.sem, act.sem.value))
            m = dve.do(VE.reciprocal, s1_sum[i][:], s1_sum[i][:])
            dve.wait(m, attn_read[b])
            m = dve.do(VE.tensor_tensor, s1_att[i][:].rearrange("p (h d) -> p h d", d=DH),
                       o.ap[0:N, 0:D].rearrange("p (h d) -> p h d", d=DH),
                       s1_sum[i][:].unsqueeze(2).to_broadcast([N, H, DH]), ALU.mult)
            o.free = (m,)
            o_done[b] = m

        def cross0_out(b):
            i = b % 2
            marks = {}
            yield from to_channels(s1_att[i][:], o_done[b], KC, misc, s1_attT[i][:], marks, 0)
            yield
            bank = misc.take(pe)
            pe.wait(marks[0])
            for f in range(2 * KC):
                m = project(bank.ap[:, f * N:(f + 1) * N],
                            [(W1[:, k, f * P:(f + 1) * P], s1_attT[i][:, k, :]) for k in range(KC)])
            yield
            act.wait(m)
            for f in range(2 * KC):
                mh = act.do(SC.activation, s1_h[i][:, f, :], bank.ap[:, f * N:(f + 1) * N],
                            ACT.Relu, bias=ch("b1", f))
            bank.free = (mh,)
            yield
            bank = misc.take(pe)
            pe.wait(mh)
            m = project(bank.ap[0:N, 0:D], [(s1_h[i][:, k, :], W2[:, k, :]) for k in range(2 * KC)])
            yield
            yield from norm(b, Result(bank.ap[0:N, 0:D], bank), m, res, res_mark[b], misc)

        for t in range(-1, B + 1):
            weave(cross0_heads(t) if 0 <= t < B else None,
                  cross0_out(t - 1) if t >= 1 else None,
                  cross0_operands(t + 1) if t + 1 < B else None)

        fence()
        work.restart()
        misc = banks(0, 8)
        R = [N, B, E0]
        logit = work.tensor("logit", R)
        prob = work.tensor("prob", R)
        top = work.tensor("top", R)
        top_i = work.tensor("top_i", R, U32)
        small = work.tensor("small", [N, 8, B])
        e_k = work.tensor("e_k", [N, 2, B])
        w_k = work.tensor("w_k", [N, 2, B])
        pick = [work.tensor(f"pick{k}", R) for k in range(2)]
        dense = work.tensor("dense", R)
        tmp = work.tensor("tmp", R)
        part = work.tensor("part", [N, B, P], BF16)
        pick16 = work.tensor("pick16", [N, 2, B, P], BF16)
        partT = work.tensor("partT", [P, T], BF16)
        pickT = work.tensor("pickT", [P, 2, B, N], BF16)
        junk = [work.tensor(f"junk{i}", [N, HALF]) for i in range(3)]
        cnt = work.tensor("cnt", [N, 2, B, 4])
        rank = work.tensor("rank", [N, 2, B])
        kept = work.tensor("kept", [N, 2, B])
        slot = work.tensor("slot", [N, 2, B])
        slot2 = work.tensor("slot2", [N, 2, B])
        put_i = work.tensor("put_i", [N, 2, B], U32)
        get_i = work.tensor("get_i", [N, 2, B], U32)

        bank = misc.take(pe)
        lg = bank.ap[0:N, 0:B * E0].rearrange("p (b e) -> p b e", e=E0)
        pe.wait(w2_ready)
        for b in range(B):
            pe.wait(x_ch_mark[b])
            m = project(bank.ap[0:N, b * E0:(b + 1) * E0],
                        [(x_ch[:, k, cols(b)], router[:, k, :]) for k in range(KC)])

        def chain(first, *steps):
            m = first
            for op, args, kw in steps:
                dve.wait(m)
                m = dve.do(op, *args, **kw)
            return m

        def st(op, *args, **kw):
            return (op, args, kw)

        def wide(t):
            return t.unsqueeze(2).to_broadcast(R)

        m_set = dve.do(VE.memset, part[:], 0.0)
        m_set = dve.do(VE.memset, pick16[:], 0.0)
        m_set = dve.do(VE.memset, cnt[:], 0.0)
        mx, den = small[:, 0, :], small[:, 1, :]
        m = chain(m,
                  st(VE.tensor_reduce, mx, lg, X, ALU.max),
                  st(VE.tensor_tensor, logit[:], lg, wide(mx), ALU.subtract))
        bank.free = (m,)
        act.wait(m)
        m = act.do(SC.activation, prob[:], logit[:], ACT.Exp)
        m = chain(m,
                  st(VE.tensor_reduce, den, prob[:], X, ALU.add),
                  st(VE.reciprocal, den, den),
                  st(VE.tensor_tensor, prob[:], prob[:], wide(den), ALU.mult))
        dve.wait(m)
        for b in range(B):
            m = dve.do(VE.max, top[:, b, :], prob[:, b, :])
        dve.wait(m)
        for b in range(B):
            m = dve.do(VE.max_index, top_i[:, b, :], top[:, b, :], prob[:, b, :])
        tsum = small[:, 2, :]
        m = chain(m,
                  st(VE.tensor_tensor, tsum, top[:, :, 0], top[:, :, 1], ALU.add),
                  st(VE.tensor_scalar, tsum, tsum, 1e-6, None, ALU.add),
                  st(VE.reciprocal, tsum, tsum))
        dve.wait(m)
        for k in range(2):
            dve.do(VE.tensor_tensor, w_k[:, k, :], top[:, :, k], tsum, ALU.mult)
            m = dve.do(VE.tensor_copy, e_k[:, k, :], top_i[:, :, k])
        dve.wait(m)
        for k in range(2):
            m = dve.do(VE.tensor_tensor, pick[k][:], iota8[:].unsqueeze(1).to_broadcast(R),
                       wide(e_k[:, k, :]), ALU.is_equal)
        m = chain(m,
                  st(VE.tensor_tensor, dense[:], pick[0][:], wide(w_k[:, 0, :]), ALU.mult),
                  st(VE.tensor_tensor, tmp[:], pick[1][:], wide(w_k[:, 1, :]), ALU.mult),
                  st(VE.tensor_tensor, dense[:], dense[:], tmp[:], ALU.add),
                  st(VE.tensor_tensor, tmp[:], pick[0][:], pick[1][:], ALU.add),
                  st(VE.scalar_tensor_tensor, dense[:], tmp[:], -1.0, dense[:], ALU.add, ALU.add),
                  st(VE.tensor_copy, part[:, :, 0:E0], dense[:]),
                  st(VE.tensor_tensor, tmp[:], dense[:], part[:, :, 0:E0], ALU.subtract),
                  st(VE.tensor_copy, part[:, :, E0:2 * E0], tmp[:]),
                  st(VE.tensor_tensor, part[:, :, 2 * E0:3 * E0], tmp[:], part[:, :, E0:2 * E0],
                     ALU.subtract))
        dve.wait(m)
        for k in range(2):
            for j in range(3):
                m = dve.do(VE.tensor_copy, pick16[:, k, :, j * E0:(j + 1) * E0], pick[k][:])

        def transpose16(src, n, dst, m):
            i = misc.at % 8
            bank = misc.take(pe)
            pe.wait(m, m_ident16)
            for t in range(n):
                m = pe.do(TE.transpose, psum16[:, i, t * N:(t + 1) * N], src(t),
                          ident16[0:N, 0:N], signal=t == n - 1)
            act.wait(m)
            m = act.do(SC.activation, dst, psum16[:, i, 0:n * N], ACT.Copy)
            bank.free = (m,)
            return m

        m_partT = transpose16(lambda t: part[:, t, :], B, partT[:], m)
        for k in range(2):
            m_pickT = transpose16(lambda t: pick16[:, k, t, :], B,
                                  pickT[:, k, :, :].rearrange("p b n -> p (b n)"), m)
        pe.wait(m_partT, m_pickT)
        jmark = [None] * 3
        jn = 0
        for k in range(2):
            for b in range(B):
                halves = []
                for hf in range(2):
                    bank = misc.take(pe)
                    m = project(bank.ap[0:N, 0:HALF],
                                [(pickT[:, k, b, :], partT[:, hf * HALF:(hf + 1) * HALF])])
                    halves.append((bank, m))
                w = w_k[:, k, b:b + 1]
                col = 0
                for hf, (bank, m) in enumerate(halves):
                    dve.wait(m)
                    cut = min(max(b - 4 * hf, 0), 4) * N
                    for lo, hi, op in ((0, cut, ALU.is_ge), (cut, HALF, ALU.is_gt)):
                        if hi > lo:
                            dve.wait(jmark[jn % 3])
                            jmark[jn % 3] = dve.do(
                                VE.tensor_scalar, junk[jn % 3][:, lo:hi], bank.ap[0:N, lo:hi], w,
                                None, op, ALU.add, accum_out=cnt[:, k, b, col:col + 1])
                            jn += 1
                            col += 1
                    if b // 4 == hf:
                        own = slice(b % 4 * N, (b % 4 + 1) * N)
                        dve.wait(jmark[jn % 3])
                        jmark[jn % 3] = dve.do(
                            VE.scalar_tensor_tensor, junk[jn % 3][:, own], bank.ap[0:N, own], w,
                            before[:], ALU.is_equal, ALU.mult, accum_out=cnt[:, k, b, 3:4])
                        jn += 1
                    bank.free = (jmark[(jn - 1) % 3],)
        m = chain((dve.sem, dve.sem.value),
                  st(VE.tensor_reduce, rank[:], cnt[:], X, ALU.add),
                  st(VE.tensor_scalar, kept[:], rank[:], float(CAP), None, ALU.is_lt),
                  st(VE.tensor_scalar, slot[:], rank[:], float(CAP - 1), None, ALU.min),
                  st(VE.scalar_tensor_tensor, slot[:], e_k[:], float(CAP), slot[:], ALU.mult,
                     ALU.add),
                  st(VE.tensor_copy, get_i[:], slot[:]),
                  st(VE.tensor_tensor, slot2[:], slot[:],
                     slot_tab[:].rearrange("p (k b) -> p k b", k=2), ALU.subtract),
                  st(VE.tensor_tensor, slot2[:], slot2[:], kept[:], ALU.mult),
                  st(VE.tensor_tensor, slot2[:], slot2[:],
                     slot_tab[:].rearrange("p (k b) -> p k b", k=2), ALU.add),
                  st(VE.tensor_copy, put_i[:], slot2[:]),
                  st(VE.tensor_tensor, w_k[:], w_k[:], kept[:], ALU.mult))
        s_put = sem("dma_put")
        pool.wait(m, disp_zeroed)
        for k in range(2):
            for b in range(B):
                put = pool.dma(GP.indirect_dma_start, s_put, disp[:, :],
                               bass.IndirectOffsetOnAxis(put_i[:, k, b:b + 1], axis=0),
                               x_tok[:, b, :], None)
        m_slots = m

        e_in = [work.tensor(f"e_in{i}", [HC, 2, D]) for i in range(2)]
        e_inT = [work.tensor(f"e_inT{i}", [P, KC, CAP]) for i in range(2)]
        silu = Ring([work.tensor(f"silu{i}", [P, CAP])[:] for i in range(3)])
        hid0 = [work.tensor(f"hid0_{i}", [P, F0 // P, CAP]) for i in range(2)]
        e_out = [work.tensor(f"e_out{i}", [HC, 2, D]) for i in range(2)]
        s_in = [sem(f"dma_e_in{i}") for i in range(2)]
        s_out = [sem(f"dma_e_out{i}") for i in range(2)]
        in_mark, inT_mark, hid_mark, inT_read, hid_read, eo_mark = {}, {}, {}, {}, {}, {}
        in_read = {}
        FT = F0 // P

        def expert_in(e):
            i = e % 2
            sp.wait(put)
            if e >= 2:
                sp.wait(in_read[e - 2])
            in_mark[e] = sp.dma(SY.dma_start, s_in[i], e_in[i][:],
                                disp[e * CAP:(e + 1) * CAP, :].rearrange("(t p) d -> p t d", p=HC))
            yield
            yield
            bank = misc.take(pe)
            pe.wait(in_mark[e])
            for c in range(KC):
                for t in range(2):
                    m = pe.do(TE.transpose, bank.ap[:, c * CAP + t * HC:c * CAP + (t + 1) * HC],
                              e_in[i][:, t, c * P:(c + 1) * P], ident[0:HC, 0:HC],
                              signal=c == 1 and t == 1)
            in_read[e] = m
            yield
            act.wait(m)
            if e >= 2:
                act.wait(inT_read[e - 2])
            inT_mark[e] = act.do(SC.activation, e_inT[i][:],
                                 bank.ap[:, 0:KC * CAP].rearrange("p (c s) -> p c s", c=KC),
                                 ACT.Copy)
            bank.free = (inT_mark[e],)

        def expert_up(e):
            i, r = e % 2, e % NEB
            pe.wait(inT_mark[e], expert_ready[e])
            if e >= 2:
                dve.wait(hid_read[e - 2])
            for f in range(FT):
                bank = misc.take(pe)
                for j, w in enumerate((wg_sb, wu_sb)):
                    m = project(bank.ap[:, j * CAP:(j + 1) * CAP],
                                [(w[r][:, k, f * P:(f + 1) * P], e_inT[i][:, k, :])
                                 for k in range(KC)])
                s = silu.take(act)
                act.wait(m)
                ms = act.do(SC.activation, s.ap, bank.ap[:, 0:CAP], ACT.Silu)
                dve.wait(ms, m)
                hid_mark[e] = dve.do(VE.tensor_tensor, hid0[i][:, f, :], bank.ap[:, CAP:2 * CAP],
                                     s.ap, ALU.mult)
                s.free = (hid_mark[e],)
                bank.free = (hid_mark[e],)
                yield
            inT_read[e] = m

        def expert_down(e):
            i, r = e % 2, e % NEB
            bank = misc.take(pe)
            pe.wait(hid_mark[e])
            for t in range(2):
                m = project(bank.ap[0:HC, t * D:(t + 1) * D],
                            [(hid0[i][:, f, t * HC:(t + 1) * HC], wd_sb[r][:, f, :])
                             for f in range(FT)])
                yield
            hid_read[e] = m
            expert_read[e] = m
            if e + NEB < E0:
                load_expert(e + NEB)
            dve.wait(m)
            if e >= 2:
                dve.wait(eo_mark[e - 2])
            m = dve.do(VE.tensor_copy, e_out[i][:].rearrange("p t d -> p (t d)"),
                       bank.ap[0:HC, :])
            bank.free = (m,)
            act.wait(m)
            eo_mark[e] = act.dma(SC.dma_start, s_out[i],
                                 eout[e * CAP:(e + 1) * CAP, :].rearrange("(t p) d -> p t d", p=HC),
                                 e_out[i][:])

        for t in range(-1, E0 + 1):
            weave(expert_up(t) if 0 <= t < E0 else None,
                  expert_down(t - 1) if t >= 1 else None,
                  expert_in(t + 1) if t + 1 < E0 else None)
        got = [[work.tensor(f"got{k}_{i}", [N, D]) for i in range(4)] for k in range(2)]
        s_get = [sem(f"dma_get{i}") for i in range(4)]
        pool.wait(eo_mark[E0 - 1], eo_mark[E0 - 2])
        get_mark, got_read = {}, {}

        def combine(b):
            i = b % 4
            if b >= 4:
                pool.wait(got_read[b - 4])
            for k in range(2):
                m = pool.dma(GP.indirect_dma_start, s_get[i], got[k][i][:], None, eout[:, :],
                             bass.IndirectOffsetOnAxis(get_i[:, k, b:b + 1], axis=0))
            yield
            dve.wait(m, put)
            m = dve.do(VE.scalar_tensor_tensor, res[:, b, :], got[0][i][:], w_k[:, 0, b:b + 1],
                       x_tok[:, b, :], ALU.mult, ALU.add)
            dve.wait(m)
            m = dve.do(VE.scalar_tensor_tensor, res[:, b, :], got[1][i][:], w_k[:, 1, b:b + 1],
                       res[:, b, :], ALU.mult, ALU.add)
            got_read[b] = m
            yield from norm(b, None, None, res, m, misc)

        for b in range(0, B, 2):
            weave(combine(b), combine(b + 1))

        fence()
        work.restart()
        ring.restart()
        proj, sbk, ybk, misc = banks(0, 2), banks(2, 2), banks(4, 2), banks(6, 2)
        s3_q = [work.tensor(f"s3_q{i}", [P, KC, HPT, N]) for i in range(2)]
        s3_k = [work.tensor(f"s3_k{i}", [P, KC, N]) for i in range(2)]
        s3_v = [work.tensor(f"s3_v{i}", [N, HW]) for i in range(2)]
        s3_sq = Ring([work.tensor(f"s3_sq{i}", [N, 4, N])[:] for i in range(2)])
        s3_a = Ring([work.tensor(f"s3_a{i}", [N, 4, N])[:] for i in range(3)])
        s3_y = work.tensor("s3_y", [N, HW])
        s3_y2 = work.tensor("s3_y2", [N, HW])
        s3_yT = [work.tensor(f"s3_yT{i}", [P, HW // P, N]) for i in range(2)]
        s3_ms = [work.tensor(f"s3_ms{i}", [N, H]) for i in range(2)]
        s3_rms = [work.tensor(f"s3_rms{i}", [N, H]) for i in range(2)]
        s_w4 = sem("dma_w4")
        sp.wait(*end_marks())
        Wq4, _ = load(ring, "Wq4", [P, KC, HW], s_w4)
        Wk4, _ = load(ring, "Wk4", [CK, CKC, HW], s_w4)
        Wv4, _ = load(ring, "Wv4", [CK, CKC, HW], s_w4)
        Wo4, _ = load(ring, "Wo4", [P, HW // P, D], s_w4)
        bout4, _ = load(ring, "bout4", [N, D], s_w4)
        w4_ready = (s_w4, s_w4.value)
        s4_att = ring.tensor("s4_att", [N, HW])
        s4_attT = ring.tensor("s4_attT", [P, HW // P, N])

        pool.wait(w3_ready)
        m_wo3 = pool.do(GP.tensor_scalar, Wo3[:], Wo3[:], ch("g3"), None, ALU.mult)
        qkv3, y3, read3, yT_read = {}, {}, {}, {}

        def quad_operands(b):
            i = b % 2
            pe.wait(w3_ready, x_ch_mark[b])
            if b >= 2:
                act.wait(read3[b - 2])
                dve.wait(read3[b - 2])
            for c in range(KC):
                bank = proj.take(pe)
                m = project(bank.ap[:, 0:N], [(Wq3[:, k, c * P:(c + 1) * P], x_ch[:, k, cols(b)])
                                              for k in range(KC)])
                m = project(bank.ap[:, N:2 * N], [(Wk3[:, k, c * P:(c + 1) * P], x_ch[:, k, cols(b)])
                                                  for k in range(KC)])
                dve.wait(m)
                mq = dve.do(VE.tensor_tensor, s3_q[i][:, c, :, :],
                            bank.ap[:, 0:N].unsqueeze(1).to_broadcast([P, HPT, N]),
                            headq[:].unsqueeze(2).to_broadcast([P, HPT, N]), ALU.mult)
                act.wait(mq)
                mk = act.do(SC.activation, s3_k[i][:, c, :], bank.ap[:, N:2 * N], ACT.Copy)
                bank.free = (mq, mk)
                yield
            for c in range(2):
                bank = proj.take(pe)
                m = project(bank.ap[0:N, :], [(x_ch[:, k, cols(b)], Wv3[:, k, c * 512:(c + 1) * 512])
                                              for k in range(KC)])
                if c:
                    dve.wait(m)
                    mv2 = dve.do(VE.tensor_copy, s3_v[i][:, 512:], bank.ap[0:N, :])
                    bank.free = (mv2,)
                else:
                    act.wait(m)
                    mv = act.do(SC.activation, s3_v[i][:, 0:512], bank.ap[0:N, :], ACT.Copy)
                    bank.free = (mv,)
                yield
            qkv3[b] = (mq, mk, mv, mv2)

        def quad_heads(b):
            i = b % 2
            pe.wait(*qkv3[b])
            held = []
            ybank = None
            for g in list(range(4)) + [None]:
                if g is not None:
                    bank = sbk.take(pe)
                    c, h0 = g // 2, g % 2 * 4
                    m = project(bank.ap[0:N, 0:4 * N],
                                [(s3_k[i][:, c, :],
                                  s3_q[i][:, c, h0:h0 + 4, :].rearrange("p h n -> p (h n)"))])
                    s = s3_sq.take(act)
                    act.wait(m)
                    m = act.do(SC.activation, s.ap,
                               bank.ap[0:N, 0:4 * N].rearrange("p (h n) -> p h n", n=N),
                               ACT.Square, bias=1.0)
                    bank.free = (m,)
                    q = s3_a.take(dve)
                    dve.wait(m)
                    m = dve.do(VE.scalar_tensor_tensor, q.ap, s.ap, 1.0,
                               half_causal[:].unsqueeze(1).to_broadcast([N, 4, N]), ALU.add,
                               ALU.mult)
                    s.free = (m,)
                    held.append((g, q, m))
                if len(held) > 1 or g is None:
                    pg, q, m = held.pop(0)
                    if pg % 2 == 0:
                        ybank = ybk.take(pe)
                    pe.wait(m)
                    for j in range(4):
                        h = pg * 4 + j
                        m = project(ybank.ap[0:N, h % 8 * DHW:(h % 8 + 1) * DHW],
                                    [(q.ap[:, j, :], s3_v[i][:, h * DHW:(h + 1) * DHW])])
                    q.free = (m,)
                    if pg % 2:
                        y3[b, pg // 2] = (ybank, m)
                yield
            read3[b] = m

        def quad_out(b):
            i = b % 2
            for j in range(2):
                bank, m = y3[b, j]
                act.wait(m)
                if (b - 1, "y2") in y3:
                    act.wait(y3[b - 1, "y2"])
                m = act.do(SC.activation, s3_y2[:, j * 512:(j + 1) * 512], bank.ap[0:N, :],
                           ACT.Square)
                dve.wait(m)
                m = dve.do(VE.tensor_reduce, s3_ms[i][:, j * 8:(j + 1) * 8],
                           s3_y2[:, j * 512:(j + 1) * 512].rearrange("p (h d) -> p h d", d=DHW),
                           X, ALU.add)
            y3[b, "y2"] = m
            dve.wait(m)
            m = dve.do(VE.tensor_scalar, s3_ms[i][:], s3_ms[i][:], 1.0 / DHW, RMS1_EPS, ALU.mult,
                       ALU.add)
            m = power(s3_rms[i][:], s3_ms[i][:], m)
            yield
            dve.wait(m)
            if (b - 1, "yread") in y3:
                dve.wait(y3[b - 1, "yread"])
            for j in range(2):
                bank, _ = y3[b, j]
                m = dve.do(VE.tensor_tensor,
                           s3_y[:, j * 512:(j + 1) * 512].rearrange("p (h d) -> p h d", d=DHW),
                           bank.ap[0:N, :].rearrange("p (h d) -> p h d", d=DHW),
                           s3_rms[i][:, j * 8:(j + 1) * 8].unsqueeze(2).to_broadcast([N, 8, DHW]),
                           ALU.mult)
                bank.free = (m,)
            yield
            marks = {}
            yield from to_channels(s3_y[:], m, HW // P, misc, s3_yT[i][:], marks, 0)
            y3[b, "yread"] = (pe.sem, pe.sem.value)
            yield
            bank = misc.take(pe)
            pe.wait(marks[0], m_wo3)
            m = project(bank.ap[0:N, 0:D], [(s3_yT[i][:, k, :], Wo3[:, k, :])
                                            for k in range(HW // P)])
            yield
            yield from norm(b, Result(bank.ap[0:N, 0:D], bank), m, x_tok, x_tok_mark[b], misc)

        for t in range(-1, B + 1):
            weave(quad_out(t - 1) if t >= 1 else None,
                  quad_operands(t + 1) if t + 1 < B else None,
                  quad_heads(t) if 0 <= t < B else None)

        fence()
        work.restart()
        wts.restart()
        s_w5, s_w5b = sem("dma_w5"), sem("dma_w5b")
        sp.wait(*end_marks())
        ffn_w = {}
        for name, shape in (("wq5", [P, KC, D]), ("wk5", [P, KC, D]), ("wv5", [P, KC, D]),
                            ("wo5", [P, KC, KEPT]), ("gate5", [P, KC, E1])):
            ffn_w[name], _ = load(ring if name != "gate5" else wts, name, shape, s_w5)
        w5_ready = (s_w5, s_w5.value)
        HT = HID // P
        for name, shape in (("e0_up", [P, KC, HID]), ("e1_w1", [P, KC, HID]),
                            ("e1_w2", [P, KC, HID]), ("e2_l1", [P, KC, HID]),
                            ("e2_l2", [P, HT, HID]), ("e2_l3", [P, HT, HID]),
                            ("e3_down", [P, KC, D]), ("e3_up", [P, KC, HID]),
                            ("e0_down", [P, HT, KEPT]), ("e1_down", [P, HT, KEPT]),
                            ("e2_l4", [P, HT, KEPT]), ("e3_out", [P, HT, KEPT])):
            ffn_w[name], _ = load(wts, name, shape, s_w5b)
        w5b_ready = (s_w5b, s_w5b.value)

        s_banks, t_banks, o_banks, misc = banks(0, 3), banks(3, 2), banks(5, 1), banks(6, 2)
        s4_q = [work.tensor(f"s4_q{i}", [P, H, N]) for i in range(2)]
        s4_k = [work.tensor(f"s4_k{i}", [P, HW // P, S]) for i in range(2)]
        s4_v = [work.tensor(f"s4_v{i}", [SCH, NCH, HW]) for i in range(1)]
        s4_p = Ring([work.tensor(f"s4_p{i}", [N, S])[:] for i in range(2)])
        s4_pT = Ring([work.tensor(f"s4_pT{i}", [SCH, NCH * N])[:] for i in range(2)])
        s4_sum = [work.tensor(f"s4_sum{i}", [N, H]) for i in range(2)]
        s4_max = [work.tensor(f"s4_max{i}", [N, H]) for i in range(2)]
        m_q0 = dve.do(VE.memset, s4_q[0][:], 0.0)
        m_q0 = dve.do(VE.memset, s4_q[1][:], 0.0)
        qk4, v4, read4, att4, att_read = {}, {}, {}, {}, {}

        def cross1_operands(b):
            i = b % 2
            if b >= 2:
                act.wait(read4[b - 2])
                dve.wait(read4[b - 2])
            cb = ctx_sb[(B + b) % 3]
            pe.wait(w4_ready, ctx_ready[B + b])
            act.wait(m_q0)
            dve.wait(m_q0)
            for t in range(HW // P):
                bank = misc.take(pe)
                m = project(bank.ap[:, 0:S], [(Wk4[:, k, t * P:(t + 1) * P], cb[:, k, :])
                                              for k in range(CKC)])
                if t % 2:
                    dve.wait(m)
                    mk = dve.do(VE.tensor_copy, s4_k[i][:, t, :], bank.ap[:, 0:S])
                    mkd = mk
                else:
                    act.wait(m)
                    mk = act.do(SC.activation, s4_k[i][:, t, :], bank.ap[:, 0:S], ACT.Copy)
                    mka = mk
                bank.free = (mk,)
                yield
            pe.wait(x_ch_mark[b])
            for t in range(HW // P):
                bank = misc.take(pe)
                m = project(bank.ap[:, 0:N], [(Wq4[:, k, t * P:(t + 1) * P], x_ch[:, k, cols(b)])
                                              for k in range(KC)])
                act.wait(m)
                dve.wait(m)
                ma = act.do(SC.activation, s4_q[i][0:64, 2 * t, :], bank.ap[0:64, 0:N], ACT.Copy,
                            scale=DHW ** -0.5)
                md = dve.do(VE.tensor_scalar, s4_q[i][64:128, 2 * t + 1, :], bank.ap[64:128, 0:N],
                            DHW ** -0.5, None, ALU.mult)
                bank.free = (ma, md)
                if t % 2:
                    yield
            qk4[b] = (mka, mkd, ma, md)
            add_bias(b, bout4, w4_ready)

        def cross1_values(b):
            cb = ctx_sb[(B + b) % 3]
            if b:
                act.wait(read4[b - 1])
                dve.wait(read4[b - 1])
            for c in range(NCH):
                for j in range(2):
                    bank = misc.take(pe)
                    pe.wait(w4_ready, ctx_ready[B + b])
                    m = project(bank.ap[0:SCH, :],
                                [(cb[:, k, c * SCH:(c + 1) * SCH], Wv4[:, k, j * 512:(j + 1) * 512])
                                 for k in range(CKC)])
                    if j:
                        dve.wait(m)
                        mv = dve.do(VE.tensor_copy, s4_v[0][:, c, 512:], bank.ap[0:SCH, :])
                        mvd = mv
                    else:
                        act.wait(m)
                        mv = act.do(SC.activation, s4_v[0][:, c, 0:512], bank.ap[0:SCH, :],
                                    ACT.Copy)
                        mva = mv
                    bank.free = (mv,)
            v4[b] = (mva, mvd)
            ctx_read[B + b] = m
            if B + b + 3 < 2 * B:
                load_ctx(B + b + 3)
            yield

        def cross1_heads(b):
            i = b % 2
            pe.wait(*qk4[b])
            pe.wait(*v4[b])
            for half in range(2):
                o = o_banks.take(pe)
                yield from softmax_heads(
                    b, None, lambda h: s4_q[i][:, h, :], lambda h: s4_k[i][:, h // 2, :],
                    lambda c, h: s4_v[0][:, c, h * DHW:(h + 1) * DHW], DHW, s4_p, s4_pT, s_banks,
                    t_banks, o, s4_sum[i], s4_max[i], SCH, half * 8, 8)
                read4[b] = o_mark[0]
                hs = slice(half * 8, half * 8 + 8)
                dve.wait((act.sem, act.sem.value), att_read.get(b - 1))
                m = dve.do(VE.reciprocal, s4_sum[i][:, hs], s4_sum[i][:, hs])
                dve.wait(m, read4[b])
                m = dve.do(VE.tensor_tensor,
                           s4_att[:, half * 512:(half + 1) * 512].rearrange("p (h d) -> p h d", d=DHW),
                           o.ap[0:N, :].rearrange("p (h d) -> p h d", d=DHW),
                           s4_sum[i][:, hs].unsqueeze(2).to_broadcast([N, 8, DHW]), ALU.mult)
                o.free = (m,)
            att4[b] = m

        def cross1_out(b):
            marks = {}
            yield from to_channels(s4_att[:], att4[b], HW // P, misc, s4_attT[:], marks, 0,
                                   wait=(att_read.get(("T", b - 1)),))
            att_read[b] = (pe.sem, pe.sem.value)
            yield
            bank = misc.take(pe)
            pe.wait(marks[0])
            m = project(bank.ap[0:N, 0:D], [(s4_attT[:, k, :], Wo4[:, k, :])
                                            for k in range(HW // P)])
            att_read["T", b] = m
            yield
            yield from norm(b, Result(bank.ap[0:N, 0:D], bank), m, res, res_mark[b], misc)

        for t in range(-1, B + 1):
            if 0 <= t < B:
                weave(cross1_values(t))
            weave(cross1_out(t - 1) if t >= 1 else None,
                  cross1_heads(t) if 0 <= t < B else None,
                  cross1_operands(t + 1) if t + 1 < B else None)

        fence()
        work.restart()
        proj, sbk, obk, misc = banks(0, 2), banks(2, 2), banks(4, 2), banks(6, 2)
        xf = work.tensor("xf", [P, KC, T])
        h5 = [work.tensor(f"h5_{i}", [N, D]) for i in range(2)]
        hT = [work.tensor(f"hT{i}", [P, KC, N]) for i in range(2)]
        sq5 = [work.tensor(f"sq5_{i}", [N, 2 * D]) for i in range(1)]
        ms5 = [work.tensor(f"ms5_{i}", [N, 2 * H]) for i in range(2)]
        rs5 = [work.tensor(f"rs5_{i}", [N, 2 * H]) for i in range(2)]
        qk5 = [work.tensor(f"qk5_{i}", [N, 2 * D]) for i in range(2)]
        q5 = [work.tensor(f"q5_{i}", [P, KC, N]) for i in range(2)]
        k5 = [work.tensor(f"k5_{i}", [P, KC, HPT, N]) for i in range(2)]
        v5 = [work.tensor(f"v5_{i}", [N, H, DH + 1]) for i in range(2)]
        sc5 = Ring([work.tensor(f"sc5_{i}", [N, 4, N])[:] for i in range(3)])
        pT5 = Ring([work.tensor(f"pT5_{i}", [N, 4 * N])[:] for i in range(2)])
        mx5 = [work.tensor(f"mx5_{i}", [N, H]) for i in range(2)]
        rd5 = [work.tensor(f"rd5_{i}", [N, H]) for i in range(2)]
        at5 = [work.tensor(f"at5_{i}", [N, D]) for i in range(2)]
        at5T = [work.tensor(f"at5T{i}", [P, KC, N]) for i in range(2)]
        x_in5 = work.tensor("x_in5", [N, B, D])
        for i in range(2):
            m_v5 = dve.do(VE.memset, v5[i][:], 1.0)
        qkv5, heads5 = {}, {}
        x_in5_mark = {}

        def rms_rows(b, src, src_mark, i, out_tile):
            act.wait(src_mark)
            m = act.do(SC.activation, sq5[0][:, 0:D], src, ACT.Square,
                       accum_out=ms5[i][:, 0:1])
            dve.wait(m)
            m = dve.do(VE.tensor_scalar, ms5[i][:, 0:1], ms5[i][:, 0:1], 1.0 / D, RMS_EPS,
                       ALU.mult, ALU.add)
            m = power(rs5[i][:, 0:1], ms5[i][:, 0:1], m)
            yield
            dve.wait(m)
            return dve.do(VE.tensor_scalar, out_tile, src, rs5[i][:, 0:1], None, ALU.mult)

        def ffn_operands(b):
            i = b % 2
            if b >= 2:
                for l in (act, dve, pe):
                    l.wait(*heads5[b - 2])
            if b >= 1:
                act.wait(qkv5[b - 1][0])
            pool.wait(x_tok_mark[b])
            x_in5_mark[b] = pool.do(GP.tensor_copy, x_in5[:, b, :], x_tok[:, b, :])
            m = yield from rms_rows(b, x_tok[:, b, :], x_tok_mark[b], i, h5[i][:])
            yield
            bank = misc.take(pe)
            pe.wait(m)
            for c in range(KC):
                m = pe.do(TE.transpose, bank.ap[:, c * N:(c + 1) * N],
                          h5[i][:, c * P:(c + 1) * P], ident[0:N, 0:N])
            yield
            act.wait(m)
            for c in range(KC):
                m = act.do(SC.activation, hT[i][:, c, :], bank.ap[:, c * N:(c + 1) * N], ACT.Copy,
                           scale=ch("n1", c))
            bank.free = (m,)
            yield
            bank = proj.take(pe)
            pe.wait(m, w5_ready)
            for j, w in enumerate(("wq5", "wk5")):
                m = project(bank.ap[0:N, j * D:(j + 1) * D],
                            [(hT[i][:, k, :], ffn_w[w][:, k, :]) for k in range(KC)])
            vb = proj.take(pe)
            mv = project(vb.ap[0:N, 0:D], [(hT[i][:, k, :], ffn_w["wv5"][:, k, :])
                                           for k in range(KC)])
            act.wait(m)
            ms = act.do(SC.activation, sq5[0][:], bank.ap[0:N, :], ACT.Square)
            dve.wait(ms)
            m = dve.do(VE.tensor_reduce, ms5[i][:], sq5[0][:].rearrange("p (h d) -> p h d", d=DH),
                       X, ALU.add)
            dve.wait(m)
            m = dve.do(VE.tensor_scalar, ms5[i][:], ms5[i][:], 1.0 / DH, RMS_EPS, ALU.mult,
                       ALU.add)
            m = power(rs5[i][:], ms5[i][:], m)
            act.wait(mv, m_v5)
            mv = act.do(SC.activation, v5[i][:, :, 0:DH],
                        vb.ap[0:N, 0:D].rearrange("p (h d) -> p h d", d=DH), ACT.Copy)
            vb.free = (mv,)
            yield
            dve.wait(m)
            m = dve.do(VE.tensor_tensor, qk5[i][:].rearrange("p (h d) -> p h d", d=DH),
                       bank.ap[0:N, :].rearrange("p (h d) -> p h d", d=DH),
                       rs5[i][:].unsqueeze(2).to_broadcast([N, 2 * H, DH]), ALU.mult)
            bank.free = (m,)
            yield
            bank = misc.take(pe)
            pe.wait(m)
            for c in range(2 * KC):
                m = pe.do(TE.transpose, bank.ap[:, c * N:(c + 1) * N],
                          qk5[i][:, c * P:(c + 1) * P], ident[0:N, 0:N])
            yield
            act.wait(m)
            mq = act.do(SC.activation, q5[i][:],
                        bank.ap[:, 0:KC * N].rearrange("p (c n) -> p c n", n=N), ACT.Copy,
                        scale=ch("qn"))
            dve.wait(mq)
            for c in range(KC):
                mk = dve.do(VE.scalar_tensor_tensor, k5[i][:, c, :, :],
                            bank.ap[:, (KC + c) * N:(KC + c + 1) * N].unsqueeze(1)
                            .to_broadcast([P, HPT, N]), ch("kn"),
                            headq[:].unsqueeze(2).to_broadcast([P, HPT, N]), ALU.mult, ALU.mult)
            bank.free = (mq, mk)
            qkv5[b] = (mq, mk, mv)

        def ffn_heads(b):
            i = b % 2
            pe.wait(*qkv5[b])
            o = obk.take(pe)
            held, ready5 = [], []
            for g in range(6):
                if g < 4:
                    c, h0 = g // 2, g % 2 * 4
                    bank = sbk.take(pe)
                    m = project(bank.ap[0:N, 0:4 * N],
                                [(q5[i][:, c, :],
                                  k5[i][:, c, h0:h0 + 4, :].rearrange("p h n -> p (h n)"))])
                    s = sc5.take(dve)
                    dve.wait(m)
                    m = dve.do(VE.tensor_tensor, s.ap,
                               bank.ap[0:N, 0:4 * N].rearrange("p (h n) -> p h n", n=N),
                               causal_add[:].unsqueeze(1).to_broadcast([N, 4, N]), ALU.add)
                    bank.free = (m,)
                    dve.wait(m)
                    m = dve.do(VE.tensor_reduce, mx5[i][:, 4 * g:4 * g + 4], s.ap, X, ALU.max)
                    dve.wait(m)
                    m = dve.do(VE.tensor_tensor, s.ap, s.ap,
                               mx5[i][:, 4 * g:4 * g + 4].unsqueeze(2).to_broadcast([N, 4, N]),
                               ALU.subtract)
                    act.wait(m)
                    m = act.do(SC.activation, s.ap, s.ap, ACT.Exp)
                    held.append((g, s, m))
                if g >= 1 and held and (g > 4 or len(held) > 1 or g == 4):
                    pg, s, m = held.pop(0)
                    bank = misc.take(pe)
                    pe.wait(m)
                    for j in range(4):
                        m = pe.do(TE.transpose, bank.ap[0:N, j * N:(j + 1) * N], s.ap[:, j, :],
                                  ident[0:N, 0:N])
                    s.free = (m,)
                    pT = pT5.take(act)
                    act.wait(m)
                    m = act.do(SC.activation, pT.ap, bank.ap[0:N, 0:4 * N], ACT.Copy)
                    bank.free = (m,)
                    ready5.append((pg, pT, m))
                if len(ready5) > 1 or (g == 5 and ready5):
                    pg, pT, m = ready5.pop(0)
                    pe.wait(m)
                    for j in range(4):
                        h = 4 * pg + j
                        m = project(o.ap[0:N, h * (DH + 1):(h + 1) * (DH + 1)],
                                    [(pT.ap[:, j * N:(j + 1) * N], v5[i][:, h, :])])
                    pT.free = (m,)
                yield
            assert not held and not ready5
            nd = o.ap[0:N, 0:H * (DH + 1)].rearrange("p (h d) -> p h d", d=DH + 1)
            dve.wait(m)
            m = dve.do(VE.reciprocal, rd5[i][:], nd[:, :, DH])
            dve.wait(m)
            m = dve.do(VE.tensor_tensor, at5[i][:].rearrange("p (h d) -> p h d", d=DH),
                       nd[:, :, 0:DH], rd5[i][:].unsqueeze(2).to_broadcast([N, H, DH]), ALU.mult)
            o.free = (m,)
            heads5[b] = (m,)

        def ffn_attn_out(b):
            i = b % 2
            marks = {}
            yield from to_channels(at5[i][:], heads5[b][0], KC, misc, at5T[i][:], marks, 0)
            yield
            bank = misc.take(pe)
            pe.wait(marks[0])
            m = project(bank.ap[0:N, 0:KEPT], [(at5T[i][:, k, :], ffn_w["wo5"][:, k, :])
                                               for k in range(KC)])
            dve.wait(m, x_tok_mark[b], x_in5_mark[b])
            m = dve.do(VE.tensor_tensor, x_tok[:, b, 64:], x_tok[:, b, 64:],
                       bank.ap[0:N, 0:KEPT], ALU.add)
            bank.free = (m,)
            yield
            act.wait(m)
            m = act.do(SC.activation, res[:, b, :], x_tok[:, b, :], ACT.Square,
                       accum_out=meanvar[:, b, 0:1])
            dve.wait(m)
            m = dve.do(VE.tensor_scalar, meanvar[:, b, 0:1], meanvar[:, b, 0:1], 1.0 / D, RMS_EPS,
                       ALU.mult, ALU.add)
            m = power(rstd[:, b, :], meanvar[:, b, 0:1], m)
            yield
            dve.wait(m)
            m = dve.do(VE.tensor_scalar, res[:, b, :], x_tok[:, b, :], rstd[:, b, :], None,
                       ALU.mult)
            pool.wait(m)
            x_tok_mark[b] = pool.do(GP.tensor_tensor, x_tok[:, b, :], x_tok[:, b, :],
                                    x_in5[:, b, :], ALU.add)
            yield
            bank = misc.take(pe)
            pe.wait(m)
            for c in range(KC):
                m = pe.do(TE.transpose, bank.ap[:, c * N:(c + 1) * N],
                          res[:, b, c * P:(c + 1) * P], ident[0:N, 0:N])
            yield
            act.wait(m)
            for c in range(KC):
                m = act.do(SC.activation, xf[:, c, cols(b)], bank.ap[:, c * N:(c + 1) * N],
                           ACT.Copy, scale=ch("n2", c))
            bank.free = (m,)
            x_ch_mark[b] = m

        for t in range(-1, B + 1):
            weave(ffn_attn_out(t - 1) if t >= 1 else None,
                  ffn_heads(t) if 0 <= t < B else None,
                  ffn_operands(t + 1) if t + 1 < B else None)

        fence()
        work.restart(KC * T * 4)
        ring.restart()
        misc = banks(0, 8)
        lg5 = work.tensor("lg5", [N, B, E1])
        cl5 = work.tensor("cl5", [N, B, E1])
        ok5 = work.tensor("ok5", [N, B, E1], I32)
        pr5 = work.tensor("pr5", R)
        top5 = work.tensor("top5", R)
        top5_i = work.tensor("top5_i", R, U32)
        sm5 = work.tensor("sm5", [N, 4, B])
        ek5 = work.tensor("ek5", [N, 2, B])
        wt5 = work.tensor("wt5", [N, B, E1])
        tp5 = work.tensor("tp5", [N, B, E1])
        R4 = [N, B, E1]

        def wide4(t):
            return t.unsqueeze(2).to_broadcast(R4)

        bank = misc.take(pe)
        pe.wait(w5_ready)
        for b in range(B):
            pe.wait(x_ch_mark[b])
            m = project(bank.ap[0:N, b * E1:(b + 1) * E1],
                        [(xf[:, k, cols(b)], ffn_w["gate5"][:, k, :]) for k in range(KC)])
        lg = bank.ap[0:N, 0:B * E1].rearrange("p (b e) -> p b e", e=E1)
        dve.do(VE.memset, pr5[:], -1.0)
        mz = dve.do(VE.memset, cl5[:], 0.0)
        mx, den, ts = sm5[:, 0, :], sm5[:, 1, :], sm5[:, 2, :]
        FMAX = float(np.finfo(np.float32).max)
        m = chain(m,
                  st(VE.tensor_copy, tp5[:], lg),
                  st(VE.tensor_tensor, ok5[:], tp5[:], tp5[:], ALU.is_equal),
                  st(VE.tensor_scalar, lg5[:], tp5[:], FMAX, -FMAX, ALU.min, ALU.max),
                  st(VE.copy_predicated, cl5[:], ok5[:], lg5[:]),
                  st(VE.tensor_reduce, mx, cl5[:], X, ALU.max),
                  st(VE.tensor_tensor, lg5[:], cl5[:], wide4(mx), ALU.subtract))
        bank.free = (m,)
        act.wait(m)
        m = act.do(SC.activation, tp5[:], lg5[:], ACT.Exp)
        m = chain(m,
                  st(VE.tensor_reduce, den, tp5[:], X, ALU.add),
                  st(VE.reciprocal, den, den),
                  st(VE.tensor_tensor, pr5[:, :, 0:E1], tp5[:], wide4(den), ALU.mult))
        dve.wait(m)
        for b in range(B):
            m = dve.do(VE.max, top5[:, b, :], pr5[:, b, :])
        dve.wait(m)
        for b in range(B):
            m = dve.do(VE.max_index, top5_i[:, b, :], top5[:, b, :], pr5[:, b, :])
        m = chain(m,
                  st(VE.tensor_tensor, ts, top5[:, :, 0], top5[:, :, 1], ALU.add),
                  st(VE.tensor_scalar, ts, ts, 1e-8, None, ALU.add),
                  st(VE.reciprocal, ts, ts))
        for k in range(2):
            dst = (wt5, tp5)[k]
            m = chain(m,
                      st(VE.tensor_copy, ek5[:, k, :], top5_i[:, :, k]),
                      st(VE.tensor_tensor, dst[:], iota8[:, 0:E1].unsqueeze(1).to_broadcast(R4),
                         wide4(ek5[:, k, :]), ALU.is_equal),
                      st(VE.tensor_tensor, sm5[:, 3, :], top5[:, :, k], ts, ALU.mult),
                      st(VE.tensor_tensor, dst[:], dst[:], wide4(sm5[:, 3, :]), ALU.mult))
        m_wt = chain(m, st(VE.tensor_tensor, wt5[:], wt5[:], tp5[:], ALU.add))

        hidden = Ring([work.tensor(f"hidden{i}", [P, HT, HALF])[:] for i in range(4)])
        silu5 = Ring([work.tensor(f"silu5_{i}", [P, HALF])[:] for i in range(2)])
        up, misc = banks(0, 4), banks(4, 4)
        for bk in up.bufs + misc.bufs:
            bk.free = (m_wt,)
        s_res = sem("dma_result")

        def layer(src, src_marks, w, kt, mt, func, sink=None):
            dst = hidden.take(act)
            for f in range(mt):
                bank = up.take(pe)
                pe.wait(w5b_ready, *src_marks)
                m = project(bank.ap[:, 0:HALF],
                            [(w[:, k, f * P:(f + 1) * P], src[:, k, :]) for k in range(kt)])
                act.wait(m)
                ma = act.do(SC.activation, dst.ap[:, f, :], bank.ap[:, 0:HALF], func)
                bank.free = (ma,)
                yield
            return dst, ma, m

        def add_expert(e, hf, buf, mark, w, first_base):
            for j in range(4):
                b = hf * 4 + j
                bank = misc.take(pe)
                pe.wait(mark)
                m = project(bank.ap[0:N, 0:KEPT],
                            [(buf.ap[:, k, j * N:(j + 1) * N], w[:, k, :]) for k in range(HT)])
                dve.wait(m, m_wt, x_tok_mark[b], acc_mark.get(b))
                acc_mark[b] = dve.do(VE.scalar_tensor_tensor, x_tok[:, b, 64:],
                                     bank.ap[0:N, 0:KEPT], wt5[:, b, e:e + 1],
                                     x_tok[:, b, 64:], ALU.mult, ALU.add)
                bank.free = (acc_mark[b],)
                yield
            buf.free = (m,)

        acc_mark = {}

        def experts(hf):
            x_half = xf[:, :, hf * HALF:(hf + 1) * HALF]
            w = ffn_w
            h0, m0, _ = yield from layer(x_half, (), w["e0_up"], KC, HT, ACT.Gelu)
            g1, m1, r1 = yield from layer(x_half, (), w["e2_l1"], KC, HT, ACT.Gelu)
            yield from add_expert(0, hf, h0, m0, w["e0_down"], None)
            g2, m2, r2 = yield from layer(g1.ap, (m1,), w["e2_l2"], HT, HT, ACT.Gelu)
            g1.free = (r2,)
            d3, md3, _ = yield from layer(x_half, (), w["e3_down"], KC, KC, ACT.Gelu)
            g3, m3, r3 = yield from layer(g2.ap, (m2,), w["e2_l3"], HT, HT, ACT.Gelu)
            g2.free = (r3,)
            u3, mu3, ru3 = yield from layer(d3.ap, (md3,), w["e3_up"], KC, HT, ACT.Gelu)
            d3.free = (ru3,)
            yield from add_expert(2, hf, g3, m3, w["e2_l4"], None)
            yield from add_expert(3, hf, u3, mu3, w["e3_out"], None)

        def expert_swiglu(hf):
            x_half = xf[:, :, hf * HALF:(hf + 1) * HALF]
            dst = hidden.take(dve)
            for f in range(HT):
                b1, b2_ = up.take(pe), up.take(pe)
                pe.wait(w5b_ready)
                m1 = project(b1.ap[:, 0:HALF],
                             [(ffn_w["e1_w1"][:, k, f * P:(f + 1) * P], x_half[:, k, :])
                              for k in range(KC)])
                s = silu5.take(act)
                act.wait(m1)
                m1 = act.do(SC.activation, s.ap, b1.ap[:, 0:HALF], ACT.Silu)
                b1.free = (m1,)
                m2 = project(b2_.ap[:, 0:HALF],
                             [(ffn_w["e1_w2"][:, k, f * P:(f + 1) * P], x_half[:, k, :])
                              for k in range(KC)])
                dve.wait(m1, m2)
                m = dve.do(VE.tensor_tensor, dst.ap[:, f, :], b2_.ap[:, 0:HALF], s.ap, ALU.mult)
                b2_.free = (m,)
                s.free = (m,)
                yield
            yield from add_expert(1, hf, dst, m, ffn_w["e1_down"], None)

        def store(b, m):
            sp.wait(m)
            sp.dma(SY.dma_start, s_res, out[b], x_fin[:, b, :])

        x_fin = x_tok

        def final(b):
            dve.wait(acc_mark[b])
            m = dve.do(VE.bn_stats, stats[:, b, :], x_tok[:, b, :])
            dve.wait(m)
            m = dve.do(VE.bn_aggr, meanvar[:, b, :], stats[:, b, :])
            dve.wait(m)
            m = dve.do(VE.tensor_scalar, meanvar[:, b, 1:2], meanvar[:, b, 1:2], LN_EPS, None,
                       ALU.add)
            yield
            m = power(rstd[:, b, :], meanvar[:, b, 1:2], m)
            yield
            dve.wait(m)
            m = dve.do(VE.tensor_scalar, res[:, b, :], x_tok[:, b, :], meanvar[:, b, 0:1],
                       rstd[:, b, :], ALU.subtract, ALU.mult)
            sp.wait(m)
            sp.dma(SY.dma_start, s_res, out[b], res[:, b, :])

        weave(expert_swiglu(0))
        weave(expert_swiglu(1))
        weave(experts(0))
        weave(experts(1), (s for b in range(4) for s in final(b)))
        weave(*[final(b) for b in range(4, 8)])
        sp.wait((s_res, s_res.value))

        block = ctx.enter_context(nc.Block())

        @block.tensor
        def _(eng):
            pe.run(eng)

        @block.scalar
        def _(eng):
            act.run(eng)

        @block.vector
        def _(eng):
            dve.run(eng)

        @block.gpsimd
        def _(eng):
            pool.run(eng)

        @block.sync
        def _(eng):
            sp.run(eng)


def layout(i):
    f = np.float32
    c = np.ascontiguousarray

    def tiles(w, p=P):
        return c(w.reshape(w.shape[0] // p, p, w.shape[1]).transpose(1, 0, 2))

    def rows(v, n):
        return c(np.broadcast_to(v, (n, v.shape[0])))

    def col(v):
        return c(v.reshape(-1, P).T)

    a = {}
    a["xT"] = tiles(c(i["x"].reshape(T, D).T))
    a["x_tok"] = c(i["x"].transpose(1, 0, 2))
    a["ctxT"] = c(i["ctx_768"].reshape(B, S, CKC, CK).transpose(0, 3, 2, 1))
    a["Wqkv"] = tiles(i["L0_attn_Wqkv"])
    bqkv = i["L0_attn_bqkv"]
    om = np.zeros((P, 4 * FM), f)
    for h in range(4):
        om[h * DH:(h + 1) * DH, h * FM:(h + 1) * FM] = i["L0_attn_omega"]
        om[64 + h * DH:64 + (h + 1) * DH, h * FM:(h + 1) * FM] = -0.5
    a["omega"] = om
    a["vbias0"] = rows(bqkv[2 * D:], N)
    a["Wout0"] = tiles(i["L0_attn_Wout"])
    a["bout0"] = rows(i["L0_attn_bout"], N)
    a["Wq1"] = tiles(i["L0_xattn_Wq"])
    a["Wk1"] = tiles(i["L0_xattn_Wk"], CK)
    a["Wv1"] = tiles(i["L0_xattn_Wv"], CK)
    a["bv1"] = rows(i["L0_xattn_bv"], SCH)
    a["W1"] = tiles(i["L0_xattn_W1"])
    a["W2"] = tiles(i["L0_xattn_W2"])
    a["b2"] = rows(i["L0_xattn_b2"], N)
    a["router"] = tiles(c(i["L0_ffn_router_w"].T))
    a["wg"] = c(i["L0_ffn_wg"].reshape(E0, KC, P, F0).transpose(0, 2, 1, 3))
    a["wu"] = c(i["L0_ffn_wu"].reshape(E0, KC, P, F0).transpose(0, 2, 1, 3))
    a["wd"] = c(i["L0_ffn_wd"].reshape(E0, F0 // P, P, D).transpose(0, 2, 1, 3))
    a["Wq3"] = tiles(c(i["L1_attn_Wq"].T))
    a["Wk3"] = tiles(c(i["L1_attn_Wk"].T))
    a["Wv3"] = tiles(c(i["L1_attn_Wv"].T))
    a["Wo3"] = tiles(c(i["L1_attn_Wo"].T))
    a["Wq4"] = tiles(i["L1_xattn_w_q"])
    a["Wk4"] = tiles(i["L1_xattn_w_k"], CK)
    a["Wv4"] = tiles(i["L1_xattn_w_v"], CK)
    a["Wo4"] = tiles(i["L1_xattn_w_out"])
    a["bout4"] = rows(i["L1_xattn_b_out"], N)
    for k, n in (("wq5", "wq"), ("wk5", "wk"), ("wv5", "wv"), ("gate5", "gate_w"),
                 ("e0_up", "e0_up"), ("e1_w1", "e1_w1"), ("e1_w2", "e1_w2"), ("e2_l1", "e2_l1"),
                 ("e2_l2", "e2_l2"), ("e2_l3", "e2_l3"), ("e3_down", "e3_down"),
                 ("e3_up", "e3_up")):
        a[k] = tiles(c(i["L1_ffn_" + n].T))
    for k, n in (("wo5", "wo"), ("e0_down", "e0_down"), ("e1_down", "e1_down"),
                 ("e2_l4", "e2_l4"), ("e3_out", "e3_out")):
        a[k] = tiles(c(i["L1_ffn_" + n].T[:, D - KEPT:]))
    a["chan"] = c(np.concatenate([
        col(bqkv[0:D]), col(bqkv[D:2 * D]), col(i["L0_xattn_bq"]), col(i["L0_xattn_bk"]),
        col(i["L0_xattn_b1"]), col(np.tile(i["L1_attn_g_weight"], 2)), col(i["L1_ffn_n1_w"]),
        col(i["L1_ffn_n2_w"]), col(np.tile(i["L1_ffn_qn_w"], HPT)),
        col(np.tile(i["L1_ffn_kn_w"], HPT))], axis=1))
    a["ident"] = np.eye(P, dtype=f)
    a["headq"] = c((np.arange(P)[:, None] // DH == np.arange(HPT)[None, :]) * f(0.25)).astype(f)
    n = np.arange(N)
    a["half_causal"] = c((n[:, None] <= n[None, :]) * f(0.5)).astype(f)
    a["causal_add"] = np.where(n[None, :] > n[:, None], f(-3e38), f(0)).astype(f)
    a["before"] = (n[None, :] < n[:, None]).astype(f)
    a["slot_tab"] = c((SLOTS + np.arange(2 * B)[None, :] * N + n[:, None])).astype(f)
    a["iota8"] = rows(np.arange(E0).astype(f), N)
    return a


def kernel(**inputs):
    import concourse.bacc as bacc
    from concourse.bass_utils import run_bass_kernel_spmd

    arrays = layout({k: np.asarray(v) for k, v in inputs.items()})
    nc = bacc.Bacc("TRN2", target_bir_lowering=False, num_devices=1)
    aps = {k: nc.dram_tensor("in_" + k, v.shape, mybir.dt.from_np(v.dtype),
                             kind="ExternalInput").ap() for k, v in arrays.items()}
    out = nc.dram_tensor("out", (B, N, D), F32, kind="ExternalOutput").ap()
    program(nc, aps, out)
    r = run_bass_kernel_spmd(nc, [{"in_" + k: v for k, v in arrays.items()}], core_ids=[0])
    return r.results[0]["out"]
```

```python
from contextlib import ExitStack

import numpy as np

import concourse.bass as bass
from concourse import mybir

F32 = mybir.dt.float32
BF16 = mybir.dt.bfloat16
F16 = mybir.dt.float16
U32 = mybir.dt.uint32
I32 = mybir.dt.int32
ALU = mybir.AluOpType
ACT = mybir.ActivationFunctionType
X = mybir.AxisListType.X

P = 128
B, N, D = 8, 112, 256
T = B * N
KC = D // P
S, DC = 375, 192
SCH = 125
NCH = S // SCH
H, DH = 16, 16
DHW = 64
HW = H * DHW
FM = 64
HALF = 4 * N
HPT = P // DH
E0, F0, CAP = 8, 1024, int(1.25 * T / 8)
SLOTS = E0 * CAP
HC = CAP // 2
E1, HID = 4, 512
KEPT = D - 64
BANK = 512
LN_EPS, RMS1_EPS, RMS_EPS = 1e-5, 1e-5, 1.1920929e-07
WSCALE = 64.0
KB = 1024
REST, REST_POWER, POWER_NS = 1500.0, 1500.0, 180.0


class Sem:

    def __init__(self, nc, ctx, name):
        self.handle = ctx.enter_context(nc.semaphore(name))
        self.value = 0

    def add(self, by):
        self.value += by
        return (self, self.value)


def size(ap):
    return int(np.prod(ap.shape[1:]))


class Lane:

    def __init__(self, nc, ctx, name):
        self.sem = Sem(nc, ctx, "done_" + name)
        self.queue = []
        self.waited = {}
        self.busy = 0.0

    def wait(self, *marks):
        for mark in marks:
            if mark is None:
                continue
            sem, value = mark
            if self.waited.get(sem, 0) < value:
                self.waited[sem] = value
                self.queue.append((None, sem, value, None))

    def do(self, op, *args, signal=True, **kw):
        self.queue.append((op, args, kw, self.sem.handle if signal else None))
        if "start" in kw:
            left, right = args[1], args[2]
            passes = 4 if left.dtype == F32 else 1
            self.busy += passes * max(size(right) / 2.4, size(left) / 1.2)
        return self.sem.add(1) if signal else None

    def dma(self, op, sem, *args, **kw):
        self.queue.append((op, args, kw, (sem.handle, 16)))
        return sem.add(16)

    def run(self, eng):
        for op, args, kw, sem in self.queue:
            if op is None:
                eng.wait_ge(args.handle, kw)
            else:
                ins = op(*args, **kw)
                if isinstance(sem, tuple):
                    ins.then_inc(sem[0], sem[1])
                elif sem is not None:
                    ins.then_inc(sem, 1)


class Buf:

    def __init__(self, ap):
        self.ap = ap
        self.free = ()


class Ring:

    def __init__(self, aps):
        self.bufs = [Buf(a) for a in aps]

    def take(self, *writers):
        buf = next(b for b in self.bufs if b.free is not None)
        self.bufs.remove(buf)
        self.bufs.append(buf)
        for lane in writers:
            lane.wait(*buf.free)
        buf.free = None
        return buf


class Region:

    def __init__(self, nc, base, size):
        self.nc, self.base, self.size, self.at = nc, base, size, 0

    def tensor(self, name, shape, dtype=F32):
        words = 1
        for n in shape[1:]:
            words *= n
        size = words * mybir.dt.size(dtype)
        size += -size % 32
        assert self.at + size <= self.size, (name, self.at, size, self.size)
        t = self.nc.alloc_sbuf_tensor_at(name, list(shape), dtype, offset=self.base + self.at)
        self.at += size
        return t

    def restart(self, at=0):
        self.at = at


class Weaver:

    def __init__(self, pe):
        self.pe, self.hurry = pe, False

    def __call__(self, *streams):
        live, passed = list(streams), 0
        while live:
            for stream in list(live):
                step = next(stream, "end")
                passed = passed + 1 if step == "pass" else 0
                self.hurry = passed >= len(live)
                assert passed <= 3 * len(live), "every stream waits for another"
                if step == "end":
                    live.remove(stream)

    def rest(self, ns):
        end = self.pe.busy + ns
        yield
        while self.pe.busy < end and not self.hurry:
            yield "pass"


def until(table, *keys):
    while any(k not in table for k in keys):
        yield "pass"


def follow(work, items):
    for i in items:
        yield from work(i)


def program(nc, a, out):
    ctx = ExitStack()
    with ctx:
        pe, act, dve, pool, sp = (Lane(nc, ctx, n) for n in ("pe", "act", "dve", "pool", "sp"))
        weave = Weaver(pe)
        rest = weave.rest
        TE, SC, VE, GP, SY = nc.tensor, nc.scalar, nc.vector, nc.gpsimd, nc.sync

        def sem(name):
            return Sem(nc, ctx, name)

        START = -(-nc.sbuf_base // 32) * 32
        ARENA = (nc.sbuf_usable_end - START) // 32 * 32
        ctx.enter_context(nc.sbuf_tensor("arena", [P, ARENA], mybir.dt.uint8))
        keep_kb, wts_kb, ring_kb = 36.5, 51.25, 48
        keep = Region(nc, START, keep_kb * KB)
        wts = Region(nc, START + int(keep_kb * KB), wts_kb * KB)
        ring = Region(nc, START + int((keep_kb + wts_kb) * KB), ring_kb * KB)
        work = Region(nc, START + int((keep_kb + wts_kb + ring_kb) * KB),
                      ARENA - int((keep_kb + wts_kb + ring_kb) * KB))

        psum = ctx.enter_context(nc.psum_tensor("psum", [P, 8, BANK], F32))
        psum16 = psum[:, :, :].bitcast(BF16)

        def banks(first, count):
            ring = Ring([psum[:, i, :] for i in range(first, first + count)])
            for i, buf in enumerate(ring.bufs):
                buf.number = first + i
            return ring

        x_tok = keep.tensor("x_tok", [N, B, D])
        x_ch = keep.tensor("x_ch", [P, KC, T])
        res = keep.tensor("res", [N, B, D])
        ctx_raw = keep.tensor("ctx_raw", [P, 2, S])
        ctx16 = [keep.tensor(f"ctx16_{i}", [P, 3, S], F16) for i in range(3)]
        ident = keep.tensor("ident", [P, P])
        ident16 = keep.tensor("ident16", [P, P], BF16)
        headq = keep.tensor("headq", [P, HPT])
        headq16 = keep.tensor("headq16", [P, HPT], F16)
        half_causal = keep.tensor("half_causal", [N, N])
        causal_add = keep.tensor("causal_add", [N, N])
        before = keep.tensor("before", [N, N])
        chan = keep.tensor("chan", [P, 19])
        stats = keep.tensor("stats", [N, B, 6])
        meanvar = keep.tensor("meanvar", [N, B, 2])
        rstd = keep.tensor("rstd", [N, B, 1])
        minus_half = keep.tensor("minus_half", [N, 2 * H])
        slot_tab = keep.tensor("slot_tab", [N, 2 * B])
        iota8 = keep.tensor("iota8", [N, E0])

        s_const, s_x = sem("dma_const"), sem("dma_x")
        for name, t in (("xT", x_ch), ("chan", chan)):
            sp.dma(SY.dma_start, s_x, t[:], a[name])
        x_ready = (s_x, s_x.value)

        def load(region, name, shape, s):
            t = region.tensor("w_" + name, shape)
            return t, sp.dma(SY.dma_start, s, t[:], a[name])

        s_w0 = sem("dma_w0")
        Wqkv, _ = load(wts, "Wqkv", [P, KC, 3 * D], s_w0)
        omega, _ = load(wts, "omega", [P, 4 * FM], s_w0)
        vbias0, _ = load(wts, "vbias0", [N, D], s_w0)
        w0_ready = (s_w0, s_w0.value)
        for name, t in (("x_tok", x_tok), ("ident", ident), ("headq", headq),
                        ("half_causal", half_causal), ("causal_add", causal_add),
                        ("before", before), ("slot_tab", slot_tab), ("iota8", iota8)):
            sp.dma(SY.dma_start, s_const, t[:], a[name])
        s_w0b = sem("dma_w0b")
        Wout0, _ = load(wts, "Wout0", [P, KC, D], s_w0b)
        bout0, _ = load(wts, "bout0", [N, D], s_w0b)
        const_ready = (s_const, s_const.value)
        w0b_ready = (s_w0b, s_w0b.value)
        s_ctx = sem("dma_ctx")
        ctx_ready, ctx_read = {}, {}

        CTX_PRODUCTS = ((0, 0), (0, 1), (2, 0), (1, 2), (1, 3))

        def load_ctx(i):
            if i:
                sp.wait(ctx_ready[i - 1])
            m = sp.dma(SY.dma_start, s_ctx, ctx_raw[:], a["ctxT"][i % B])
            t = ctx16[i % 3]
            if i >= 3:
                pool.wait(ctx_read[i - 3])
            pool.wait(m)
            pool.do(GP.tensor_copy, t[:, 0, :], ctx_raw[:, 0, :], signal=False)
            m = pool.do(GP.tensor_copy, t[:, 1, :], ctx_raw[:, 1, :])
            pool.wait(m)
            m = pool.do(GP.tensor_tensor, t[:, 2, :], ctx_raw[:, 0, :], t[:, 0, :], ALU.subtract)
            pool.wait(m)
            ctx_ready[i] = pool.do(GP.tensor_tensor, t[64:128, 1, :], ctx_raw[64:128, 1, :],
                                   t[64:128, 1, :], ALU.subtract)
            pool.wait(ctx_ready[i])

        def split_ctx_weights(w16, raw, ready):
            act.wait(ready)
            m = act.do(SC.activation, w16[:, 0::2, :], raw[:], ACT.Copy, scale=WSCALE)
            dve.wait(m)
            dve.do(VE.scalar_tensor_tensor, w16[:, 1, :], raw[:, 0, :], WSCALE, w16[:, 0, :],
                   ALU.mult, ALU.subtract)
            dve.do(VE.scalar_tensor_tensor, w16[0:64, 3, :], raw[0:64, 1, :], WSCALE,
                   w16[0:64, 2, :], ALU.mult, ALU.subtract)
            return dve.do(VE.memset, w16[64:128, 3, :], 0.0)

        s_w1 = sem("dma_w1")
        Wq1, _ = load(wts, "Wq1", [P, KC, D], s_w1)
        Wkv1, _ = load(wts, "Wkv1", [P, 2, 2 * D], s_w1)
        Wkv1_16 = wts.tensor("Wkv1_16", [P, 4, 2 * D], F16)
        bv1, _ = load(wts, "bv1", [N, D], s_w1)
        W1, _ = load(wts, "W1", [P, KC, 2 * D], s_w1)
        W2, _ = load(wts, "W2", [P, 2 * KC, D], s_w1)
        b2, _ = load(wts, "b2", [N, D], s_w1)
        w1_ready = (s_w1, s_w1.value)
        s_w2 = sem("dma_w2")
        router, _ = load(wts, "router", [P, KC, E0], s_w2)
        w2_ready = (s_w2, s_w2.value)

        MATS = (("wg", KC, F0), ("wu", KC, F0), ("wd", F0 // P, D))
        first_raw = Region(nc, ring.base + 24 * KB, 24 * KB)
        raw0 = [first_raw.tensor("raw0_" + n, [P, k, w]) for n, k, w in MATS]
        e16 = [[ring.tensor(f"{n}16_{i}", [P, 2, k, w], F16) for n, k, w in MATS]
               for i in range(2)]
        s_exp = [sem(f"dma_expert{i}") for i in range(3)]
        raw_ready = {}
        for j, (n, _, _) in enumerate(MATS):
            raw_ready[0, j] = sp.dma(SY.dma_start, s_exp[j], raw0[j][:], a[n][0])
        s_w3 = sem("dma_w3")
        Wq3, _ = load(wts, "Wq3", [P, KC, D], s_w3)
        Wk3, _ = load(wts, "Wk3", [P, KC, D], s_w3)
        Wv3, _ = load(wts, "Wv3", [P, KC, HW], s_w3)
        Wo3, _ = load(wts, "Wo3", [P, HW // P, D], s_w3)
        w3_ready = (s_w3, s_w3.value)

        disp = nc.dram_tensor("dispatched", [SLOTS + 2 * T, D], F32)
        eout = nc.dram_tensor("expert_out", [SLOTS, D], F32)

        zeros = keep.tensor("zeros", [P, D])
        m_zero = pool.do(GP.memset, zeros[:], 0.0)
        pool.do(GP.memset, minus_half[:], -0.5)
        pool.wait(const_ready)
        m_ident16 = pool.do(GP.tensor_copy, ident16[:], ident[:])
        m_headq16 = pool.do(GP.tensor_copy, headq16[:], headq[:])
        s_zero = sem("dma_zero")
        sp.wait(m_zero)
        for i in range(SLOTS // HC // 2):
            rows = disp[2 * i * HC:2 * (i + 1) * HC, :].rearrange("(t p) d -> p t d", p=HC)
            for t in range(2):
                sp.dma(SY.dma_start, s_zero, rows[:, t, :], zeros[0:HC, :])
        disp_zeroed = (s_zero, s_zero.value)

        for i in range(3):
            load_ctx(i)

        def cols(b):
            return slice(b * N, (b + 1) * N)

        x_tok_mark = {b: const_ready for b in range(B)}
        x_ch_mark = {b: x_ready for b in range(B)}
        res_mark = {}

        def add_bias(b, bias, ready):
            pool.wait(ready, x_tok_mark[b])
            res_mark[b] = pool.do(GP.tensor_tensor, res[:, b, :], x_tok[:, b, :], bias[:], ALU.add)

        def power(out_ap, in_ap, mark):
            pool.wait(mark)
            return pool.do(GP.tensor_tensor, out_ap, in_ap, minus_half[:, 0:in_ap.shape[-1]],
                           ALU.pow)

        def norm(b, y, y_mark, base, base_mark, misc):
            if y is not None:
                dve.wait(y_mark, base_mark)
                m = dve.do(VE.tensor_tensor, res[:, b, :], base[:, b, :], y.ap, ALU.add)
                y.done(m)
            else:
                m = base_mark
            dve.wait(m)
            m = dve.do(VE.bn_stats, stats[:, b, :], res[:, b, :])
            dve.wait(m)
            m = dve.do(VE.bn_aggr, meanvar[:, b, :], stats[:, b, :])
            dve.wait(m)
            m = dve.do(VE.tensor_scalar, meanvar[:, b, 1:2], meanvar[:, b, 1:2], LN_EPS, None,
                       ALU.add)
            m = power(rstd[:, b, :], meanvar[:, b, 1:2], m)
            yield from rest(REST_POWER)
            dve.wait(m)
            m = dve.do(VE.tensor_scalar, x_tok[:, b, :], res[:, b, :], meanvar[:, b, 0:1],
                       rstd[:, b, :], ALU.subtract, ALU.mult)
            x_tok_mark[b] = m
            yield from rest(REST)
            yield from to_channels(x_tok[:, b, :], m, KC, misc, x_ch[:, :, cols(b)], x_ch_mark, b)

        def to_channels(tok, mark, tiles, misc, ch, marks, key, wait=()):
            for t0 in range(0, tiles, 4):
                n = min(4, tiles - t0)
                bank = misc.take(pe)
                pe.wait(mark, const_ready)
                for t in range(n):
                    m = pe.do(TE.transpose, bank.ap[:, t * N:(t + 1) * N],
                              tok[:, (t0 + t) * P:(t0 + t + 1) * P], ident[0:N, 0:N],
                              signal=t == n - 1)
                yield from rest(REST / 2)
                act.wait(m, *wait)
                m2 = act.do(SC.activation, ch[:, t0:t0 + n, :],
                            bank.ap[:, 0:n * N].rearrange("p (t n) -> p t n", n=N), ACT.Copy)
                bank.free = (m2,)
                marks[key] = m2

        class Result:

            def __init__(self, ap, bank):
                self.ap, self.bank = ap, bank

            def done(self, mark):
                self.bank.free = (mark,)

        def project(bank_ap, pairs, signal=True):
            for i, (l, r) in enumerate(pairs):
                last = i == len(pairs) - 1
                m = pe.do(TE.matmul, bank_ap, l, r, start=i == 0, stop=last,
                          signal=signal and last)
            return m

        CH = dict(bq0=0, bk0=2, bq1=4, bk1=6, b1=8, g3=12, n1=13, n2=15, qn=17, kn=18)

        def ch(name, i=0):
            return chan[:, CH[name] + i:CH[name] + i + 1]

        def end_marks():
            return [(l.sem, l.sem.value) for l in (pe, act, dve, pool) if l.sem.value]

        def fence():
            marks = end_marks()
            for l in (pe, act, dve, pool):
                l.wait(*marks)
            return marks

        q_f = work.tensor("q_f", [P, 4, HALF])
        k_f = [work.tensor(f"k_f{i}", [P, 4, HALF]) for i in range(2)]
        q_feat = [work.tensor(f"q_feat{i}", [P, H // 2, HALF]) for i in range(2)]
        k_feat = [work.tensor(f"k_feat{i}", [N, H * FM]) for i in range(2)]
        v_one = [work.tensor(f"v_one{i}", [N, H, DH + 1]) for i in range(2)]
        kv = [work.tensor(f"kv{i}", [P, H // 2, 2 * (DH + 1)]) for i in range(2)]
        att0 = [work.tensor(f"att0_{i}", [N, D]) for i in range(2)]
        att0T = [work.tensor(f"att0T_{i}", [P, KC, N]) for i in range(2)]
        rden = [work.tensor(f"rden{i}", [N, H]) for i in range(2)]
        for i in range(2):
            m_v_one = dve.do(VE.memset, v_one[i][:], 1.0)
            m_kv0 = dve.do(VE.memset, kv[i][:], 0.0)
        proj, misc = banks(0, 4), banks(4, 4)
        done0 = {}
        q_feat_mark, k_f_mark, q_f_read, read = {}, {}, {}, {}

        def features(hf):
            for kind, dst, bias in ((0, q_f, "bq0"), (1, k_f[hf], "bk0")):
                for c in range(KC):
                    bank = proj.take(pe)
                    pe.wait(w0_ready, x_ready)
                    m = project(bank.ap[:, 0:HALF],
                                [(Wqkv[:, k, kind * D + c * P:kind * D + (c + 1) * P],
                                  x_ch[:, k, hf * HALF:(hf + 1) * HALF]) for k in range(KC)])
                    if kind == 0 and hf:
                        act.wait(q_f_read[hf - 1])
                        dve.wait(q_f_read[hf - 1])
                    act.wait(m)
                    dve.wait(m)
                    md = ma = None
                    for turn in range(2):
                        jd, ja = turn, 1 - turn
                        dve.wait(ma)
                        act.wait(md)

                        def half(j):
                            return (bank.ap[64 * j:64 * j + 64, 0:HALF],
                                    chan[64 * j:64 * j + 64, CH[bias] + c:CH[bias] + c + 1])

                        src, bp = half(jd)
                        md_next = dve.do(VE.tensor_scalar, dst[0:64, 2 * c + jd, :], src, bp, None,
                                         ALU.add)
                        src, bp = half(ja)
                        ma = act.do(SC.activation, dst[64:128, 2 * c + ja, :], src, ACT.Square,
                                    bias=bp)
                        md = md_next
                    bank.free = (md, ma)
                    yield
                if kind == 0:
                    q_marks = (md, ma)
                else:
                    k_f_mark[hf] = (md, ma)
            for pair in range(H // 2):
                bank = proj.take(pe)
                pe.wait(*q_marks)
                m = project(bank.ap[:, 0:HALF], [(omega[:, pair % 2 * P:(pair % 2 + 1) * P],
                                                  q_f[:, pair // 2, :])])
                act.wait(m)
                q_feat_mark[hf] = act.do(SC.activation, q_feat[hf][:, pair, :],
                                         bank.ap[:, 0:HALF], ACT.Exp)
                bank.free = (q_feat_mark[hf],)
                yield
            q_f_read[hf] = m
            done0[hf] = True

        def linear_attention(b):
            i, hf, lc = b % 2, b // 4, slice(b % 4 * N, (b % 4 + 1) * N)
            yield from until(done0, hf)
            if b >= 2:
                act.wait(read[b - 2])
                dve.wait(read[b - 2])
            pe.wait(*k_f_mark[hf])
            for t0 in (0, 2):
                bank = misc.take(pe)
                for t in (t0, t0 + 1):
                    m = project(bank.ap[0:N, (t - t0) * 256:(t - t0 + 1) * 256],
                                [(k_f[hf][:, t, lc], omega[:])])
                act.wait(m)
                k_mark = act.do(SC.activation, k_feat[i][:, t0 * 256:(t0 + 2) * 256],
                                bank.ap[0:N, :], ACT.Exp)
                bank.free = (k_mark,)
                yield
            bank = misc.take(pe)
            m = project(bank.ap[0:N, 0:D], [(x_ch[:, k, cols(b)], Wqkv[:, k, 2 * D:])
                                            for k in range(KC)])
            dve.wait(m, m_v_one)
            v_mark = dve.do(VE.tensor_tensor, v_one[i][:, :, 0:DH],
                            bank.ap[0:N, 0:D].rearrange("p (h d) -> p h d", d=DH),
                            vbias0[:].rearrange("p (h d) -> p h d", d=DH), ALU.add)
            bank.free = (v_mark,)
            add_bias(b, bout0, w0b_ready)
            yield
            bank = misc.take(pe)
            pe.wait(k_mark, v_mark)
            W = 2 * (DH + 1)
            for pair in range(H // 2):
                m = project(bank.ap[:, pair * W:(pair + 1) * W],
                            [(k_feat[i][:, pair * P:(pair + 1) * P],
                              v_one[i][:, 2 * pair:2 * pair + 2, :].rearrange("p h d -> p (h d)"))])
            dve.wait(m, m_kv0)
            blocks = bank.ap[:, 0:H // 2 * W].rearrange("p (g w) -> p g w", w=W)
            for j in range(2):
                kv_mark = dve.do(VE.tensor_copy,
                                 kv[i][64 * j:64 * j + 64, :, (DH + 1) * j:(DH + 1) * (j + 1)],
                                 blocks[64 * j:64 * j + 64, :, (DH + 1) * j:(DH + 1) * (j + 1)])
            bank.free = (kv_mark,)
            yield from rest(REST)
            bank = misc.take(pe)
            pe.wait(kv_mark, q_feat_mark[hf])
            for pair in range(H // 2):
                m = project(bank.ap[0:N, pair * W:(pair + 1) * W],
                            [(q_feat[hf][:, pair, lc], kv[i][:, pair, :])])
            read[b] = m
            nd = bank.ap[0:N, 0:H * (DH + 1)].rearrange("p (h d) -> p h d", d=DH + 1)
            dve.wait(m)
            m = dve.do(VE.tensor_scalar, rden[i][:], nd[:, :, DH], 1e-6, None, ALU.add)
            dve.wait(m)
            m = dve.do(VE.reciprocal, rden[i][:], rden[i][:])
            dve.wait(m)
            m = dve.do(VE.tensor_tensor, att0[i][:].rearrange("p (h d) -> p h d", d=DH),
                       nd[:, :, 0:DH], rden[i][:].unsqueeze(2).to_broadcast([N, H, DH]), ALU.mult)
            bank.free = (m,)
            yield from rest(REST)
            marks = {}
            yield from to_channels(att0[i][:], m, KC, misc, att0T[i][:], marks, 0)
            yield from rest(REST)
            bank = misc.take(pe)
            pe.wait(marks[0], w0b_ready)
            m = project(bank.ap[0:N, 0:D], [(att0T[i][:, k, :], Wout0[:, k, :]) for k in range(KC)])
            yield from norm(b, Result(bank.ap[0:N, 0:D], bank), m, res, res_mark[b], misc)

        def split_wkv1():
            yield from until(read, 1)
            later["wkv1"] = split_ctx_weights(Wkv1_16, Wkv1, w1_ready)

        later = {}
        weave(follow(features, (0, 1)), follow(linear_attention, range(0, B, 2)),
              follow(linear_attention, range(1, B, 2)), split_wkv1())

        fence()
        work.restart()

        class Heads:

            def __init__(self, dv, to_t, to_o, p_sb, pT_sb, s_banks, t_banks, o_banks):
                self.to_t, self.to_o = to_t, to_o
                self.dv, self.p_sb, self.pT_sb = dv, p_sb, pT_sb
                self.s_banks, self.t_banks, self.o_banks = s_banks, t_banks, o_banks
                self.in_t, self.in_o = [], []
                self.o = None

            def step(self, head):
                split = None
                if len(self.in_t) == self.to_t or (head is None and self.in_t):
                    old, p, m = self.in_t.pop(0)
                    bank = self.t_banks.take(pe)
                    pe.wait(m)
                    for c in range(NCH):
                        m = pe.do(TE.transpose, bank.ap[0:SCH, c * N:(c + 1) * N],
                                  p.ap[:, c * SCH:(c + 1) * SCH], ident[0:N, 0:N],
                                  signal=c == NCH - 1)
                    p.free = (m,)
                    pT = self.pT_sb.take(act, dve)
                    act.wait(m)
                    split = (bank, pT, act.do(SC.activation, pT.ap[:, 0, :],
                                              bank.ap[0:SCH, 0:NCH * N], ACT.Copy))
                if head is not None:
                    bank = self.s_banks.take(pe)
                    pe.wait(*head["qk_marks"])
                    (qh, ql), (kh, kl) = head["q"], head["k"]
                    m = project(bank.ap[0:N, 0:S], [(qh, kh), (qh, kl), (ql, kh)])
                    dve.wait(m)
                    mm = dve.do(VE.tensor_reduce, head["nmax"], bank.ap[0:N, 0:S], X, ALU.max,
                                negate=True)
                    p = self.p_sb.take(act)
                    act.wait(mm)
                    m = act.do(SC.activation, p.ap, bank.ap[0:N, 0:S], ACT.Exp, bias=head["nmax"],
                               accum_out=head["sum"])
                    bank.free = (m,)
                    head["exp"] = m
                    self.in_t.append((head, p, m))
                if split is not None:
                    bank, pT, m = split
                    dve.wait(m)
                    m = dve.do(VE.tensor_tensor, pT.ap[:, 1, :], bank.ap[0:SCH, 0:NCH * N],
                               pT.ap[:, 0, :], ALU.subtract)
                    bank.free = (m,)
                    self.in_o.append((old, pT, m))
                if self.in_o and (len(self.in_o) > self.to_o - self.to_t or head is None):
                    old, pT, m = self.in_o.pop(0)
                    dv = self.dv
                    if old["first"]:
                        self.o = self.o_banks.take(pe)
                    pe.wait(m, *old["v_marks"]())
                    at = old["at"]
                    for c in range(NCH):
                        chunk = slice(c * N, (c + 1) * N)
                        v = old["v"](c)
                        pe.do(TE.matmul, self.o.ap[0:N, at:at + 2 * dv], pT.ap[:, 0, chunk],
                              v, start=c == 0, stop=False, signal=False)
                        m = pe.do(TE.matmul, self.o.ap[0:N, at:at + dv], pT.ap[:, 1, chunk],
                                  v[:, 0:dv], start=False, stop=c == NCH - 1,
                                  signal=c == NCH - 1)
                    pT.free = (m,)
                    if old["last"] is not None:
                        old["last"](self.o, m, old["exp"])

            def drain(self):
                for _ in range(self.to_o):
                    self.step(None)
                    yield

        def weigh_heads(att, o_ap, sums, heads, dv, marks):
            dve.wait(*marks)
            mr = dve.do(VE.reciprocal, sums, sums)
            m = dve.do(VE.tensor_reduce, att.rearrange("p (h d) -> p h d", d=dv),
                       o_ap.rearrange("p (h t d) -> p h d t", t=2, d=dv), X, ALU.add)
            dve.wait(m, mr)
            m2 = dve.do(VE.tensor_tensor, att.rearrange("p (h d) -> p h d", d=dv),
                        att.rearrange("p (h d) -> p h d", d=dv),
                        sums.unsqueeze(2).to_broadcast([N, heads, dv]), ALU.mult)
            return m, m2

        PARTS = ((0, 0), (0, 1), (1, 0))

        def split16(high, low, src, bank, mark, scale=1.0):
            act.wait(mark)
            mh = act.do(SC.activation, high, src, ACT.Copy, scale=scale)
            dve.wait(mh)
            ml = dve.do(VE.scalar_tensor_tensor, low, src, scale, high, ALU.mult, ALU.subtract)
            bank.free = (ml,)
            return mh, ml

        s1_q = [work.tensor(f"s1_q{i}", [P, KC, 2, HPT, 2, N], F16) for i in range(2)]
        s1_q16 = [work.tensor(f"s1_q16_{i}", [P, 2, 2 * N], F16) for i in range(2)]
        s1_kf = [work.tensor(f"s1_kf{i}", [P, S]) for i in range(2)]
        s1_k = [work.tensor(f"s1_k{i}", [P, KC, 2, S], F16) for i in range(2)]
        s1_v = [work.tensor(f"s1_v{i}", [SCH, NCH, H, 2, DH], F16) for i in range(2)]
        s1_p = Ring([work.tensor(f"s1_p{i}", [N, S])[:] for i in range(4)])
        s1_pT = Ring([work.tensor(f"s1_pT{i}", [SCH, 2, NCH * N], F16)[:] for i in range(3)])
        s1_att = [work.tensor(f"s1_att{i}", [N, D]) for i in range(2)]
        s1_attT = [work.tensor(f"s1_attT{i}", [P, KC, 2 * N]) for i in range(2)]
        s1_h = [work.tensor(f"s1_h{i}", [P, 2 * KC, 2 * N]) for i in range(2)]
        s1_sum = [work.tensor(f"s1_sum{i}", [N, H]) for i in range(2)]
        s1_max = [work.tensor(f"s1_max{i}", [N, H]) for i in range(2)]
        s_banks, t_banks, o_banks, misc = banks(0, 2), banks(2, 2), banks(4, 1), banks(5, 3)
        qkv_mark, attn_read, o_done, o_read = {}, {}, {}, {}
        kf_read = [None] * KC
        q16_read = [None] * KC

        def cross0_operands(b):
            i = b % 2
            if b >= 2:
                yield from until(attn_read, b - 2)
                act.wait(attn_read[b - 2])
                dve.wait(attn_read[b - 2])
                pool.wait(attn_read[b - 2])
            c16 = ctx16[b % 3]
            pe.wait(later["wkv1"], ctx_ready[b])
            for c in range(KC):
                bank = misc.take(pe)
                m = project(bank.ap[:, 0:S], [(Wkv1_16[:, w, c * P:(c + 1) * P], c16[:, t, :])
                                              for t, w in CTX_PRODUCTS])
                act.wait(m)
                act.wait(kf_read[c])
                mk = act.do(SC.activation, s1_kf[c][:], bank.ap[:, 0:S], ACT.Identity,
                            scale=1 / WSCALE, bias=ch("bk1", c))
                bank.free = (mk,)
                dve.wait(mk)
                mkh = dve.do(VE.tensor_copy, s1_k[i][:, c, 0, :], s1_kf[c][:])
                pool.wait(mkh)
                mk = kf_read[c] = pool.do(GP.tensor_tensor, s1_k[i][:, c, 1, :], s1_kf[c][:],
                                          s1_k[i][:, c, 0, :], ALU.subtract)
                yield
            for c in range(NCH):
                bank = misc.take(pe)
                m = project(bank.ap[0:SCH, 0:D], [(c16[:, t, c * SCH:(c + 1) * SCH],
                                                   Wkv1_16[:, w, D:]) for t, w in CTX_PRODUCTS])
                mvh, mv = split16(s1_v[i][:, c, :, 0, :], s1_v[i][:, c, :, 1, :],
                                  bank.ap[0:SCH, 0:D].rearrange("p (h d) -> p h d", d=DH), bank, m,
                                  1 / WSCALE)
                yield
            ctx_read[b] = m
            load_ctx(b + 3)
            add_bias(b, b2, w1_ready)
            qkv_mark[b] = (mkh, mk, mvh, mv)

        def cross0_queries(b):
            if b >= 4:
                yield from until(attn_read, b - 3)
            dve.wait(m_headq16)
            qt = s1_q[b // 2 % 2]
            if b >= 4:
                dve.wait(attn_read[b - 3])
            for c in range(KC):
                bank = misc.take(pe)
                pe.wait(x_ch_mark[b], x_ch_mark[b + 1])
                m = project(bank.ap[:, 0:2 * N],
                            [(Wq1[:, k, c * P:(c + 1) * P], x_ch[:, k, b * N:(b + 2) * N])
                             for k in range(KC)])
                act.wait(m, q16_read[c])
                mh = act.do(SC.activation, s1_q16[c][:, 0, :], bank.ap[:, 0:2 * N],
                            ACT.Identity, bias=ch("bq1", c))
                dve.wait(mh)
                mq = dve.do(VE.scalar_tensor_tensor, s1_q16[c][:, 1, :], bank.ap[:, 0:2 * N],
                            ch("bq1", c), s1_q16[c][:, 0, :], ALU.add, ALU.subtract)
                bank.free = (mq,)
                yield
                dve.wait(mq)
                for j in range(2):
                    for h in range(0, HPT, 2):
                        some = [P, 2, 2 * N]
                        mq = dve.do(
                            VE.tensor_tensor,
                            qt[:, c, j, h:h + 2].rearrange("p h b n -> p h (b n)"),
                            s1_q16[c][:, j, :].unsqueeze(1).to_broadcast(some),
                            headq16[:, h:h + 2].unsqueeze(2).to_broadcast(some), ALU.mult)
                        yield
                q16_read[c] = mq
                yield
            qkv_mark["q", b // 2] = mq

        pipe = Heads(DH, 3, 5, s1_p, s1_pT, s_banks, t_banks, o_banks)

        def cross0_heads(b):
            i = b % 2

            def last(o, m, m_exp):
                attn_read[b] = m
                dve.wait(o_read.get(b - 2))
                m, m2 = weigh_heads(s1_att[i][:], o.ap[0:N, :], s1_sum[i][:], H, DH, (m_exp, m))
                o.free = (m,)
                pool.wait(m2, w1_ready)
                o_done[b] = pool.do(GP.tensor_tensor, s1_att[i][:], s1_att[i][:], bv1[:], ALU.add)

            yield from until(qkv_mark, b, ("q", b // 2))
            if b >= 2:
                yield from until(o_read, b - 2)
            for h in range(H):
                pipe.step(dict(
                    q=[s1_q[b // 2 % 2][:, h // HPT, j, h % HPT, b % 2, :] for j in range(2)],
                    k=[s1_k[i][:, h // HPT, j, :] for j in range(2)], at=h * 2 * DH, first=h == 0,
                    v=lambda c, h=h: s1_v[i][:, c, h, :, :].rearrange("p t d -> p (t d)"),
                    qk_marks=(*qkv_mark[b], qkv_mark["q", b // 2]), v_marks=lambda: (),
                    nmax=s1_max[i][:, h:h + 1], sum=s1_sum[i][:, h:h + 1],
                    last=last if h == H - 1 else None))
                yield
            if b == B - 1:
                yield from pipe.drain()

        def cross0_out(b):
            i = b // 2 % 2
            for j in range(2):
                marks = {}
                yield from until(o_done, b - 1 + j)
                yield from rest(REST_POWER)
                yield from to_channels(s1_att[j][:], o_done[b - 1 + j], KC, misc,
                                       s1_attT[i][:, :, j * N:(j + 1) * N], marks, 0)
                o_read[b - 1 + j] = marks[0]
            pe.wait(o_read[b - 1], o_read[b])
            yield from rest(REST)
            for f in range(2 * KC):
                bank = misc.take(pe)
                m = project(bank.ap[:, 0:2 * N],
                            [(W1[:, k, f * P:(f + 1) * P], s1_attT[i][:, k, :]) for k in range(KC)])
                act.wait(m)
                mh = act.do(SC.activation, s1_h[i][:, f, :], bank.ap[:, 0:2 * N],
                            ACT.Relu, bias=ch("b1", f))
                bank.free = (mh,)
                yield
            yield from rest(REST)
            for j in range(2):
                bank = misc.take(pe)
                pe.wait(mh)
                m = project(bank.ap[0:N, 0:D], [(s1_h[i][:, k, j * N:(j + 1) * N], W2[:, k, :])
                                                for k in range(2 * KC)])
                yield
                yield from norm(b - 1 + j, Result(bank.ap[0:N, 0:D], bank), m, res,
                                res_mark[b - 1 + j], misc)

        raw_read, e16_mark, up_read, expert_read = {}, {}, {}, {}
        raws = [raw0]

        def split_expert(e, j):
            src, dst = raws[-1][j], e16[e % 2][j]
            if e == 1:
                act.wait(*(m for k in range(3) for m in raw_read[0, k]))
            act.wait(raw_ready[e, j], (up_read if j < 2 else expert_read).get(e - 2))
            half_ = src.shape[1] // 2
            for ks in (slice(0, half_), slice(half_, 2 * half_)):
                mh = act.do(SC.activation, dst[:, 0, ks], src[:, ks], ACT.Copy, scale=WSCALE)
                dve.wait(mh)
                ml = dve.do(VE.scalar_tensor_tensor, dst[:, 1, ks], src[:, ks], WSCALE,
                            dst[:, 0, ks], ALU.mult, ALU.subtract)
                yield
            raw_read[e, j] = (mh, ml)
            e16_mark[e, j] = ml

        def split_expert0():
            for j in range(3):
                yield from until(attn_read, j + 1)
                yield from split_expert(0, j)

        weave(split_expert0(), follow(cross0_heads, range(B)), follow(cross0_out, range(1, B, 2)),
              follow(cross0_operands, range(B)), follow(cross0_queries, range(0, B, 2)))

        fence()
        work.restart()
        misc = banks(0, 8)
        raw = [work.tensor("raw_" + n, [P, k, w]) for n, k, w in MATS]
        raws.append(raw)

        def load_expert(e, marks):
            for j, (n, _, _) in enumerate(MATS):
                sp.wait(*marks, *(raw_read.get((e - 1, j)) or ()))
                raw_ready[e, j] = sp.dma(SY.dma_start, s_exp[j], raw[j][:], a[n][e])

        load_expert(1, end_marks())
        R = [N, B, E0]
        logit = work.tensor("logit", R)
        prob = work.tensor("prob", R)
        top = work.tensor("top", R)
        top_i = work.tensor("top_i", R, U32)
        small = work.tensor("small", [N, 8, B])
        e_k = work.tensor("e_k", [N, 2, B])
        w_k = keep.tensor("w_k", [N, 2, B])
        pick = [work.tensor(f"pick{k}", R) for k in range(2)]
        dense = work.tensor("dense", R)
        tmp = work.tensor("tmp", R)
        part = work.tensor("part", [N, B, P], BF16)
        pick16 = work.tensor("pick16", [N, 2, B, P], BF16)
        partT = work.tensor("partT", [P, T], BF16)
        pickT = work.tensor("pickT", [P, 2, B, N], BF16)
        junk = [work.tensor(f"junk{i}", [N, HALF]) for i in range(3)]
        cnt = work.tensor("cnt", [N, 2, B, 4])
        rank = work.tensor("rank", [N, 2, B])
        kept = work.tensor("kept", [N, 2, B])
        slot = work.tensor("slot", [N, 2, B])
        slot2 = work.tensor("slot2", [N, 2, B])
        put_i = work.tensor("put_i", [N, 2, B], U32)
        get_i = keep.tensor("get_i", [N, 2, B], U32)

        bank = misc.take(pe)
        lg = bank.ap[0:N, 0:B * E0].rearrange("p (b e) -> p b e", e=E0)
        pe.wait(w2_ready)
        for b in range(B):
            pe.wait(x_ch_mark[b])
            m = project(bank.ap[0:N, b * E0:(b + 1) * E0],
                        [(x_ch[:, k, cols(b)], router[:, k, :]) for k in range(KC)])

        def chain(first, *steps):
            m = first
            for op, args, kw in steps:
                dve.wait(m)
                m = dve.do(op, *args, **kw)
            return m

        def st(op, *args, **kw):
            return (op, args, kw)

        def wide(t):
            return t.unsqueeze(2).to_broadcast(R)

        m_set = dve.do(VE.memset, part[:], 0.0)
        m_set = dve.do(VE.memset, pick16[:], 0.0)
        m_set = dve.do(VE.memset, cnt[:], 0.0)
        mx, den = small[:, 0, :], small[:, 1, :]
        m = chain(m,
                  st(VE.tensor_reduce, mx, lg, X, ALU.max),
                  st(VE.tensor_tensor, logit[:], lg, wide(mx), ALU.subtract))
        bank.free = (m,)
        act.wait(m)
        m = act.do(SC.activation, prob[:], logit[:], ACT.Exp)
        m = chain(m,
                  st(VE.tensor_reduce, den, prob[:], X, ALU.add),
                  st(VE.reciprocal, den, den),
                  st(VE.tensor_tensor, prob[:], prob[:], wide(den), ALU.mult))
        dve.wait(m)
        for b in range(B):
            m = dve.do(VE.max, top[:, b, :], prob[:, b, :])
        dve.wait(m)
        for b in range(B):
            m = dve.do(VE.max_index, top_i[:, b, :], top[:, b, :], prob[:, b, :])
        tsum = small[:, 2, :]
        m = chain(m,
                  st(VE.tensor_tensor, tsum, top[:, :, 0], top[:, :, 1], ALU.add),
                  st(VE.tensor_scalar, tsum, tsum, 1e-6, None, ALU.add),
                  st(VE.reciprocal, tsum, tsum))
        dve.wait(m)
        for k in range(2):
            dve.do(VE.tensor_tensor, w_k[:, k, :], top[:, :, k], tsum, ALU.mult)
            m = dve.do(VE.tensor_copy, e_k[:, k, :], top_i[:, :, k])
        dve.wait(m)
        for k in range(2):
            m = dve.do(VE.tensor_tensor, pick[k][:], iota8[:].unsqueeze(1).to_broadcast(R),
                       wide(e_k[:, k, :]), ALU.is_equal)
        m = chain(m,
                  st(VE.tensor_tensor, dense[:], pick[0][:], wide(w_k[:, 0, :]), ALU.mult),
                  st(VE.tensor_tensor, tmp[:], pick[1][:], wide(w_k[:, 1, :]), ALU.mult),
                  st(VE.tensor_tensor, dense[:], dense[:], tmp[:], ALU.add),
                  st(VE.tensor_tensor, tmp[:], pick[0][:], pick[1][:], ALU.add),
                  st(VE.scalar_tensor_tensor, dense[:], tmp[:], -1.0, dense[:], ALU.add, ALU.add),
                  st(VE.tensor_copy, part[:, :, 0:E0], dense[:]),
                  st(VE.tensor_tensor, tmp[:], dense[:], part[:, :, 0:E0], ALU.subtract),
                  st(VE.tensor_copy, part[:, :, E0:2 * E0], tmp[:]),
                  st(VE.tensor_tensor, part[:, :, 2 * E0:3 * E0], tmp[:], part[:, :, E0:2 * E0],
                     ALU.subtract))
        dve.wait(m)
        for k in range(2):
            for j in range(3):
                m = dve.do(VE.tensor_copy, pick16[:, k, :, j * E0:(j + 1) * E0], pick[k][:])

        def transpose16(src, n, dst, m):
            bank = misc.take(pe)
            i = bank.number
            pe.wait(m, m_ident16)
            for t in range(n):
                m = pe.do(TE.transpose, psum16[:, i, t * N:(t + 1) * N], src(t),
                          ident16[0:N, 0:N], signal=t == n - 1)
            act.wait(m)
            m = act.do(SC.activation, dst, psum16[:, i, 0:n * N], ACT.Copy)
            bank.free = (m,)
            return m

        m_partT = transpose16(lambda t: part[:, t, :], B, partT[:], m)
        for k in range(2):
            m_pickT = transpose16(lambda t: pick16[:, k, t, :], B,
                                  pickT[:, k, :, :].rearrange("p b n -> p (b n)"), m)
        pe.wait(m_partT, m_pickT)
        jmark = [None] * 3
        jn = 0
        s_put = sem("dma_put")
        for k in range(2):
            for b in range(B):
                halves = []
                for hf in range(2):
                    bank = misc.take(pe)
                    m = project(bank.ap[0:N, 0:HALF],
                                [(pickT[:, k, b, :], partT[:, hf * HALF:(hf + 1) * HALF])])
                    halves.append((bank, m))
                w = w_k[:, k, b:b + 1]
                col = 0
                for hf, (bank, m) in enumerate(halves):
                    dve.wait(m)
                    cut = min(max(b - 4 * hf, 0), 4) * N
                    for lo, hi, op in ((0, cut, ALU.is_ge), (cut, HALF, ALU.is_gt)):
                        if hi > lo:
                            dve.wait(jmark[jn % 3])
                            jmark[jn % 3] = dve.do(
                                VE.tensor_scalar, junk[jn % 3][:, lo:hi], bank.ap[0:N, lo:hi], w,
                                None, op, ALU.add, accum_out=cnt[:, k, b, col:col + 1])
                            jn += 1
                            col += 1
                    if b // 4 == hf:
                        own = slice(b % 4 * N, (b % 4 + 1) * N)
                        dve.wait(jmark[jn % 3])
                        jmark[jn % 3] = dve.do(
                            VE.scalar_tensor_tensor, junk[jn % 3][:, own], bank.ap[0:N, own], w,
                            before[:], ALU.is_equal, ALU.mult, accum_out=cnt[:, k, b, 3:4])
                        jn += 1
                    bank.free = (jmark[(jn - 1) % 3],)
            tab = slot_tab[:, k * B:(k + 1) * B]
            m = chain((dve.sem, dve.sem.value),
                      st(VE.tensor_reduce, rank[:, k], cnt[:, k], X, ALU.add),
                      st(VE.tensor_scalar, kept[:, k], rank[:, k], float(CAP), None, ALU.is_lt),
                      st(VE.tensor_scalar, slot[:, k], rank[:, k], float(CAP - 1), None, ALU.min),
                      st(VE.scalar_tensor_tensor, slot[:, k], e_k[:, k], float(CAP), slot[:, k],
                         ALU.mult, ALU.add),
                      st(VE.tensor_tensor, slot2[:, k], slot[:, k], tab, ALU.subtract),
                      st(VE.tensor_tensor, slot2[:, k], slot2[:, k], kept[:, k], ALU.mult),
                      st(VE.tensor_tensor, slot2[:, k], slot2[:, k], tab, ALU.add),
                      st(VE.tensor_copy, put_i[:, k], slot2[:, k]))
            pool.wait(m, disp_zeroed)
            for b in range(B):
                put = pool.dma(GP.indirect_dma_start, s_put, disp[:, :],
                               bass.IndirectOffsetOnAxis(put_i[:, k, b:b + 1], axis=0),
                               x_tok[:, b, :], None)
        m = dve.do(VE.tensor_copy, get_i[:], slot[:])
        m = dve.do(VE.tensor_tensor, w_k[:], w_k[:], kept[:], ALU.mult)

        e_in = [work.tensor(f"e_in{i}", [HC, 2, D]) for i in range(2)]
        e_inT = [work.tensor(f"e_inT{i}", [P, 2, KC, CAP], F16) for i in range(2)]
        silu = Ring([work.tensor(f"silu{i}", [P, 2, CAP])[:] for i in range(3)])
        hid0 = [work.tensor(f"hid0_{i}", [P, 2, F0 // P, CAP], F16) for i in range(2)]
        e_out = [work.tensor(f"e_out{i}", [HC, 2, D]) for i in range(2)]
        s_in = [sem(f"dma_e_in{i}") for i in range(2)]
        s_out = [sem(f"dma_e_out{i}") for i in range(2)]
        in_mark, inT_mark, hid_mark, inT_read, hid_read, eo_mark = {}, {}, {}, {}, {}, {}
        in_read = {}
        FT = F0 // P

        def expert_in(e):
            i = e % 2
            act.wait(put)
            if e >= 2:
                yield from until(in_read, e - 2)
                act.wait(in_read[e - 2])
            in_mark[e] = act.dma(SC.dma_start, s_in[i], e_in[i][:],
                                disp[e * CAP:(e + 1) * CAP, :].rearrange("(t p) d -> p t d", p=HC))
            yield from rest(3 * REST)
            if e >= 2:
                yield from until(up_read, e - 2)
            bank = misc.take(pe)
            pe.wait(in_mark[e])
            for c in range(KC):
                for t in range(2):
                    m = pe.do(TE.transpose, bank.ap[:, c * CAP + t * HC:c * CAP + (t + 1) * HC],
                              e_in[i][:, t, c * P:(c + 1) * P], ident[0:HC, 0:HC],
                              signal=c == 1 and t == 1)
            in_read[e] = m
            yield
            if e >= 2:
                act.wait(inT_read[e - 2])
            _, inT_mark[e] = split16(e_inT[i][:, 0], e_inT[i][:, 1],
                                     bank.ap[:, 0:KC * CAP].rearrange("p (c s) -> p c s", c=KC),
                                     bank, m)

        def expert_up(e):
            i = e % 2
            yield from until(inT_mark, e)
            yield from until(e16_mark, (e, 0), (e, 1))
            pe.wait(inT_mark[e], e16_mark[e, 0], e16_mark[e, 1])
            if e >= 2:
                yield from until(hid_read, e - 2)
                act.wait(hid_read[e - 2])
                dve.wait(hid_read[e - 2])
            def parts(f, s, m):
                act.wait(m)
                mh = act.do(SC.activation, hid0[i][:, 0, f:f + 2, :], s.ap, ACT.Copy)
                dve.wait(mh)
                s.free = (dve.do(VE.tensor_tensor, hid0[i][:, 1, f:f + 2, :], s.ap,
                                 hid0[i][:, 0, f:f + 2, :], ALU.subtract),)
                hid_mark[e] = s.free[0]

            pair = None
            for f in range(FT):
                bank = misc.take(pe)
                for j in range(2):
                    m = project(bank.ap[:, j * CAP:(j + 1) * CAP],
                                [(e16[i][j][:, a_, k, f * P:(f + 1) * P], e_inT[i][:, b_, k, :])
                                 for k in range(KC) for a_, b_ in PARTS])
                if f % 2 == 0:
                    s = silu.take(act, dve)
                act.wait(m)
                ms = act.do(SC.activation, s.ap[:, f % 2, :], bank.ap[:, 0:CAP], ACT.Silu,
                            scale=1 / WSCALE)
                dve.wait(ms, m)
                m2 = dve.do(VE.scalar_tensor_tensor, s.ap[:, f % 2, :], bank.ap[:, CAP:2 * CAP],
                            1 / WSCALE, s.ap[:, f % 2, :], ALU.mult, ALU.mult)
                bank.free = (m2,)
                if f % 2 == 0 and pair is not None:
                    parts(*pair)
                if f % 2:
                    pair = (f - 1, s, m2)
                yield
            parts(*pair)
            inT_read[e] = up_read[e] = m

        def expert_down(e):
            i = e % 2
            yield from until(up_read, e)
            yield from until(e16_mark, (e, 2))
            yield from rest(2 * REST)
            bank = misc.take(pe)
            pe.wait(hid_mark[e], e16_mark[e, 2])
            for t in range(2):
                m = project(bank.ap[0:HC, t * D:(t + 1) * D],
                            [(hid0[i][:, a_, f, t * HC:(t + 1) * HC], e16[i][2][:, b_, f, :])
                             for f in range(FT) for a_, b_ in PARTS])
                yield
            hid_read[e] = m
            expert_read[e] = m
            dve.wait(m)
            if e >= 2:
                dve.wait(eo_mark[e - 2])
            m = dve.do(VE.tensor_scalar, e_out[i][:].rearrange("p t d -> p (t d)"),
                       bank.ap[0:HC, :], 1 / WSCALE, None, ALU.mult)
            bank.free = (m,)
            sp.wait(m)
            eo_mark[e] = sp.dma(SY.dma_start, s_out[i],
                                eout[e * CAP:(e + 1) * CAP, :].rearrange("(t p) d -> p t d", p=HC),
                                e_out[i][:])

        def split_next(e):
            for j in range(3):
                if e >= 2:
                    yield from until(up_read if j < 2 else expert_read, e - 2)
                yield from split_expert(e, j)
                if e + 1 < E0:
                    n = MATS[j][0]
                    sp.wait(*raw_read[e, j])
                    raw_ready[e + 1, j] = sp.dma(SY.dma_start, s_exp[j], raw[j][:], a[n][e + 1])

        weave(*(follow(work_, range(E0)) for work_ in (expert_down, expert_up, expert_in)),
              follow(split_next, range(1, E0)))

        fence()
        work.restart()
        ring.restart()
        proj = sbk = misc = banks(0, 4)
        ybk = banks(4, 4)
        s3_q = [work.tensor(f"s3_q{i}", [P, KC, HPT, 2, N]) for i in range(2)]
        s3_k = [work.tensor(f"s3_k{i}", [P, KC, 2, N]) for i in range(2)]
        s3_v = [work.tensor(f"s3_v{i}", [N, 2, HW], F16) for i in range(2)]
        s3_a16 = Ring([work.tensor(f"s3_a16_{i}", [N, 2, 4, N], F16)[:] for i in range(3)])
        s3_a = Ring([work.tensor(f"s3_a{i}", [N, 4, N])[:] for i in range(3)])
        s3_y = [work.tensor(f"s3_y{i}", [N, HW]) for i in range(2)]
        s3_y2 = [work.tensor(f"s3_y2_{i}", [N, HW // 2]) for i in range(2)]
        s3_yT = [work.tensor(f"s3_yT{i}", [P, HW // P, N]) for i in range(2)]
        s3_ms = [work.tensor(f"s3_ms{i}", [N, H]) for i in range(2)]
        s3_rms = [work.tensor(f"s3_rms{i}", [N, H]) for i in range(2)]
        s_w4 = sem("dma_w4")
        sp.wait(*end_marks())
        Wq4, _ = load(ring, "Wq4", [P, KC, HW], s_w4)
        spent = Region(nc, wts.base, 30 * KB)
        Wk4, _ = load(spent, "Wk4", [P, 2, HW], s_w4)
        Wv4, _ = load(spent, "Wv4", [P, 2, HW], s_w4)
        Wk4_16 = ring.tensor("Wk4_16", [P, 4, HW], F16)
        Wv4_16 = ring.tensor("Wv4_16", [P, 4, HW], F16)
        Wo4, _ = load(ring, "Wo4", [P, HW // P, D], s_w4)
        bout4, _ = load(ring, "bout4", [N, D], s_w4)
        w4_ready = (s_w4, s_w4.value)

        NG = 7
        got = [spent.tensor(f"got{i}", [N, 2, D]) for i in range(NG)]
        s_get = [sem(f"dma_get{i}") for i in range(NG)]
        pool.wait(eo_mark[E0 - 1], eo_mark[E0 - 2])
        get_mark, got_read, combined = {}, {}, {}

        def get(b):
            for k in range(2):
                get_mark[b] = pool.dma(GP.indirect_dma_start, s_get[b % NG], got[b % NG][:, k, :],
                                       None, eout[:, :],
                                       bass.IndirectOffsetOnAxis(get_i[:, k, b:b + 1], axis=0))

        for b in range(2):
            get(b)

        def combine(b):
            i = b % NG
            yield from until(get_mark, b)
            m = get_mark[b]
            yield from rest(2 * REST)
            dve.wait(m, put)
            m = dve.do(VE.scalar_tensor_tensor, res[:, b, :], got[i][:, 0, :], w_k[:, 0, b:b + 1],
                       x_tok[:, b, :], ALU.mult, ALU.add)
            dve.wait(m)
            m = dve.do(VE.scalar_tensor_tensor, res[:, b, :], got[i][:, 1, :], w_k[:, 1, b:b + 1],
                       res[:, b, :], ALU.mult, ALU.add)
            got_read[b] = m
            if b + 2 < B:
                if b + 2 >= NG:
                    pool.wait(got_read[b + 2 - NG])
                get(b + 2)
            yield from norm(b, None, None, res, m, misc)
            combined[b] = True

        s4_att = ring.tensor("s4_att", [N, HW])
        s4_attT = ring.tensor("s4_attT", [P, HW // P, N])

        pool.wait(w3_ready)
        m_wo3 = pool.do(GP.tensor_scalar, Wo3[:], Wo3[:], ch("g3"), None, ALU.mult)
        qkv3, y3, read3, y2_read = {}, {}, {}, [None, None]

        def quad_operands(b):
            i = b % 2
            yield from until(combined, b, b + 1 - b % 2)
            if b >= 2:
                yield from until(read3, b - 2)
            pe.wait(w3_ready, x_ch_mark[b])
            if b >= 2:
                act.wait(read3[b - 2])
                dve.wait(read3[b - 2])
            if b % 2 == 0:
                j = b // 2 % 2
                pe.wait(x_ch_mark[b + 1])
                for c in range(KC):
                    bank = proj.take(pe)
                    for w, at in ((Wq3, 0), (Wk3, 2 * N)):
                        m = project(bank.ap[:, at:at + 2 * N],
                                    [(w[:, k, c * P:(c + 1) * P], x_ch[:, k, b * N:(b + 2) * N])
                                     for k in range(KC)])
                    if b >= 4:
                        dve.wait(read3[b - 3])
                        act.wait(read3[b - 3])
                    dve.wait(m)
                    mq = dve.do(VE.tensor_tensor, s3_q[j][:, c].rearrange("p h b n -> p h (b n)"),
                                bank.ap[:, 0:2 * N].unsqueeze(1).to_broadcast([P, HPT, 2 * N]),
                                headq[:].unsqueeze(2).to_broadcast([P, HPT, 2 * N]), ALU.mult)
                    act.wait(mq)
                    mk = act.do(SC.activation, s3_k[j][:, c].rearrange("p b n -> p (b n)"),
                                bank.ap[:, 2 * N:4 * N], ACT.Copy)
                    bank.free = (mq, mk)
                    yield
                qkv3["q", b // 2] = (mq, mk)
            for c in range(2):
                bank = proj.take(pe)
                m = project(bank.ap[0:N, :],
                            [(x_ch[:, k, cols(b)], Wv3[:, k, c * 512:(c + 1) * 512])
                             for k in range(KC)])
                mv = split16(s3_v[i][:, 0, c * 512:(c + 1) * 512],
                             s3_v[i][:, 1, c * 512:(c + 1) * 512], bank.ap[0:N, :], bank, m)
                yield
            qkv3[b] = mv

        def quad_heads(b):
            i = b % 2
            yield from until(qkv3, b)
            if b >= 2:
                yield from until(y3, (b - 2, "free"))
            pe.wait(*qkv3[b], *qkv3["q", b // 2])
            j2 = b // 2 % 2
            held = []
            ybank = None
            for g in list(range(4)) + [None] * 2:
                if g is not None:
                    bank = sbk.take(pe)
                    c, h0 = g // 2, g % 2 * 4
                    m = project(bank.ap[0:N, 0:4 * N],
                                [(s3_k[j2][:, c, b % 2, :], s3_q[j2][:, c, h0:h0 + 4, b % 2, :])])
                    q = s3_a.take(act)
                    act.wait(m)
                    m = act.do(SC.activation, q.ap,
                               bank.ap[0:N, 0:4 * N].rearrange("p (h n) -> p h n", n=N),
                               ACT.Square, bias=1.0)
                    bank.free = (m,)
                    dve.wait(m)
                    m = dve.do(VE.scalar_tensor_tensor, q.ap, q.ap, 1.0,
                               half_causal[:].unsqueeze(1).to_broadcast([N, 4, N]), ALU.add,
                               ALU.mult)
                    q16 = s3_a16.take(act, dve)
                    act.wait(m)
                    m = act.do(SC.activation, q16.ap[:, 0], q.ap, ACT.Copy)
                    dve.wait(m)
                    m = dve.do(VE.tensor_tensor, q16.ap[:, 1], q.ap, q16.ap[:, 0], ALU.subtract)
                    q.free = (m,)
                    held.append((g, q16, m))
                    yield
                if len(held) > 2 or (g is None and held):
                    pg, q, m = held.pop(0)
                    if pg % 2 == 0:
                        ybank = ybk.take(pe)
                    pe.wait(m)
                    for j in range(4):
                        h = pg * 4 + j
                        m = project(ybank.ap[0:N, h % 8 * DHW:(h % 8 + 1) * DHW],
                                    [(q.ap[:, k, j, :], s3_v[i][:, l, h * DHW:(h + 1) * DHW])
                                     for k, l in PARTS])
                    q.free = (m,)
                    if pg % 2:
                        y3[b, pg // 2] = (ybank, m)
                yield
            read3[b] = m

        def quad_out(b):
            i = b % 2
            yield from until(y3, (b, 0), (b, 1))
            for j in range(2):
                bank, m = y3[b, j]
                act.wait(m, y2_read[i])
                m = act.do(SC.activation, s3_y2[i][:], bank.ap[0:N, :], ACT.Square)
                dve.wait(m)
                m = y2_read[i] = dve.do(VE.tensor_reduce, s3_ms[i][:, j * 8:(j + 1) * 8],
                                        s3_y2[i][:].rearrange("p (h d) -> p h d", d=DHW), X,
                                        ALU.add)
            dve.wait(m)
            m = dve.do(VE.tensor_scalar, s3_ms[i][:], s3_ms[i][:], 1.0 / DHW, RMS1_EPS, ALU.mult,
                       ALU.add)
            m = power(s3_rms[i][:], s3_ms[i][:], m)
            yield from rest(REST_POWER + H * POWER_NS)
            dve.wait(m)
            dve.wait(y3.get((b - 2, "yread")))
            for j in range(2):
                bank, _ = y3[b, j]
                m = dve.do(VE.tensor_tensor,
                           s3_y[i][:, j * 512:(j + 1) * 512].rearrange("p (h d) -> p h d", d=DHW),
                           bank.ap[0:N, :].rearrange("p (h d) -> p h d", d=DHW),
                           s3_rms[i][:, j * 8:(j + 1) * 8].unsqueeze(2).to_broadcast([N, 8, DHW]),
                           ALU.mult)
                bank.free = (m,)
            y3[b, "free"] = True
            yield from rest(REST)
            marks = {}
            yield from to_channels(s3_y[i][:], m, HW // P, misc, s3_yT[i][:], marks, 0)
            y3[b, "yread"] = (pe.sem, pe.sem.value)
            yield from rest(REST)
            bank = misc.take(pe)
            pe.wait(marks[0], m_wo3)
            m = project(bank.ap[0:N, 0:D], [(s3_yT[i][:, k, :], Wo3[:, k, :])
                                            for k in range(HW // P)])
            yield
            yield from norm(b, Result(bank.ap[0:N, 0:D], bank), m, x_tok, x_tok_mark[b], misc)

        def split_w4():
            for name, w16, raw in (("wk4", Wk4_16, Wk4), ("wv4", Wv4_16, Wv4)):
                yield from until(read3, len(later))
                later[name] = split_ctx_weights(w16, raw, w4_ready)

        weave(*(follow(combine, range(j, B, 4)) for j in range(4)),
              follow(quad_out, range(0, B, 2)), follow(quad_out, range(1, B, 2)),
              follow(quad_operands, range(B)),
              follow(quad_heads, range(B)), split_w4())

        fence()
        work.restart()
        wts.restart()
        s_w5, s_w5b = sem("dma_w5"), sem("dma_w5b")
        sp.wait(*end_marks())
        ffn_w = {}
        for name, shape in (("wq5", [P, KC, D]), ("wk5", [P, KC, D]), ("wv5", [P, KC, D]),
                            ("wo5", [P, KC, KEPT]), ("gate5", [P, KC, E1])):
            ffn_w[name], _ = load(ring if name != "gate5" else wts, name, shape, s_w5)
        w5_ready = (s_w5, s_w5.value)
        HT = HID // P
        for name, shape in (("e0_up", [P, KC, HID]), ("e1_w1", [P, KC, HID]),
                            ("e1_w2", [P, KC, HID]), ("e2_l1", [P, KC, HID]),
                            ("e2_l2", [P, HT, HID]), ("e2_l3", [P, HT, HID]),
                            ("e3_down", [P, KC, D]), ("e3_up", [P, KC, HID]),
                            ("e0_down", [P, HT, KEPT]), ("e1_down", [P, HT, KEPT]),
                            ("e2_l4", [P, HT, KEPT]), ("e3_out", [P, HT, KEPT])):
            ffn_w[name], _ = load(wts, name, shape, s_w5b)
        w5b_ready = (s_w5b, s_w5b.value)

        s_banks, t_banks, o_banks, misc = banks(0, 2), banks(2, 2), banks(4, 1), banks(5, 3)
        s4_q = [work.tensor(f"s4_q{i}", [P, H, 2, 2, N], F16) for i in range(2)]
        s4_k = [work.tensor(f"s4_k{i}", [P, HW // P, 2, S], F16) for i in range(2)]
        s4_v = [work.tensor(f"s4_v{j}", [SCH, NCH, H // 2, 2, DHW], F16) for j in range(2)]
        s4_p = Ring([work.tensor(f"s4_p{i}", [N, S])[:] for i in range(3)])
        s4_pT = Ring([work.tensor(f"s4_pT{i}", [SCH, 2, NCH * N], F16)[:] for i in range(3)])
        s4_sum = [work.tensor(f"s4_sum{i}", [N, H]) for i in range(2)]
        s4_max = [work.tensor(f"s4_max{i}", [N, H]) for i in range(2)]
        m_q0 = dve.do(VE.memset, s4_q[0][:], 0.0)
        m_q0 = dve.do(VE.memset, s4_q[1][:], 0.0)
        qk4, v4, read4, att4, att_read = {}, {}, {}, {}, {}

        def cross1_operands(b):
            i = b % 2
            if b >= 2:
                yield from until(read4, b - 2)
            if b >= 2:
                act.wait(read4[b - 2])
                dve.wait(read4[b - 2])
            c16 = ctx16[(B + b) % 3]
            pe.wait(later["wk4"], w4_ready, ctx_ready[B + b])
            for t in range(HW // P):
                bank = misc.take(pe)
                m = project(bank.ap[:, 0:S], [(Wk4_16[:, w, t * P:(t + 1) * P], c16[:, c, :])
                                              for c, w in CTX_PRODUCTS])
                mk = split16(s4_k[i][:, t, 0, :], s4_k[i][:, t, 1, :], bank.ap[:, 0:S], bank, m,
                             1 / WSCALE)
                yield
            qk4[b] = mk
            add_bias(b, bout4, w4_ready)

        def cross1_queries(b):
            if b >= 4:
                yield from until(read4, b - 3)
            act.wait(m_q0)
            dve.wait(m_q0)
            pe.wait(x_ch_mark[b], x_ch_mark[b + 1])
            qt = s4_q[b // 2 % 2]
            if b >= 4:
                act.wait(read4[b - 3])
                dve.wait(read4[b - 3])
            for t in range(HW // P):
                bank = misc.take(pe)
                m = project(bank.ap[:, 0:2 * N],
                            [(Wq4[:, k, t * P:(t + 1) * P], x_ch[:, k, b * N:(b + 2) * N])
                             for k in range(KC)])
                act.wait(m)
                for j, rows in enumerate((slice(0, 64), slice(64, 128))):
                    ma = act.do(SC.activation,
                                qt[rows, 2 * t + j, 0].rearrange("p b n -> p (b n)"),
                                bank.ap[rows, 0:2 * N], ACT.Copy, scale=DHW ** -0.5)
                dve.wait(ma)
                for j, rows in enumerate((slice(0, 64), slice(64, 128))):
                    md = dve.do(VE.scalar_tensor_tensor,
                                qt[rows, 2 * t + j, 1].rearrange("p b n -> p (b n)"),
                                bank.ap[rows, 0:2 * N], DHW ** -0.5,
                                qt[rows, 2 * t + j, 0].rearrange("p b n -> p (b n)"),
                                ALU.mult, ALU.subtract)
                bank.free = (ma, md)
                if t % 2:
                    yield
            qk4["q", b // 2] = (ma, md)

        def cross1_values(b, j):
            c16 = ctx16[(B + b) % 3]
            if b:
                yield from until(read4, (b - 1, j))
                act.wait(read4[b - 1, j])
                dve.wait(read4[b - 1, j])
            pe.wait(later["wv4"], ctx_ready[B + b])
            for c in range(NCH):
                bank = misc.take(pe)
                m = project(bank.ap[0:SCH, :],
                            [(c16[:, t, c * SCH:(c + 1) * SCH],
                              Wv4_16[:, w, j * 512:(j + 1) * 512]) for t, w in CTX_PRODUCTS])
                marks = split16(s4_v[j][:, c, :, 0, :], s4_v[j][:, c, :, 1, :],
                                   bank.ap[0:SCH, :].rearrange("p (h d) -> p h d", d=DHW), bank,
                                   m, 1 / WSCALE)
                yield
            v4[b, j] = marks
            if j:
                yield from until(qk4, b)
                ctx_read[B + b] = (pe.sem, pe.sem.value)
                if B + b + 3 < 2 * B:
                    load_ctx(B + b + 3)

        pipe = Heads(DHW, 2, 4, s4_p, s4_pT, s_banks, t_banks, o_banks)
        HB = BANK // (2 * DHW)

        def cross1_heads(b):
            i = b % 2

            def last(h0):
                def finish(o, m, m_exp):
                    if h0 + HB == H:
                        read4[b] = m
                    if h0 % (H // 2):
                        read4[b, h0 // (H // 2)] = m
                    dve.wait(att_read.get(b - 1))
                    m, m2 = weigh_heads(s4_att[:, h0 * DHW:(h0 + HB) * DHW], o.ap[0:N, :],
                                        s4_sum[i][:, h0:h0 + HB], HB, DHW, (m_exp, m))
                    o.free = (m,)
                    if h0 + HB == H:
                        att4[b] = m2
                return finish

            yield from until(qk4, b, ("q", b // 2))
            for h in range(H):
                if h % (H // 2) == 0:
                    yield from until(v4, (b, h // (H // 2)))
                if h == HB and b:
                    yield from until(att_read, b - 1)
                pipe.step(dict(
                    q=[s4_q[b // 2 % 2][:, h, j, b % 2, :] for j in range(2)],
                    k=[s4_k[i][:, h // 2, j, :] for j in range(2)],
                    at=h % HB * 2 * DHW, first=h % HB == 0,
                    v=lambda c, h=h: s4_v[h // 8][:, c, h % 8, :, :].rearrange("p t d -> p (t d)"),
                    qk_marks=(*qk4[b], *qk4["q", b // 2]),
                    v_marks=lambda h=h: v4[b, h // 8],
                    nmax=s4_max[i][:, h:h + 1], sum=s4_sum[i][:, h:h + 1],
                    last=last(h - h % HB) if h % HB == HB - 1 else None))
                yield
            if b == B - 1:
                yield from pipe.drain()

        def cross1_out(b):
            marks = {}
            yield from until(att4, b)
            yield from rest(REST)
            yield from to_channels(s4_att[:], att4[b], HW // P, misc, s4_attT[:], marks, 0,
                                   wait=(att_read.get(("T", b - 1)),))
            att_read[b] = (pe.sem, pe.sem.value)
            yield from rest(REST)
            bank = misc.take(pe)
            pe.wait(marks[0])
            m = project(bank.ap[0:N, 0:D], [(s4_attT[:, k, :], Wo4[:, k, :])
                                            for k in range(HW // P)])
            att_read["T", b] = m
            yield
            yield from norm(b, Result(bank.ap[0:N, 0:D], bank), m, res, res_mark[b], misc)

        def values_in_turn():
            for b in range(B):
                for j in range(2):
                    yield from cross1_values(b, j)

        weave(follow(cross1_heads, range(B)), values_in_turn(), follow(cross1_out, range(B)),
              follow(cross1_operands, range(B)), follow(cross1_queries, range(0, B, 2)))

        fence()
        work.restart()
        ring.restart()
        proj = sbk = misc = banks(0, 6)
        obk = banks(6, 2)
        xf = work.tensor("xf", [P, KC, T])
        xf16 = ring.tensor("xf16", [P, 2, KC, T], F16)
        h5 = [work.tensor(f"h5_{i}", [N, D]) for i in range(4)]
        hT = [work.tensor(f"hT{i}", [P, KC, N]) for i in range(4)]
        sq5 = [work.tensor(f"sq5_{i}", [N, 2 * D]) for i in range(4)]
        ms5 = [work.tensor(f"ms5_{i}", [N, 2 * H]) for i in range(4)]
        rs5 = [work.tensor(f"rs5_{i}", [N, 2 * H]) for i in range(4)]
        qk5 = [work.tensor(f"qk5_{i}", [N, 2 * D]) for i in range(4)]
        q5 = [work.tensor(f"q5_{i}", [P, KC, N]) for i in range(4)]
        k5 = [ring.tensor(f"k5_{i}", [P, KC, HPT, N]) for i in range(4)]
        v5 = [work.tensor(f"v5_{i}", [N, 2, H, DH + 1], F16) for i in range(4)]
        sc5 = Ring([work.tensor(f"sc5_{i}", [N, 4, N])[:] for i in range(4)])
        pT5 = Ring([work.tensor(f"pT5_{i}", [N, 2, 4 * N], F16)[:] for i in range(4)])
        mx5 = [work.tensor(f"mx5_{i}", [N, H]) for i in range(2)]
        rd5 = [work.tensor(f"rd5_{i}", [N, H]) for i in range(2)]
        at5 = [work.tensor(f"at5_{i}", [N, D]) for i in range(4)]
        at5T = [work.tensor(f"at5T{i}", [P, KC, N]) for i in range(2)]
        x_in5 = work.tensor("x_in5", [N, B, D])
        for i in range(4):
            dve.do(VE.memset, v5[i][:, 0], 1.0)
            m_v5 = dve.do(VE.memset, v5[i][:, 1], 0.0)
        mask16 = work.tensor("mask16", [N, 4, N], BF16)
        for j in range(4):
            m_mask = pool.do(GP.tensor_copy, mask16[:, j, :], causal_add[:])
        xf16_mark = {}
        qkv5, heads5, out5 = {}, {}, {}
        x_in5_mark = {}

        def rms_rows(b, src, src_mark, i, out_tile):
            act.wait(src_mark)
            m = act.do(SC.activation, sq5[i][:, 0:D], src, ACT.Square,
                       accum_out=ms5[i][:, 0:1])
            dve.wait(m)
            m = dve.do(VE.tensor_scalar, ms5[i][:, 0:1], ms5[i][:, 0:1], 1.0 / D, RMS_EPS,
                       ALU.mult, ALU.add)
            m = power(rs5[i][:, 0:1], ms5[i][:, 0:1], m)
            yield from rest(REST_POWER)
            dve.wait(m)
            return dve.do(VE.tensor_scalar, out_tile, src, rs5[i][:, 0:1], None, ALU.mult)

        def ffn_operands(b):
            i = b % 4
            if b >= 4:
                yield from until(heads5, b - 4)
                for l in (act, dve, pe):
                    l.wait(*heads5[b - 4])
            pool.wait(x_tok_mark[b])
            x_in5_mark[b] = pool.do(GP.tensor_copy, x_in5[:, b, :], x_tok[:, b, :])
            m = yield from rms_rows(b, x_tok[:, b, :], x_tok_mark[b], i, h5[i][:])
            yield from rest(REST)
            bank = misc.take(pe)
            pe.wait(m)
            for c in range(KC):
                m = pe.do(TE.transpose, bank.ap[:, c * N:(c + 1) * N],
                          h5[i][:, c * P:(c + 1) * P], ident[0:N, 0:N])
            yield from rest(REST / 2)
            act.wait(m)
            for c in range(KC):
                m = act.do(SC.activation, hT[i][:, c, :], bank.ap[:, c * N:(c + 1) * N], ACT.Copy,
                           scale=ch("n1", c))
            bank.free = (m,)
            yield from rest(REST)
            bank = proj.take(pe)
            pe.wait(m, w5_ready)
            for j, w in enumerate(("wq5", "wk5")):
                m = project(bank.ap[0:N, j * D:(j + 1) * D],
                            [(hT[i][:, k, :], ffn_w[w][:, k, :]) for k in range(KC)])
            vb = proj.take(pe)
            mv = project(vb.ap[0:N, 0:D], [(hT[i][:, k, :], ffn_w["wv5"][:, k, :])
                                           for k in range(KC)])
            act.wait(m)
            ms = act.do(SC.activation, sq5[i][:], bank.ap[0:N, :], ACT.Square)
            dve.wait(ms)
            m = dve.do(VE.tensor_reduce, ms5[i][:], sq5[i][:].rearrange("p (h d) -> p h d", d=DH),
                       X, ALU.add)
            dve.wait(m)
            m = dve.do(VE.tensor_scalar, ms5[i][:], ms5[i][:], 1.0 / DH, RMS_EPS, ALU.mult,
                       ALU.add)
            m = power(rs5[i][:], ms5[i][:], m)
            act.wait(mv, m_v5)
            dve.wait(m_v5)
            mvh, mv = split16(v5[i][:, 0, :, 0:DH], v5[i][:, 1, :, 0:DH],
                              vb.ap[0:N, 0:D].rearrange("p (h d) -> p h d", d=DH), vb, mv)
            yield from rest(REST_POWER + 2 * H * POWER_NS)
            dve.wait(m)
            m = dve.do(VE.tensor_tensor, qk5[i][:].rearrange("p (h d) -> p h d", d=DH),
                       bank.ap[0:N, :].rearrange("p (h d) -> p h d", d=DH),
                       rs5[i][:].unsqueeze(2).to_broadcast([N, 2 * H, DH]), ALU.mult)
            bank.free = (m,)
            yield from rest(REST)
            bank = misc.take(pe)
            pe.wait(m)
            for c in range(2 * KC):
                m = pe.do(TE.transpose, bank.ap[:, c * N:(c + 1) * N],
                          qk5[i][:, c * P:(c + 1) * P], ident[0:N, 0:N])
            yield from rest(REST / 2)
            act.wait(m)
            mq = act.do(SC.activation, q5[i][:],
                        bank.ap[:, 0:KC * N].rearrange("p (c n) -> p c n", n=N), ACT.Copy,
                        scale=ch("qn"))
            dve.wait(mq)
            for c in range(KC):
                mk = dve.do(VE.scalar_tensor_tensor, k5[i][:, c, :, :],
                            bank.ap[:, (KC + c) * N:(KC + c + 1) * N].unsqueeze(1)
                            .to_broadcast([P, HPT, N]), ch("kn"),
                            headq[:].unsqueeze(2).to_broadcast([P, HPT, N]), ALU.mult, ALU.mult)
            bank.free = (mq, mk)
            qkv5[b] = (mq, mk, mvh, mv)

        def ffn_heads(b):
            i, j4 = b % 2, b % 4
            yield from until(qkv5, b)
            if b >= 4:
                yield from until(out5, b - 4)
            pe.wait(m_mask, *qkv5[b])
            o = obk.take(pe)
            held, ready5 = [], []
            for g in range(6):
                if g < 4:
                    c, h0 = g // 2, g % 2 * 4
                    bank = sbk.take(pe)
                    m = project(bank.ap[0:N, 0:4 * N],
                                [(q5[j4][:, c, :],
                                  k5[j4][:, c, h0:h0 + 4, :].rearrange("p h n -> p (h n)")),
                                 (ident16[0:N, 0:N], mask16[:].rearrange("p h n -> p (h n)"))])
                    sc = bank.ap[0:N, 0:4 * N].rearrange("p (h n) -> p h n", n=N)
                    dve.wait(m)
                    m = dve.do(VE.tensor_reduce, mx5[i][:, 4 * g:4 * g + 4], sc, X, ALU.max,
                               negate=True)
                    s = sc5.take(act)
                    act.wait(m)
                    for j in range(4):
                        m = act.do(SC.activation, s.ap[:, j, :], sc[:, j, :], ACT.Exp,
                                   bias=mx5[i][:, 4 * g + j:4 * g + j + 1])
                    bank.free = (m,)
                    held.append((g, s, m))
                    yield
                if len(held) > 1 or (g >= 4 and held):
                    pg, s, m = held.pop(0)
                    bank = misc.take(pe)
                    pe.wait(m)
                    for j in range(4):
                        m = pe.do(TE.transpose, bank.ap[0:N, j * N:(j + 1) * N], s.ap[:, j, :],
                                  ident[0:N, 0:N])
                    s.free = (m,)
                    pT = pT5.take(act, dve)
                    _, m = split16(pT.ap[:, 0, :], pT.ap[:, 1, :], bank.ap[0:N, 0:4 * N], bank, m)
                    ready5.append((pg, pT, m))
                    yield
                if len(ready5) > 1 or (g == 5 and ready5):
                    pg, pT, m = ready5.pop(0)
                    pe.wait(m)
                    for j in range(4):
                        h = 4 * pg + j
                        m = project(o.ap[0:N, h * (DH + 1):(h + 1) * (DH + 1)],
                                    [(pT.ap[:, k, j * N:(j + 1) * N], v5[j4][:, l, h, :])
                                     for k, l in PARTS])
                    pT.free = (m,)
                yield
            assert not held and not ready5
            nd = o.ap[0:N, 0:H * (DH + 1)].rearrange("p (h d) -> p h d", d=DH + 1)
            dve.wait(m)
            m = dve.do(VE.reciprocal, rd5[i][:], nd[:, :, DH])
            dve.wait(m)
            m = dve.do(VE.tensor_tensor, at5[j4][:].rearrange("p (h d) -> p h d", d=DH),
                       nd[:, :, 0:DH], rd5[i][:].unsqueeze(2).to_broadcast([N, H, DH]), ALU.mult)
            o.free = (m,)
            heads5[b] = (m,)

        def ffn_attn_out(b):
            i = b % 2
            marks = {}
            yield from until(heads5, b)
            yield from to_channels(at5[b % 4][:], heads5[b][0], KC, misc, at5T[i][:], marks, 0)
            yield from rest(REST)
            bank = misc.take(pe)
            pe.wait(marks[0])
            out5[b] = marks[0]
            m = project(bank.ap[0:N, 0:KEPT], [(at5T[i][:, k, :], ffn_w["wo5"][:, k, :])
                                               for k in range(KC)])
            dve.wait(m, x_tok_mark[b], x_in5_mark[b])
            m = dve.do(VE.tensor_tensor, x_tok[:, b, 64:], x_tok[:, b, 64:],
                       bank.ap[0:N, 0:KEPT], ALU.add)
            bank.free = (m,)
            yield
            act.wait(m)
            m = act.do(SC.activation, res[:, b, :], x_tok[:, b, :], ACT.Square,
                       accum_out=meanvar[:, b, 0:1])
            dve.wait(m)
            m = dve.do(VE.tensor_scalar, meanvar[:, b, 0:1], meanvar[:, b, 0:1], 1.0 / D, RMS_EPS,
                       ALU.mult, ALU.add)
            m = power(rstd[:, b, :], meanvar[:, b, 0:1], m)
            yield from rest(REST_POWER)
            dve.wait(m)
            m = dve.do(VE.tensor_scalar, res[:, b, :], x_tok[:, b, :], rstd[:, b, :], None,
                       ALU.mult)
            pool.wait(m)
            x_tok_mark[b] = pool.do(GP.tensor_tensor, x_tok[:, b, :], x_tok[:, b, :],
                                    x_in5[:, b, :], ALU.add)
            yield from rest(REST)
            bank = misc.take(pe)
            pe.wait(m)
            for c in range(KC):
                m = pe.do(TE.transpose, bank.ap[:, c * N:(c + 1) * N],
                          res[:, b, c * P:(c + 1) * P], ident[0:N, 0:N])
            yield
            act.wait(m)
            for c in range(KC):
                m = act.do(SC.activation, xf[:, c, cols(b)], bank.ap[:, c * N:(c + 1) * N],
                           ACT.Copy, scale=ch("n2", c))
            bank.free = (m,)
            x_ch_mark[b] = m
            act.wait(m)
            mh = act.do(SC.activation, xf16[:, 0, :, cols(b)], xf[:, :, cols(b)], ACT.Copy)
            pool.wait(mh)
            xf16_mark[b] = pool.do(GP.tensor_tensor, xf16[:, 1, :, cols(b)], xf[:, :, cols(b)],
                                   xf16[:, 0, :, cols(b)], ALU.subtract)

        w16 = {}

        def split_w5(region, name):
            t = region.tensor(name + "_16", [P, 2] + list(ffn_w[name].shape[1:]), F16)
            act.wait(w5b_ready)
            m = act.do(SC.activation, t[:, 0], ffn_w[name][:], ACT.Copy, scale=WSCALE)
            dve.wait(m)
            m = dve.do(VE.scalar_tensor_tensor, t[:, 1], ffn_w[name][:], WSCALE, t[:, 0], ALU.mult,
                       ALU.subtract)
            w16[name] = (t, m)

        def split_first():
            yield from until(out5, 3)
            split_w5(Region(nc, ring.base + ring.at, 4 * KB), "e0_up")

        weave(*(follow(ffn_attn_out, range(j, B, 2)) for j in range(2)),
              *(follow(ffn_heads, range(j, B, 2)) for j in range(2)),
              *(follow(ffn_operands, range(j, B, 4)) for j in range(4)), split_first())

        fence()
        free = Region(nc, ring.base, ring.at)
        free.restart(2 * KC * T * 2)
        work.restart(KC * T * 4)
        up, misc = banks(0, 4), banks(4, 4)
        lg5 = work.tensor("lg5", [N, B, E1])
        cl5 = work.tensor("cl5", [N, B, E1])
        ok5 = work.tensor("ok5", [N, B, E1], I32)
        pr5 = work.tensor("pr5", R)
        top5 = work.tensor("top5", R)
        top5_i = work.tensor("top5_i", R, U32)
        sm5 = work.tensor("sm5", [N, 4, B])
        ek5 = work.tensor("ek5", [N, 2, B])
        wt5 = work.tensor("wt5", [N, B, E1])
        tp5 = work.tensor("tp5", [N, B, E1])
        R4 = [N, B, E1]
        FMAX = float(np.finfo(np.float32).max)
        chosen = {}

        def wide4(t):
            return t.unsqueeze(2).to_broadcast(R4)

        def steps(m, *work_):
            for one in work_:
                m = chain(m, one)
                yield
            return m

        def route():
            bank = misc.take(pe)
            pe.wait(w5_ready)
            for b in range(B):
                pe.wait(x_ch_mark[b])
                m = project(bank.ap[0:N, b * E1:(b + 1) * E1],
                            [(xf[:, k, cols(b)], ffn_w["gate5"][:, k, :]) for k in range(KC)])
            lg = bank.ap[0:N, 0:B * E1].rearrange("p (b e) -> p b e", e=E1)
            dve.do(VE.memset, pr5[:], -1.0)
            dve.do(VE.memset, cl5[:], 0.0)
            mx, den, ts = sm5[:, 0, :], sm5[:, 1, :], sm5[:, 2, :]
            dve.wait(m)
            m = dve.do(VE.tensor_copy, tp5[:], lg)
            bank.free = (m,)
            m = yield from steps(
                m,
                st(VE.tensor_tensor, ok5[:], tp5[:], tp5[:], ALU.is_equal),
                st(VE.tensor_scalar, lg5[:], tp5[:], FMAX, -FMAX, ALU.min, ALU.max),
                st(VE.copy_predicated, cl5[:], ok5[:], lg5[:]),
                st(VE.tensor_reduce, mx, cl5[:], X, ALU.max),
                st(VE.tensor_tensor, lg5[:], cl5[:], wide4(mx), ALU.subtract))
            act.wait(m)
            m = act.do(SC.activation, tp5[:], lg5[:], ACT.Exp)
            yield
            m = yield from steps(
                m,
                st(VE.tensor_reduce, den, tp5[:], X, ALU.add),
                st(VE.reciprocal, den, den),
                st(VE.tensor_tensor, pr5[:, :, 0:E1], tp5[:], wide4(den), ALU.mult))
            dve.wait(m)
            for b in range(B):
                m = dve.do(VE.max, top5[:, b, :], pr5[:, b, :])
            yield
            dve.wait(m)
            for b in range(B):
                m = dve.do(VE.max_index, top5_i[:, b, :], top5[:, b, :], pr5[:, b, :])
            yield
            m = yield from steps(
                m,
                st(VE.tensor_tensor, ts, top5[:, :, 0], top5[:, :, 1], ALU.add),
                st(VE.tensor_scalar, ts, ts, 1e-8, WSCALE, ALU.add, ALU.mult),
                st(VE.reciprocal, ts, ts))
            for k in range(2):
                dst = (wt5, tp5)[k]
                m = yield from steps(
                    m,
                    st(VE.tensor_copy, ek5[:, k, :], top5_i[:, :, k]),
                    st(VE.tensor_tensor, dst[:], iota8[:, 0:E1].unsqueeze(1).to_broadcast(R4),
                       wide4(ek5[:, k, :]), ALU.is_equal),
                    st(VE.tensor_tensor, sm5[:, 3, :], top5[:, :, k], ts, ALU.mult),
                    st(VE.tensor_tensor, dst[:], dst[:], wide4(sm5[:, 3, :]), ALU.mult))
            chosen["wt"] = chain(m, st(VE.tensor_tensor, wt5[:], wt5[:], tp5[:], ALU.add))

        hidden = Ring([work.tensor(f"hidden{i}", [P, 2, HT, HALF], F16)[:] for i in range(5)])
        raw5 = Ring([work.tensor(f"raw5_{i}", [P, HALF])[:] for i in range(4)])
        s_res = sem("dma_result")

        def split_weights():
            for region, names in ((free, ("e1_w1", "e1_w2", "e0_down", "e1_down", "e2_l1",
                                          "e2_l2", "e3_down")),
                                  (work, ("e2_l3", "e3_up", "e2_l4", "e3_out"))):
                for name in names:
                    split_w5(region, name)
                    yield

        def parts_of(raw, m, dst, f):
            act.wait(m)
            m = act.do(SC.activation, dst.ap[:, 0, f, :], raw.ap, ACT.Copy)
            pool.wait(m)
            m = raw_mark = pool.do(GP.tensor_tensor, dst.ap[:, 1, f, :], raw.ap,
                                   dst.ap[:, 0, f, :], ALU.subtract)
            raw.free = (raw_mark,)
            return m

        def product(bank, name, f, src, kt):
            t, ready = w16[name]
            pe.wait(ready)
            return project(bank.ap[:, 0:HALF],
                           [(t[:, a_, k, f * P:(f + 1) * P], src[:, b_, k, :])
                            for k in range(kt) for a_, b_ in PARTS])

        def layer(src, src_mark, name):
            yield from until(w16, name)
            kt, n = ffn_w[name].shape[1:]
            dst = hidden.take(act, pool)
            for f in range(n // P):
                bank = up.take(pe)
                pe.wait(src_mark)
                m = product(bank, name, f, src, kt)
                raw = raw5.take(act)
                act.wait(m)
                ma = act.do(SC.activation, raw.ap, bank.ap[:, 0:HALF], ACT.Gelu, scale=1 / WSCALE)
                bank.free = (ma,)
                mark = parts_of(raw, ma, dst, f)
                yield
            return dst, mark, m

        def gated(hf):
            yield from until(w16, "e1_w1", "e1_w2")
            dst = hidden.take(act, pool)
            for f in range(HT):
                b1, b2_ = up.take(pe), up.take(pe)
                m1 = product(b1, "e1_w1", f, x_half[hf], KC)
                m2 = product(b2_, "e1_w2", f, x_half[hf], KC)
                raw = raw5.take(act, dve)
                act.wait(m1)
                m1 = act.do(SC.activation, raw.ap, b1.ap[:, 0:HALF], ACT.Silu, scale=1 / WSCALE)
                b1.free = (m1,)
                dve.wait(m1, m2)
                m = dve.do(VE.scalar_tensor_tensor, raw.ap, b2_.ap[:, 0:HALF], 1 / WSCALE, raw.ap,
                           ALU.mult, ALU.mult)
                b2_.free = (m,)
                mark = parts_of(raw, m, dst, f)
                yield
            return dst, mark

        def add_expert(e, hf, buf, mark, name):
            yield from until(chosen, "wt")
            yield from until(w16, name)
            t, ready = w16[name]
            for j in range(4):
                b = hf * 4 + j
                bank = misc.take(pe)
                pe.wait(mark, ready)
                m = project(bank.ap[0:N, 0:KEPT],
                            [(buf.ap[:, a_, k, j * N:(j + 1) * N], t[:, b_, k, :])
                             for k in range(HT) for a_, b_ in PARTS])
                dve.wait(m, chosen["wt"], x_tok_mark[b], acc_mark.get(b))
                acc_mark[b] = dve.do(VE.scalar_tensor_tensor, x_tok[:, b, 64:],
                                     bank.ap[0:N, 0:KEPT], wt5[:, b, e:e + 1],
                                     x_tok[:, b, 64:], ALU.mult, ALU.add)
                bank.free = (acc_mark[b],)
                yield
            buf.free = (m,)

        acc_mark = {}
        x_half = [xf16[:, :, :, hf * HALF:(hf + 1) * HALF] for hf in range(2)]
        x_half_mark = [xf16_mark[hf * 4 + 3] for hf in range(2)]

        def experts():
            h0 = []
            for hf in range(2):
                h0.append((yield from layer(x_half[hf], x_half_mark[hf], "e0_up")))
            g1 = []
            for hf in range(2):
                g1.append((yield from gated(hf)))
            for hf in range(2):
                yield from add_expert(0, hf, *h0[hf][:2], "e0_down")
            for hf in range(2):
                yield from add_expert(1, hf, *g1[hf], "e1_down")
            d, u, g = [None] * 2, [None] * 2, [None] * 2
            for hf in range(2):
                d[hf] = yield from layer(x_half[hf], x_half_mark[hf], "e3_down")
            for hf in range(2):
                u[hf] = yield from layer(d[hf][0].ap, d[hf][1], "e3_up")
                d[hf][0].free = (u[hf][2],)
            for hf in range(2):
                g[hf] = yield from layer(x_half[hf], x_half_mark[hf], "e2_l1")
                yield from add_expert(3, hf, *u[hf][:2], "e3_out")
            for name in ("e2_l2", "e2_l3"):
                for hf in range(2):
                    src = g[hf]
                    g[hf] = yield from layer(src[0].ap, src[1], name)
                    src[0].free = (g[hf][2],)
                    if name == "e2_l3" and hf:
                        yield from add_expert(2, 0, *g[0][:2], "e2_l4")
                        last["half"] = True
            yield from add_expert(2, 1, *g[1][:2], "e2_l4")

        last = {}

        def final(b):
            dve.wait(acc_mark[b])
            m = dve.do(VE.bn_stats, stats[:, b, :], x_tok[:, b, :])
            dve.wait(m)
            m = dve.do(VE.bn_aggr, meanvar[:, b, :], stats[:, b, :])
            dve.wait(m)
            m = dve.do(VE.tensor_scalar, meanvar[:, b, 1:2], meanvar[:, b, 1:2], LN_EPS, None,
                       ALU.add)
            yield
            m = power(rstd[:, b, :], meanvar[:, b, 1:2], m)
            yield
            dve.wait(m)
            m = dve.do(VE.tensor_scalar, res[:, b, :], x_tok[:, b, :], meanvar[:, b, 0:1],
                       rstd[:, b, :], ALU.subtract, ALU.mult)
            sp.wait(m)
            sp.dma(SY.dma_start, s_res, out[b], res[:, b, :])

        def first_finals():
            yield from until(last, "half")
            yield from follow(final, range(4))

        weave(experts(), route(), split_weights(), first_finals())
        weave(*[final(b) for b in range(4, 8)])
        sp.wait((s_res, s_res.value))

        block = ctx.enter_context(nc.Block())

        @block.tensor
        def _(eng):
            pe.run(eng)

        @block.scalar
        def _(eng):
            act.run(eng)

        @block.vector
        def _(eng):
            dve.run(eng)

        @block.gpsimd
        def _(eng):
            pool.run(eng)

        @block.sync
        def _(eng):
            sp.run(eng)


def layout(i):
    f = np.float32
    c = np.ascontiguousarray

    def tiles(w, p=P):
        return c(w.reshape(w.shape[0] // p, p, w.shape[1]).transpose(1, 0, 2))

    def ctx_tiles(w):
        return c(np.stack([w[0:P], np.concatenate([w[P:], w[P:]])], axis=1))

    def rows(v, n):
        return c(np.broadcast_to(v, (n, v.shape[0])))

    def col(v):
        return c(v.reshape(-1, P).T)

    a = {}
    a["xT"] = tiles(c(i["x"].reshape(T, D).T))
    a["x_tok"] = c(i["x"].transpose(1, 0, 2))
    a["ctxT"] = c(ctx_tiles(i["ctx_768"].transpose(2, 0, 1)).transpose(2, 0, 1, 3))
    a["Wqkv"] = tiles(i["L0_attn_Wqkv"])
    bqkv = i["L0_attn_bqkv"]
    om = np.zeros((P, 4 * FM), f)
    for h in range(4):
        om[h * DH:(h + 1) * DH, h * FM:(h + 1) * FM] = i["L0_attn_omega"]
        om[64 + h * DH:64 + (h + 1) * DH, h * FM:(h + 1) * FM] = -0.5
    a["omega"] = om
    a["vbias0"] = rows(bqkv[2 * D:], N)
    a["Wout0"] = tiles(i["L0_attn_Wout"])
    a["bout0"] = rows(i["L0_attn_bout"], N)
    a["Wq1"] = tiles(i["L0_xattn_Wq"])
    a["Wkv1"] = ctx_tiles(np.concatenate([i["L0_xattn_Wk"], i["L0_xattn_Wv"]], axis=1))
    a["bv1"] = rows(i["L0_xattn_bv"], N)
    a["W1"] = tiles(i["L0_xattn_W1"])
    a["W2"] = tiles(i["L0_xattn_W2"])
    a["b2"] = rows(i["L0_xattn_b2"], N)
    a["router"] = tiles(c(i["L0_ffn_router_w"].T))
    a["wg"] = c(i["L0_ffn_wg"].reshape(E0, KC, P, F0).transpose(0, 2, 1, 3))
    a["wu"] = c(i["L0_ffn_wu"].reshape(E0, KC, P, F0).transpose(0, 2, 1, 3))
    a["wd"] = c(i["L0_ffn_wd"].reshape(E0, F0 // P, P, D).transpose(0, 2, 1, 3))
    a["Wq3"] = tiles(c(i["L1_attn_Wq"].T))
    a["Wk3"] = tiles(c(i["L1_attn_Wk"].T))
    a["Wv3"] = tiles(c(i["L1_attn_Wv"].T))
    a["Wo3"] = tiles(c(i["L1_attn_Wo"].T))
    a["Wq4"] = tiles(i["L1_xattn_w_q"])
    a["Wk4"] = ctx_tiles(i["L1_xattn_w_k"])
    a["Wv4"] = ctx_tiles(i["L1_xattn_w_v"])
    a["Wo4"] = tiles(i["L1_xattn_w_out"])
    a["bout4"] = rows(i["L1_xattn_b_out"], N)
    for k, n in (("wq5", "wq"), ("wk5", "wk"), ("wv5", "wv"), ("gate5", "gate_w"),
                 ("e0_up", "e0_up"), ("e1_w1", "e1_w1"), ("e1_w2", "e1_w2"), ("e2_l1", "e2_l1"),
                 ("e2_l2", "e2_l2"), ("e2_l3", "e2_l3"), ("e3_down", "e3_down"),
                 ("e3_up", "e3_up")):
        a[k] = tiles(c(i["L1_ffn_" + n].T))
    for k, n in (("wo5", "wo"), ("e0_down", "e0_down"), ("e1_down", "e1_down"),
                 ("e2_l4", "e2_l4"), ("e3_out", "e3_out")):
        a[k] = tiles(c(i["L1_ffn_" + n].T[:, D - KEPT:]))
    a["chan"] = c(np.concatenate([
        col(bqkv[0:D]), col(bqkv[D:2 * D]), col(i["L0_xattn_bq"]), col(i["L0_xattn_bk"]),
        col(i["L0_xattn_b1"]), col(np.tile(i["L1_attn_g_weight"], 2)), col(i["L1_ffn_n1_w"]),
        col(i["L1_ffn_n2_w"]), col(np.tile(i["L1_ffn_qn_w"], HPT)),
        col(np.tile(i["L1_ffn_kn_w"], HPT))], axis=1))
    a["ident"] = np.eye(P, dtype=f)
    a["headq"] = c((np.arange(P)[:, None] // DH == np.arange(HPT)[None, :]) * f(0.25)).astype(f)
    n = np.arange(N)
    a["half_causal"] = c((n[:, None] <= n[None, :]) * f(0.5)).astype(f)
    a["causal_add"] = np.where(n[None, :] > n[:, None], f(-3e38), f(0)).astype(f)
    a["before"] = (n[None, :] < n[:, None]).astype(f)
    a["slot_tab"] = c((SLOTS + np.arange(2 * B)[None, :] * N + n[:, None])).astype(f)
    a["iota8"] = rows(np.arange(E0).astype(f), N)
    return a


def kernel(**inputs):
    import concourse.bacc as bacc
    from concourse.bass_utils import run_bass_kernel_spmd

    arrays = layout({k: np.asarray(v) for k, v in inputs.items()})
    nc = bacc.Bacc("TRN2", target_bir_lowering=False, num_devices=1)
    aps = {k: nc.dram_tensor("in_" + k, v.shape, mybir.dt.from_np(v.dtype),
                             kind="ExternalInput").ap() for k, v in arrays.items()}
    out = nc.dram_tensor("out", (B, N, D), F32, kind="ExternalOutput").ap()
    program(nc, aps, out)
    r = run_bass_kernel_spmd(nc, [{"in_" + k: v for k, v in arrays.items()}], core_ids=[0])
    return r.results[0]["out"]
```
